# Optimizing a Trainium2 kernel written in Bass

```python
import numpy as np
import jax
import jax.numpy as jnp

def _softmax(x, axis=-1):
    return jax.nn.softmax(x, axis=axis)

def _gelu(x):
    return jax.nn.gelu(x, approximate=True)

def _silu(x):
    return jax.nn.silu(x)

def _sigmoid(x):
    return jax.nn.sigmoid(x)

def _layernorm(x, axis=-1, eps=1e-05):
    m = jnp.mean(x, axis=axis, keepdims=True)
    v = jnp.var(x, axis=axis, keepdims=True)
    return (x - m) / jnp.sqrt(v + eps)

def _scatter_add(tgt, idx, src, axis=0):
    return tgt.at[idx].add(src)

def _segment_sum(src, seg, n):
    return jax.ops.segment_sum(src, seg, n)
kernel_name = 'mk_gps_d1_gnn_r8_327e21'

def setup_inputs(seed: int=0):
    np.random.seed(seed)
    _w = jnp.asarray

    def _rec_inputs():
        import jax
        import jax.numpy as jnp
        _gk = jax.random.key(seed)
        x = -8.776e-05 + 1 * jax.random.normal(jax.random.fold_in(_gk, 1), (6250, 256), jnp.float32)
        src = jax.random.randint(jax.random.fold_in(_gk, 2), (100000,), 0, 6250, jnp.int32)
        dst = jnp.minimum((6250 * jax.random.uniform(jax.random.fold_in(_gk, 3), (100000,)) ** 2.0).astype(jnp.int32), 49999)
        _o = jnp.argsort(dst, stable=True)
        src = src[_o]
        dst = dst[_o]
        edge_type_3 = jax.random.randint(jax.random.fold_in(_gk, 12), (100000,), 0, 3, jnp.int32)
        node_type_4 = jax.random.randint(jax.random.fold_in(_gk, 13), (6250,), 0, 4, jnp.int32)
        return (x, src, dst, edge_type_3, node_type_4)
    x, src, dst, edge_type_3, node_type_4 = _rec_inputs()

    def _L0_gnn_setup():
        import jax, jax.numpy as jnp
        import numpy as np
        import math
        L, H, HD, D = (3, 8, 32, 256)
        TN, TE = (4, 3)

        def _layer_norm(x, g, b, eps=1e-05):
            m = jnp.mean(x, axis=-1, keepdims=True)
            v = jnp.var(x, axis=-1, keepdims=True)
            return (x - m) / jnp.sqrt(v + eps) * g + b

        def _typed_transform(xh, W, types):
            out = jnp.zeros_like(xh)
            for t in range(W.shape[0]):
                y = jnp.einsum('mhd,hde->mhe', xh, W[t])
                out = jnp.where((types == t)[:, None, None], y, out)
            return out
        N, E = (2500, 40000)
        key = jax.random.key(seed)
        ks = jax.random.split(key, 16)
        inp = {}
        inp['x'] = jax.random.normal(ks[0], (N, D), dtype=jnp.float32)
        inp['edge_index'] = jax.random.randint(ks[1], (2, E), 0, N)
        inp['edge_type'] = jax.random.randint(ks[2], (E,), 0, TE)
        inp['node_type'] = jax.random.randint(ks[3], (N,), 0, TN)
        inp['W_Q'] = jax.random.normal(ks[4], (L, TN, H, HD, HD), dtype=jnp.float32) * 0.02
        inp['W_K'] = jax.random.normal(ks[5], (L, TN, H, HD, HD), dtype=jnp.float32) * 0.02
        inp['W_V'] = jax.random.normal(ks[6], (L, TN, H, HD, HD), dtype=jnp.float32) * 0.02
        inp['W_E'] = jax.random.normal(ks[7], (L, TE, H, HD, HD), dtype=jnp.float32) * 0.02
        inp['mu'] = jnp.ones((L, H, TE), dtype=jnp.float32)
        inp['Wo'] = jax.random.normal(ks[8], (L, D, D), dtype=jnp.float32) * 0.02
        inp['bo'] = jnp.zeros((L, D), dtype=jnp.float32)
        inp['ln1_g'] = jnp.ones((L, D), dtype=jnp.float32)
        inp['ln1_b'] = jnp.zeros((L, D), dtype=jnp.float32)
        inp['ln2_g'] = jnp.ones((L, D), dtype=jnp.float32)
        inp['ln2_b'] = jnp.zeros((L, D), dtype=jnp.float32)
        inp['w1'] = jax.random.normal(ks[9], (L, D, 4 * D), dtype=jnp.float32) * 0.02
        inp['b1'] = jnp.zeros((L, 4 * D), dtype=jnp.float32)
        inp['w2'] = jax.random.normal(ks[10], (L, 4 * D, D), dtype=jnp.float32) * 0.02
        inp['b2'] = jnp.zeros((L, D), dtype=jnp.float32)
        inp['out_g'] = jnp.ones((D,), dtype=jnp.float32)
        inp['out_b'] = jnp.zeros((D,), dtype=jnp.float32)
        return inp
    _L0_gnn_all = _L0_gnn_setup()
    _L0_gnn_in = {k: v for k, v in _L0_gnn_all.items() if k in ('W_Q', 'W_K', 'W_V', 'W_E', 'mu', 'Wo', 'bo', 'ln1_g', 'ln1_b', 'ln2_g', 'ln2_b', 'w1', 'b1', 'w2', 'b2', 'out_g', 'out_b')}
    del _L0_gnn_all

    def _L0_mix_setup():
        import jax, jax.numpy as jnp
        import numpy as np
        import math
        EMBED = 256
        HEADS = 4
        HEAD_DIM = EMBED // HEADS
        OUT_DIM = 256
        LN_EPS = 1e-05

        def _qkv_init(key):
            spread = math.sqrt(3.0 / EMBED)
            gain, delta = (0.01, 0.01)
            w = jax.random.uniform(key, (EMBED, EMBED), minval=-spread, maxval=spread) * gain
            return w + delta * jnp.eye(EMBED, dtype=w.dtype)

        def _layer_norm(x, g, b):
            mu = jnp.mean(x, axis=-1, keepdims=True)
            var = jnp.mean(jnp.square(x - mu), axis=-1, keepdims=True)
            return (x - mu) * jax.lax.rsqrt(var + LN_EPS) * g + b

        def _split_heads(x, B, S):
            return x.reshape(B, S, HEADS, HEAD_DIM).transpose(0, 2, 1, 3)
        key = jax.random.key(seed)
        ks = jax.random.split(key, 6)
        seq = jax.random.normal(ks[0], (4, 1024, EMBED), dtype=jnp.float32)
        wq = _qkv_init(ks[1])
        wk = _qkv_init(ks[2])
        wv = _qkv_init(ks[3])
        bound = 1.0 / math.sqrt(EMBED)
        wo = jax.random.uniform(ks[4], (OUT_DIM, EMBED), minval=-bound, maxval=bound)
        bo = jax.random.uniform(ks[5], (OUT_DIM,), minval=-bound, maxval=bound)
        ln_k_g = jnp.ones((HEAD_DIM,), jnp.float32)
        ln_k_b = jnp.zeros((HEAD_DIM,), jnp.float32)
        ln_v_g = jnp.ones((HEAD_DIM,), jnp.float32)
        ln_v_b = jnp.zeros((HEAD_DIM,), jnp.float32)
        return {'seq': seq, 'wq': wq, 'wk': wk, 'wv': wv, 'wo': wo, 'bo': bo, 'ln_k_g': ln_k_g, 'ln_k_b': ln_k_b, 'ln_v_g': ln_v_g, 'ln_v_b': ln_v_b}
    _L0_mix_all = _L0_mix_setup()
    _L0_mix_in = {k: v for k, v in _L0_mix_all.items() if k in ('wq', 'wk', 'wv', 'wo', 'bo', 'ln_k_g', 'ln_k_b', 'ln_v_g', 'ln_v_b')}
    del _L0_mix_all

    def _L0_ffn_setup():
        import jax, jax.numpy as jnp
        import numpy as np
        BN_EPS = 0.001

        def _bn(h, g, b, m, v):
            return g * (h - m) * jax.lax.rsqrt(v + BN_EPS) + b
        key = jax.random.key(seed)
        ks = jax.random.split(key, 8)
        B, F, Df = (256, 64, 256)
        E, H, D = (8, 256, 256)
        s1 = 1.0 / np.sqrt(Df)
        s2 = 1.0 / np.sqrt(H)
        return {'x': jax.random.normal(ks[0], (B, F, Df), jnp.float32), 'Wr': jax.random.normal(ks[1], (Df, E), jnp.float32) * s1, 'br': jnp.zeros((E,), jnp.float32), 'W1': jax.random.normal(ks[2], (E, Df, H), jnp.float32) * s1, 'b1': jnp.zeros((E, H), jnp.float32), 'g1': jnp.ones((E, H), jnp.float32), 'be1': jnp.zeros((E, H), jnp.float32), 'm1': jnp.zeros((E, H), jnp.float32), 'v1': jnp.ones((E, H), jnp.float32), 'W2': jax.random.normal(ks[3], (E, H, H), jnp.float32) * s2, 'b2': jnp.zeros((E, H), jnp.float32), 'g2': jnp.ones((E, H), jnp.float32), 'be2': jnp.zeros((E, H), jnp.float32), 'm2': jnp.zeros((E, H), jnp.float32), 'v2': jnp.ones((E, H), jnp.float32), 'Wo': jax.random.normal(ks[4], (E, H, D), jnp.float32) * s2, 'bo': jnp.zeros((E, D), jnp.float32)}
    _L0_ffn_all = _L0_ffn_setup()
    _L0_ffn_in = {k: v for k, v in _L0_ffn_all.items() if k in ('Wr', 'br', 'W1', 'b1', 'g1', 'be1', 'm1', 'v1', 'W2', 'b2', 'g2', 'be2', 'm2', 'v2', 'Wo', 'bo')}
    del _L0_ffn_all
    return {'x': x, 'src': src, 'dst': dst, 'edge_type_3': edge_type_3, 'node_type_4': node_type_4, 'L0_gnn_W_Q': _L0_gnn_in['W_Q'], 'L0_gnn_W_K': _L0_gnn_in['W_K'], 'L0_gnn_W_V': _L0_gnn_in['W_V'], 'L0_gnn_W_E': _L0_gnn_in['W_E'], 'L0_gnn_mu': _L0_gnn_in['mu'], 'L0_gnn_Wo': _L0_gnn_in['Wo'], 'L0_gnn_bo': _L0_gnn_in['bo'], 'L0_gnn_ln1_g': _L0_gnn_in['ln1_g'], 'L0_gnn_ln1_b': _L0_gnn_in['ln1_b'], 'L0_gnn_ln2_g': _L0_gnn_in['ln2_g'], 'L0_gnn_ln2_b': _L0_gnn_in['ln2_b'], 'L0_gnn_w1': _L0_gnn_in['w1'], 'L0_gnn_b1': _L0_gnn_in['b1'], 'L0_gnn_w2': _L0_gnn_in['w2'], 'L0_gnn_b2': _L0_gnn_in['b2'], 'L0_gnn_out_g': _L0_gnn_in['out_g'], 'L0_gnn_out_b': _L0_gnn_in['out_b'], 'L0_mix_wq': _L0_mix_in['wq'], 'L0_mix_wk': _L0_mix_in['wk'], 'L0_mix_wv': _L0_mix_in['wv'], 'L0_mix_wo': _L0_mix_in['wo'], 'L0_mix_bo': _L0_mix_in['bo'], 'L0_mix_ln_k_g': _L0_mix_in['ln_k_g'], 'L0_mix_ln_k_b': _L0_mix_in['ln_k_b'], 'L0_mix_ln_v_g': _L0_mix_in['ln_v_g'], 'L0_mix_ln_v_b': _L0_mix_in['ln_v_b'], 'L0_ffn_Wr': _L0_ffn_in['Wr'], 'L0_ffn_br': _L0_ffn_in['br'], 'L0_ffn_W1': _L0_ffn_in['W1'], 'L0_ffn_b1': _L0_ffn_in['b1'], 'L0_ffn_g1': _L0_ffn_in['g1'], 'L0_ffn_be1': _L0_ffn_in['be1'], 'L0_ffn_m1': _L0_ffn_in['m1'], 'L0_ffn_v1': _L0_ffn_in['v1'], 'L0_ffn_W2': _L0_ffn_in['W2'], 'L0_ffn_b2': _L0_ffn_in['b2'], 'L0_ffn_g2': _L0_ffn_in['g2'], 'L0_ffn_be2': _L0_ffn_in['be2'], 'L0_ffn_m2': _L0_ffn_in['m2'], 'L0_ffn_v2': _L0_ffn_in['v2'], 'L0_ffn_Wo': _L0_ffn_in['Wo'], 'L0_ffn_bo': _L0_ffn_in['bo']}

def reference(x, src, dst, edge_type_3, node_type_4, L0_gnn_W_Q, L0_gnn_W_K, L0_gnn_W_V, L0_gnn_W_E, L0_gnn_mu, L0_gnn_Wo, L0_gnn_bo, L0_gnn_ln1_g, L0_gnn_ln1_b, L0_gnn_ln2_g, L0_gnn_ln2_b, L0_gnn_w1, L0_gnn_b1, L0_gnn_w2, L0_gnn_b2, L0_gnn_out_g, L0_gnn_out_b, L0_mix_wq, L0_mix_wk, L0_mix_wv, L0_mix_wo, L0_mix_bo, L0_mix_ln_k_g, L0_mix_ln_k_b, L0_mix_ln_v_g, L0_mix_ln_v_b, L0_ffn_Wr, L0_ffn_br, L0_ffn_W1, L0_ffn_b1, L0_ffn_g1, L0_ffn_be1, L0_ffn_m1, L0_ffn_v1, L0_ffn_W2, L0_ffn_b2, L0_ffn_g2, L0_ffn_be2, L0_ffn_m2, L0_ffn_v2, L0_ffn_Wo, L0_ffn_bo):
    import jax
    import jax.numpy as jnp

    def _L0_gnn_ref(x, edge_index, edge_type, node_type, W_Q, W_K, W_V, W_E, mu, Wo, bo, ln1_g, ln1_b, ln2_g, ln2_b, w1, b1, w2, b2, out_g, out_b):
        import jax, jax.numpy as jnp
        import numpy as np
        import math
        L, H, HD, D = (3, 8, 32, 256)
        TN, TE = (4, 3)

        def _layer_norm(x, g, b, eps=1e-05):
            m = jnp.mean(x, axis=-1, keepdims=True)
            v = jnp.var(x, axis=-1, keepdims=True)
            return (x - m) / jnp.sqrt(v + eps) * g + b

        def _typed_transform(xh, W, types):
            out = jnp.zeros_like(xh)
            for t in range(W.shape[0]):
                y = jnp.einsum('mhd,hde->mhe', xh, W[t])
                out = jnp.where((types == t)[:, None, None], y, out)
            return out
        N = x.shape[0]
        src, dst = (edge_index[0], edge_index[1])
        scale = math.sqrt(HD)
        for l in range(L):
            xh = x.reshape(N, H, HD)
            Q = _typed_transform(xh, W_Q[l], node_type)
            K = _typed_transform(xh, W_K[l], node_type)
            V = _typed_transform(xh, W_V[l], node_type)
            q_dst = Q[dst]
            kt = _typed_transform(K[src], W_E[l], edge_type)
            scores = jnp.sum(q_dst * kt, axis=-1) / scale
            scores = scores * mu[l].T[edge_type]
            m = jax.ops.segment_max(scores, dst, num_segments=N)
            m = jnp.maximum(m, -1000000000.0)
            e = jnp.exp(scores - m[dst])
            s = jax.ops.segment_sum(e, dst, num_segments=N)
            w = e / (s[dst] + 1e-10)
            agg = jax.ops.segment_sum(V[src] * w[..., None], dst, num_segments=N)
            attn = agg.reshape(N, D) @ Wo[l] + bo[l]
            x = _layer_norm(x + attn, ln1_g[l], ln1_b[l])
            h = jax.nn.gelu(x @ w1[l] + b1[l], approximate=False) @ w2[l] + b2[l]
            x = _layer_norm(x + h, ln2_g[l], ln2_b[l])
        return _layer_norm(x, out_g, out_b)

    def _L0_mix_ref(seq, wq, wk, wv, wo, bo, ln_k_g, ln_k_b, ln_v_g, ln_v_b):
        import jax, jax.numpy as jnp
        import numpy as np
        import math
        EMBED = 256
        HEADS = 4
        HEAD_DIM = EMBED // HEADS
        OUT_DIM = 256
        LN_EPS = 1e-05

        def _qkv_init(key):
            spread = math.sqrt(3.0 / EMBED)
            gain, delta = (0.01, 0.01)
            w = jax.random.uniform(key, (EMBED, EMBED), minval=-spread, maxval=spread) * gain
            return w + delta * jnp.eye(EMBED, dtype=w.dtype)

        def _layer_norm(x, g, b):
            mu = jnp.mean(x, axis=-1, keepdims=True)
            var = jnp.mean(jnp.square(x - mu), axis=-1, keepdims=True)
            return (x - mu) * jax.lax.rsqrt(var + LN_EPS) * g + b

        def _split_heads(x, B, S):
            return x.reshape(B, S, HEADS, HEAD_DIM).transpose(0, 2, 1, 3)
        B, S, _ = seq.shape
        q = _split_heads(seq @ wq.T, B, S)
        k = _split_heads(seq @ wk.T, B, S)
        v = _split_heads(seq @ wv.T, B, S)
        k = _layer_norm(k, ln_k_g, ln_k_b)
        v = _layer_norm(v, ln_v_g, ln_v_b)
        kv = jnp.einsum('bhsd,bhse->bhde', k, v) / S
        ga = jnp.einsum('bhsd,bhde->bhse', q, kv)
        ga = ga.transpose(0, 2, 1, 3).reshape(B, S, EMBED)
        return ga @ wo.T + bo

    def _L0_ffn_ref(x, Wr, br, W1, b1, g1, be1, m1, v1, W2, b2, g2, be2, m2, v2, Wo, bo):
        import jax, jax.numpy as jnp
        import numpy as np
        BN_EPS = 0.001

        def _bn(h, g, b, m, v):
            return g * (h - m) * jax.lax.rsqrt(v + BN_EPS) + b
        feat = jnp.mean(x, axis=0)
        w = jax.nn.softmax(feat @ Wr + br, axis=-1)
        h = jnp.einsum('bfd,edh->bfeh', x, W1) + b1
        h = jax.nn.relu(_bn(h, g1, be1, m1, v1))
        h = jnp.einsum('bfeh,ehk->bfek', h, W2) + b2
        h = jax.nn.relu(_bn(h, g2, be2, m2, v2))
        y = jnp.einsum('bfeh,ehd->bfed', h, Wo) + bo
        return jnp.einsum('bfed,fe->bfd', y, w)
    edge_index = jnp.stack([src, dst])
    xn = _layernorm(x, axis=-1)
    x = x + _L0_gnn_ref(xn, edge_index, edge_type_3, node_type_4, L0_gnn_W_Q, L0_gnn_W_K, L0_gnn_W_V, L0_gnn_W_E, L0_gnn_mu, L0_gnn_Wo, L0_gnn_bo, L0_gnn_ln1_g, L0_gnn_ln1_b, L0_gnn_ln2_g, L0_gnn_ln2_b, L0_gnn_w1, L0_gnn_b1, L0_gnn_w2, L0_gnn_b2, L0_gnn_out_g, L0_gnn_out_b) + _L0_mix_ref(xn[None], L0_mix_wq, L0_mix_wk, L0_mix_wv, L0_mix_wo, L0_mix_bo, L0_mix_ln_k_g, L0_mix_ln_k_b, L0_mix_ln_v_g, L0_mix_ln_v_b)[0]
    x = x + _L0_ffn_ref(_layernorm(x, axis=-1)[None], L0_ffn_Wr, L0_ffn_br, L0_ffn_W1, L0_ffn_b1, L0_ffn_g1, L0_ffn_be1, L0_ffn_m1, L0_ffn_v1, L0_ffn_W2, L0_ffn_b2, L0_ffn_g2, L0_ffn_be2, L0_ffn_m2, L0_ffn_v2, L0_ffn_Wo, L0_ffn_bo)[0]
    return x

_drawn_inputs = setup_inputs


def setup_inputs(seed=0):
    import zlib

    import numpy as np

    out = dict(_drawn_inputs(seed))
    spreads = {'L0_gnn_mu': (1.0, 0.6),
     'L0_gnn_bo': (0.0, 0.1),
     'L0_gnn_ln1_g': (1.0, 0.2),
     'L0_gnn_ln1_b': (0.0, 0.1),
     'L0_gnn_ln2_g': (1.0, 0.2),
     'L0_gnn_ln2_b': (0.0, 0.1),
     'L0_gnn_b1': (0.0, 0.338),
     'L0_gnn_b2': (0.0, 0.1),
     'L0_gnn_out_g': (1.0, 0.2),
     'L0_gnn_out_b': (0.0, 0.1),
     'L0_mix_ln_k_g': (1.0, 0.6),
     'L0_mix_ln_k_b': (0.0, 0.8),
     'L0_mix_ln_v_g': (1.0, 0.6),
     'L0_mix_ln_v_b': (0.0, 0.8),
     'L0_ffn_br': (0.0, 0.453),
     'L0_ffn_b1': (0.0, 0.611),
     'L0_ffn_g1': (1.0, 0.6),
     'L0_ffn_be1': (0.0, 0.632),
     'L0_ffn_m1': (0.0, 0.618),
     'L0_ffn_v1': (1.0, 0.6),
     'L0_ffn_b2': (0.0, 0.438),
     'L0_ffn_g2': (1.0, 0.568),
     'L0_ffn_be2': (0.0, 0.462),
     'L0_ffn_m2': (0.0, 0.455),
     'L0_ffn_v2': (1.0, 0.6),
     'L0_ffn_bo': (0.0, 0.327)}
    factors = {'L0_gnn_W_Q': 8.0,
     'L0_gnn_W_K': 8.0,
     'L0_gnn_W_V': 5.476,
     'L0_gnn_W_E': 8.0,
     'L0_gnn_Wo': 5.486,
     'L0_mix_wq': 8.0,
     'L0_mix_wk': 8.0,
     'L0_mix_wv': 8.0,
     'L0_mix_wo': 8.0,
     'L0_mix_bo': 2.993}
    for name, (base, spread) in spreads.items():
        noise = np.random.default_rng([zlib.crc32(name.encode()), seed]).standard_normal(out[name].shape)
        drawn = base * np.exp(spread * noise) if base else spread * noise
        out[name] = jnp.asarray(drawn.astype(out[name].dtype))
    for name, factor in factors.items():
        out[name] = (out[name] * factor).astype(out[name].dtype)
    return out
```

```python
from contextlib import ExitStack, contextmanager

import numpy as np

import concourse.bass as bass
from concourse import mybir

ALU = mybir.AluOpType
ACT = mybir.ActivationFunctionType
F32 = mybir.dt.float32
BF16 = mybir.dt.bfloat16
I32 = mybir.dt.int32
AX = mybir.AxisListType.X

P = 128
N, E, D = 6250, 100000, 256
L, H, HD, TN, TE = 3, 8, 32, 4, 3
FF = 4 * D
NX, HE = 8, 256
MH, MD = 4, 64
CH = 512
NCH = -(-N // CH)
NB = CH // P
NP = NCH * CH
BLK = -(-N // P)
TILES = 784
EP = TILES * P
V = TILES + BLK - 1
VP = 104
VJ = V // VP
SC = 16
VK = V // SC
CL = VK * P
RW = H * (HD + 1)
GV = 16
GH = GV // 4
NG = V // GV
BIG = 1.0e30
assert VJ * VP == V and SC * VK == V and NG * GV == V and TILES % 112 == 0 and EP >= E
TJ = TILES // 112


def ds(start, size):
    return bass.ds(start, size)


@contextmanager
def stage(nc, name, names, pool_dmas=False):
    with ExitStack() as ctx:
        s = {n: ctx.enter_context(nc.semaphore(f"{name}_{n}")) for n in names.split()}
        with nc.Block() as block:
            yield block, s
        with nc.Block() as clear:
            if pool_dmas:
                @clear.gpsimd
                def _(pool):
                    pool.dma_reset()
                    for x in s.values():
                        pool.sem_clear(x)
            else:
                @clear.sync
                def _(sp):
                    for x in s.values():
                        sp.sem_clear(x)


class Arena:

    def __init__(self, tensor, words):
        self.tensor, self.words, self.at = tensor, words, 0

    def take(self, shape, dtype=F32, parts=P):
        size = int(np.prod(shape))
        words = size if dtype != BF16 else -(-size // 2)
        words = -(-words // 8) * 8
        ap = self.tensor[0:parts, self.at:self.at + words]
        self.at += words
        assert self.at <= self.words, (self.at, self.words)
        if dtype != F32:
            ap = ap.bitcast(dtype)
        ap = ap[:, 0:size]
        if len(shape) == 2:
            ap = ap.rearrange("p (a b) -> p a b", a=shape[0])
        elif len(shape) == 3:
            ap = ap.rearrange("p (a b c) -> p a b c", a=shape[0], b=shape[1])
        return ap


def spread(dram, offset, *dims):
    return bass.AP(tensor=dram.tensor, offset=offset, ap=[list(d) for d in dims])


def along(ap, axis, count):
    ap = ap.unsqueeze(axis)
    shape = list(ap.shape)
    shape[axis] = count
    return ap.broadcast_to(shape)


def build_constants(nc, k):
    with stage(nc, "const", "filled made") as (block, s):
        @block.gpsimd
        def _(pool):
            pool.memset(k.ident[:, :], 0.0).then_inc(s["filled"], 1)
            pool.wait_ge(s["filled"], 1)
            pool.affine_select(out=k.ident[:, :], in_=k.ident[:, :], compare_op=ALU.not_equal, fill=1.0, base=0,
                               pattern=[[-1, P]], channel_multiplier=1)
            pool.iota(k.iota_row[:, :], pattern=[[1, P]], base=0, channel_multiplier=0,
                      allow_small_or_imprecise_dtypes=True)
            pool.iota(k.iota_col[:, :], pattern=[[0, 1]], base=0, channel_multiplier=1,
                      allow_small_or_imprecise_dtypes=True).then_inc(s["made"], 1)


def build_visits(nc, k, src, dst, edge_type, node_type, dram):
    a = Arena(k.arena, k.words)
    T = 112
    src_t, dst_t, et_t = (a.take([TJ * P], I32) for _ in range(3))
    comb = a.take([TJ, 3, P])
    last_i, blk_i = a.take([TJ], I32), a.take([TJ], I32)
    blk_f, tile_no, reach = a.take([TJ]), a.take([TJ]), a.take([TJ])
    reach_all, below = a.take([TILES]), a.take([TILES])
    visit_no, tile_of, block_of, block_off = (a.take([VJ]) for _ in range(4))
    tile_idx, block_i = a.take([VJ], I32), a.take([VJ], I32)
    got = a.take([VJ, 3 * P])
    keyrel, key, over = a.take([VJ, P]), a.take([VJ, P]), a.take([VJ, P])
    keyrel_b = a.take([VJ, P], BF16)
    types_i, types = a.take([NCH * NB], I32), a.take([NCH * NB])
    with stage(nc, "tiles", "edges comb_last made comb_made reach stored_comb stored_reach types shifted typed typ1") as (block, s):
        @block.sync
        def _(sp):
            for to, of in ((src_t, src), (dst_t, dst), (et_t, edge_type)):
                sp.dma_start(to[0:T, :], of.rearrange("(p f) -> p f", p=T)).then_inc(s["edges"], 16)
            with nc.allow_non_contiguous_dma(reason="once, a word per node"):
                sp.dma_start(types_i, node_type.rearrange("(b p) -> p b", p=P)).then_inc(s["types"], 16)
            sp.wait_ge(s["comb_made"], 1)
            sp.dma_start(dram.comb.rearrange("(p j) f -> p (j f)", p=T),
                         comb[0:T].rearrange("p a b c -> p (a b c)")).then_inc(s["stored_comb"], 16)
            sp.wait_ge(s["reach"], 1)
            sp.dma_start(dram.reach.rearrange("(p j) -> p j", p=T), reach[0:T]).then_inc(s["stored_reach"], 16)
            sp.wait_ge(s["stored_comb"], 16)
            sp.wait_ge(s["stored_reach"], 16)

        @block.gpsimd
        def _(pool):
            pool.iota(tile_no[0:T], pattern=[[1, TJ]], base=0, channel_multiplier=TJ,
                      allow_small_or_imprecise_dtypes=True).then_inc(s["made"], 1)
            pool.iota(visit_no[0:VP], pattern=[[VP, VJ]], base=0, channel_multiplier=1,
                      allow_small_or_imprecise_dtypes=True).then_inc(s["made"], 1)

        @block.vector
        def _(dve):
            dve.wait_ge(s["edges"], 48)
            three = [x[0:T].rearrange("p (j f) -> p j f", j=TJ) for x in (src_t, dst_t, et_t)]
            dve.scalar_tensor_tensor(comb[0:T, :, 0, :], three[0], float(TE), three[2], ALU.mult, ALU.add)
            dve.tensor_copy(comb[0:T, :, 1, :], three[0])
            dve.tensor_copy(comb[0:T, :, 2, :], three[1]).then_inc(s["comb_made"], 1)
            dve.tensor_copy(last_i[0:T], three[1][:, :, P - 1]).then_inc(s["comb_last"], 1)
            dve.wait_ge(s["comb_last"], 1)
            dve.tensor_scalar(blk_i[0:T], last_i[0:T], 7, None, ALU.arith_shift_right).then_inc(s["shifted"], 1)
            dve.wait_ge(s["shifted"], 1)
            dve.tensor_copy(blk_f[0:T], blk_i[0:T]).then_inc(s["shifted"], 1)
            dve.wait_ge(s["shifted"], 2)
            dve.wait_ge(s["made"], 2)
            dve.tensor_tensor(reach[0:T], blk_f[0:T], tile_no[0:T], ALU.add).then_inc(s["reach"], 1)
            dve.wait_ge(s["types"], 16)
            dve.tensor_copy(types, types_i).then_inc(s["typed"], 1)
            dve.wait_ge(s["typed"], 1)
            for t in range(TN):
                dve.tensor_scalar(k.onehot[:, :, t], types, float(t), None, ALU.is_equal)

    with stage(nc, "visits", "reach below count index got rel m1 m2 stored tile off turned copied keyb blocki last", True) as (block, s):
        @block.sync
        def _(sp):
            sp.dma_start(reach_all[0:VP], dram.reach.partition_broadcast(VP)).then_inc(s["reach"], 16)
            sp.wait_ge(s["last"], 1)
            sp.dma_start(dram.keyrow.rearrange("(j p) s -> p j s", p=VP), keyrel_b[0:VP]).then_inc(s["stored"], 16)
            sp.dma_start(dram.key.rearrange("(j p s) -> p j s", p=VP, j=VJ), key[0:VP]).then_inc(s["stored"], 16)
            with nc.allow_non_contiguous_dma(reason="once, a word per visit"):
                sp.dma_start(dram.blocks_i.rearrange("(j p) -> p j", p=VP), block_i[0:VP]).then_inc(s["stored"], 16)
                sp.dma_start(dram.blocks_f.rearrange("(j p) -> p j", p=VP), block_of[0:VP]).then_inc(s["stored"], 16)
            sp.wait_ge(s["stored"], 64)

        @block.vector
        def _(dve):
            dve.wait_ge(s["reach"], 16)
            for j in range(VJ):
                if j:
                    dve.wait_ge(s["count"], j)
                dve.tensor_scalar(below[0:VP], reach_all[0:VP], visit_no[0:VP, j:j + 1], None,
                                  ALU.is_lt).then_inc(s["below"], 1)
                dve.wait_ge(s["below"], j + 1)
                dve.tensor_reduce(tile_of[0:VP, j:j + 1], below[0:VP], AX, ALU.add).then_inc(s["count"], 1)
            dve.wait_ge(s["count"], VJ)
            dve.tensor_copy(tile_idx[0:VP], tile_of[0:VP]).then_inc(s["index"], 1)
            dve.tensor_tensor(block_of[0:VP], visit_no[0:VP], tile_of[0:VP], ALU.subtract).then_inc(s["tile"], 1)
            dve.wait_ge(s["tile"], 1)
            dve.tensor_copy(block_i[0:VP], block_of[0:VP])
            dve.tensor_scalar(block_off[0:VP], block_of[0:VP], -float(P), None, ALU.mult).then_inc(s["off"], 1)
            dve.wait_ge(s["off"], 1)
            dve.wait_ge(s["got"], 16 * VJ)
            dst_v = got[0:VP, :, 2 * P:3 * P]
            dve.tensor_tensor(keyrel[0:VP], dst_v, along(block_off[0:VP], 2, P), ALU.add).then_inc(s["rel"], 1)
            dve.wait_ge(s["rel"], 1)
            dve.tensor_copy(keyrel_b[0:VP], keyrel[0:VP])
            dve.tensor_scalar(over[0:VP], keyrel[0:VP], 0.0, 8192.0, ALU.is_lt, ALU.mult).then_inc(s["m1"], 1)
            dve.wait_ge(s["m1"], 1)
            dve.tensor_tensor(key[0:VP], dst_v, over[0:VP], ALU.add).then_inc(s["m2"], 1)
            dve.wait_ge(s["m2"], 1)
            dve.tensor_scalar(over[0:VP], keyrel[0:VP], P - 0.5, 8192.0, ALU.is_gt, ALU.mult).then_inc(s["m1"], 1)
            dve.wait_ge(s["m1"], 2)
            dve.tensor_tensor(key[0:VP], key[0:VP], over[0:VP], ALU.add).then_inc(s["last"], 1)
            for n, to in enumerate((k.idx_key, k.idx_value, k.keycol)):
                for half in range(2):
                    dve.wait_ge(s["turned"], 2 * n + half + 1)
                    dve.tensor_copy(to[:, half * 4 * VP:(half + 1) * 4 * VP],
                                    k.psum[:, 2 * n + half, 0:4 * VP]).then_inc(s["copied"], 1)

        @block.gpsimd
        def _(pool):
            pool.wait_ge(s["index"], 1)
            for j in range(VJ):
                pool.indirect_dma_start(out=got[0:VP, j, :], out_offset=None, in_=dram.comb,
                                        in_offset=bass.IndirectOffsetOnAxis(ap=tile_idx[0:VP, j:j + 1], axis=0)
                                        ).then_inc(s["got"], 16)

        @block.tensor
        def _(pe):
            pe.wait_ge(s["got"], 16 * VJ)
            pe.wait_ge(s["rel"], 1)
            for n in range(3):
                for half in range(2):
                    for q in range(4):
                        j = half * 4 + q
                        of = got[0:VP, j, n * P:(n + 1) * P] if n < 2 else keyrel[0:VP, j, :]
                        t = pe.transpose(k.psum[:, 2 * n + half, q * VP:(q + 1) * VP], of, k.ident[0:VP, 0:VP])
                    t.then_inc(s["turned"], 1)

    a = Arena(k.arena, k.words)
    blocks_all = a.take([V])
    key_run = a.take([CL + 2])
    differ = a.take([CL + 1], BF16)
    edge_f, edge_b = a.take([1]), a.take([1])
    upto, count, count_all, slot_no = a.take([V]), a.take([1]), a.take([NCH * NB]), a.take([NCH * NB])
    with stage(nc, "runs", "blocks keys filled differ pen edges stored upto count counts row made loaded") as (block, s):
        @block.sync
        def _(sp):
            sp.dma_start(blocks_all, dram.blocks_f.partition_broadcast(P)).then_inc(s["blocks"], 16)
            sp.dma_start(k.block_row[0:1, :], dram.blocks_i.unsqueeze(0)).then_inc(s["loaded"], 16)
            sp.wait_ge(s["filled"], 1)
            sp.dma_start(key_run[:, 1:CL + 1], spread(dram.key, 0, [CL, SC], [0, H], [1, CL])).then_inc(s["keys"], 16)
            with nc.allow_non_contiguous_dma(reason="once, a word per partition"):
                sp.dma_start(key_run[H:P, 0:1], spread(dram.key, CL - 1, [CL, SC - 1], [0, H], [1, 1])).then_inc(s["keys"], 16)
                sp.dma_start(key_run[0:P - H, CL + 1:CL + 2],
                             spread(dram.key, CL, [CL, SC - 1], [0, H], [1, 1])).then_inc(s["keys"], 16)
                sp.wait_ge(s["edges"], 2)
                sp.dma_start(dram.edge_f, edge_f[:, 0]).then_inc(s["stored"], 16)
                sp.dma_start(dram.edge_b, edge_b[:, 0]).then_inc(s["stored"], 16)
                sp.wait_ge(s["count"], 1)
                sp.dma_start(dram.counts, count[0:NCH * NB, 0]).then_inc(s["stored"], 16)
                sp.wait_ge(s["stored"], 48)
                sp.dma_start(k.edge_f8[0:H, :], dram.edge_f.rearrange("(c h) -> h c", h=H)).then_inc(s["loaded"], 16)
                sp.dma_start(k.edge_b8[0:H, :], dram.edge_b.rearrange("(c h) -> h c", h=H)).then_inc(s["loaded"], 16)
                sp.dma_start(count_all, dram.counts.partition_broadcast(P)).then_inc(s["counts"], 16)
            sp.wait_ge(s["loaded"], 48)

        @block.gpsimd
        def _(pool):
            pool.iota(slot_no, pattern=[[0, NCH * NB]], base=-P, channel_multiplier=1,
                      allow_small_or_imprecise_dtypes=True).then_inc(s["made"], 1)

        @block.vector
        def _(dve):
            dve.memset(key_run[:, 0:CL + 2:CL + 1], -1.0).then_inc(s["filled"], 1)
            dve.wait_ge(s["blocks"], 16)
            dve.memset(k.same_block[:, 0:1], 0.0)
            dve.tensor_tensor(k.same_block[:, 1:V], blocks_all[:, 1:V], blocks_all[:, 0:V - 1], ALU.is_equal)
            dve.wait_ge(s["keys"], 48)
            dve.wait_ge(s["filled"], 1)
            dve.tensor_tensor(differ, key_run[:, 0:CL + 1], key_run[:, 1:CL + 2], ALU.not_equal).then_inc(s["differ"], 1)
            dve.wait_ge(s["differ"], 1)
            dve.tensor_scalar(k.breaks[:, 0:CL + 1], differ, -BIG, None, ALU.mult).then_inc(s["pen"], 1)
            dve.wait_ge(s["pen"], 1)
            dve.tensor_reduce(edge_f, k.breaks[:, 0:CL], AX, ALU.min).then_inc(s["edges"], 1)
            dve.tensor_reduce(edge_b, k.breaks[:, 1:CL + 1], AX, ALU.min).then_inc(s["edges"], 1)
            B52 = NCH * NB
            dve.tensor_scalar(upto[0:B52], blocks_all[0:B52], k.iota_col[0:B52], None, ALU.is_le).then_inc(s["upto"], 1)
            dve.wait_ge(s["upto"], 1)
            dve.tensor_reduce(count[0:B52], upto[0:B52], AX, ALU.add).then_inc(s["count"], 1)
            dve.wait_ge(s["counts"], 16)
            dve.wait_ge(s["made"], 1)
            dve.scalar_tensor_tensor(k.idx_sums[:, :], count_all, float(P), slot_no, ALU.mult, ALU.add).then_inc(s["row"], 1)


def passed(eng, s, sem, value):
    eng.wait_ge(sem, value)
    eng.sem_inc(s["passed"], 1)


def normalize(dve, s, tag, n, x, out, stats, moments, rstd, scale=None, shift=None):
    step = lambda name: s[f"{tag}_{name}"]
    for q in range(NB):
        ins = dve.bn_stats(stats[:, q, :], x[:, q, :])
    ins.then_inc(step("stats"), 1)
    passed(dve, s, step("stats"), n)
    for q in range(NB):
        ins = dve.bn_aggr(moments[:, q, :], stats[:, q, :])
    ins.then_inc(step("moments"), 1)
    dve.wait_ge(step("rstd"), n)
    for q in range(NB):
        ins = dve.tensor_scalar(out[:, q, :], x[:, q, :], moments[:, q, 0:1], rstd[:, q:q + 1],
                                ALU.subtract, ALU.mult)
    ins.then_inc(step("unit"), 1)
    if scale is not None:
        dve.wait_ge(step("unit"), n)
        dve.tensor_tensor(out, out, along(scale, 1, NB), ALU.mult).then_inc(step("scaled"), 1)
        dve.wait_ge(step("scaled"), n)
        dve.tensor_tensor(out, out, along(shift, 1, NB), ALU.add).then_inc(step("shifted"), 1)


def inverse_root(pool, s, tag, n, moments, rstd, eps, minus_half):
    step = lambda name: s[f"{tag}_{name}"]
    pool.wait_ge(step("moments"), n)
    pool.tensor_tensor(rstd, moments[:, :, 1], eps, ALU.add).then_inc(step("eps"), 1)
    pool.wait_ge(step("eps"), n)
    pool.tensor_tensor(rstd, rstd, minus_half, ALU.pow).then_inc(step("rstd"), 1)


def norm_sems(tag):
    return " ".join(f"{tag}_{n}" for n in ("stats", "moments", "eps", "rstd", "unit", "scaled", "shifted"))


def chunk_rows(dram, c):
    return dram[ds(c * CH, CH), :].rearrange("(q p) d -> p q d", p=P)


def build_input_norm(nc, k, x, dram):
    a = Arena(k.arena, k.words)
    rows, unit = a.take([NB, D]), a.take([NB, D])
    stats, moments, rstd = a.take([NB, 6]), a.take([NB, 2]), a.take([NB])
    eps, minus_half = a.take([NB]), a.take([NB])
    with stage(nc, "innorm", "loaded stored consts passed " + norm_sems("ln")) as (block, s):
        @block.sync
        def _(sp):
            with sp.Fori(0, NCH) as c:
                sp.wait_ge(s["ln_unit"], c)
                sp.dma_start(rows, chunk_rows(x, c)).then_inc(s["loaded"], 16)

        @block.gpsimd
        def _(pool):
            pool.memset(eps, 1e-5)
            pool.memset(minus_half, -0.5).then_inc(s["consts"], 1)
            pool.wait_ge(s["consts"], 1)
            with pool.Fori(0, NCH) as c:
                inverse_root(pool, s, "ln", c + 1, moments, rstd, eps, minus_half)

        @block.vector
        def _(dve):
            with dve.Fori(0, NCH) as c:
                dve.wait_ge(s["loaded"], 16 * (c + 1))
                dve.wait_ge(s["stored"], 32 * c)
                normalize(dve, s, "ln", c + 1, rows, unit, stats, moments, rstd)

        @block.scalar
        def _(act):
            with act.Fori(0, NCH) as c:
                act.wait_ge(s["ln_unit"], c + 1)
                act.dma_start(chunk_rows(dram.xn, c), unit).then_inc(s["stored"], 16)
                act.dma_start(chunk_rows(dram.state, c), unit).then_inc(s["stored"], 16)
            act.wait_ge(s["stored"], 32 * NCH)


def build_type_weights(nc, k, w, layer, weights):
    a = Arena(k.arena, k.words)
    a.take([H, 5 * HD])
    wk = a.take([H, HD])
    we = a.take([H, TE, HD], parts=HD)
    wkT = a.take([H, P], parts=HD)
    mu = a.take([H * TE])
    with stage(nc, "typew", "loaded turned copied merged") as (block, s):
        @block.sync
        def _(sp):
            for t in range(TN):
                part = slice(t * HD, (t + 1) * HD)
                for of, to in ((w["W_Q"], weights[part, :, 0:HD]), (w["W_V"], weights[part, :, HD:2 * HD]),
                               (w["W_K"], wk[part])):
                    sp.dma_start(to, of[ds(layer, 1), t].rearrange("a h d e -> (a d) h e")).then_inc(s["loaded"], 16)

        @block.scalar
        def _(act):
            for e in range(TE):
                act.dma_start(we[:, :, e, :],
                              w["W_E"][ds(layer, 1), e].rearrange("a h d e -> (a d) h e")).then_inc(s["loaded"], 16)
            act.dma_start(mu, w["mu"][ds(layer, 1)].rearrange("a h t -> (a h t)").partition_broadcast(P)
                          ).then_inc(s["loaded"], 16)

        @block.tensor
        def _(pe):
            pe.wait_ge(s["loaded"], 16 * (3 * TN + TE + 1))
            for h in range(H):
                t = pe.transpose(k.psum[0:HD, h // 4, (h % 4) * P:(h % 4 + 1) * P], wk[:, h, :], k.ident[:, :])
            t.then_inc(s["turned"], 1)
            pe.wait_ge(s["copied"], 1)
            for h in range(H):
                t = pe.matmul(k.psum[:, 2 + h // 4, (h % 4) * P:(h % 4) * P + TE * HD], wkT[:, h, :],
                              we[:, h, :, :].rearrange("p a b -> p (a b)"), start=True, stop=True)
            t.then_inc(s["merged"], 1)

        @block.vector
        def _(dve):
            dve.wait_ge(s["turned"], 1)
            dve.tensor_copy(wkT, k.psum[0:HD, 0:2, :].rearrange("p b (h n) -> p (b h) n", n=P)).then_inc(s["copied"], 1)
            dve.wait_ge(s["merged"], 1)
            dve.wait_ge(s["loaded"], 16 * (3 * TN + TE + 1))
            for h in range(H):
                dve.scalar_tensor_tensor(
                    weights[:, h, 2 * HD:5 * HD].rearrange("p (t f) -> p t f", t=TE),
                    k.psum[:, 2 + h // 4, (h % 4) * P:(h % 4) * P + TE * HD].rearrange("p (t f) -> p t f", t=TE),
                    float(HD) ** -0.5, along(mu[:, h * TE:(h + 1) * TE], 2, HD), ALU.mult, ALU.mult)


def build_rows(nc, k, weights, dram):
    a = Arena(k.arena, k.words)
    a.take([H, 5 * HD])
    x = [a.take([D]) for _ in range(2)]
    placed = [a.take([H, TN * HD]) for _ in range(2)]
    placedT = [a.take([H, P]) for _ in range(2)]
    q_row = [a.take([D]) for _ in range(2)]
    v_row = [a.take([H, HD + 1]) for _ in range(2)]
    k_row = [a.take([TE * D]) for _ in range(2)]
    names = "x0 x1 placed turned copied multiplied evac_lo evac_hi stored_qv0 stored_qv1 stored_k0 stored_k1 passed ones"
    with stage(nc, "rows", names, True) as (block, s):
        s_x, s_qv, s_k = [s["x0"], s["x1"]], [s["stored_qv0"], s["stored_qv1"]], [s["stored_k0"], s["stored_k1"]]

        def move(copy, b, half):
            out = k.psum[:, 2 + 3 * b + half, :].rearrange("p (g h d) -> p g h d", g=4, h=4)
            copy(q_row[b][:, half * P:(half + 1) * P], out[:, 0].rearrange("p h d -> p (h d)"))
            copy(v_row[b][:, half * 4:(half + 1) * 4, 0:HD], out[:, 1])
            return copy(k_row[b].rearrange("p (e c) -> p e c", e=TE)[:, 0:2, half * P:(half + 1) * P],
                        out[:, 2:4].rearrange("p e h d -> p e (h d)"))

        @block.sync
        def _(sp):
            for sem in (s["placed"], s["turned"], s["multiplied"], s["evac_lo"], s["evac_hi"]):
                sp.sem_inc(sem, 2)
            sp.sem_inc(s["copied"], 1)
            with sp.Fori(0, NP // P // 2) as i:
                for b in range(2):
                    sp.wait_ge(s["placed"], 2 * i + b + 1)
                    sp.dma_start(x[b], dram.state[ds((2 * i + b) * P, P), :]).then_inc(s_x[b], 16)

        @block.vector
        def _(dve):
            for b in range(2):
                dve.memset(v_row[b][:, :, HD:HD + 1], 1.0).then_inc(s["ones"], 1)
            with dve.Fori(0, NP // P // 2) as i:
                for b in range(2):
                    n = 2 * i + b
                    dve.wait_ge(s_x[b], 16 * i + 16)
                    dve.wait_ge(s["turned"], n + 1)
                    dve.tensor_tensor(
                        placed[b].rearrange("p h (t d) -> p h t d", t=TN),
                        along(x[b].rearrange("p (h d) -> p h d", h=H), 2, TN),
                        along(along(k.onehot[:, ds(n, 1), :].rearrange("p a t -> p (a t)"), 1, H), 3, HD),
                        ALU.mult).then_inc(s["placed"], 1)
                for b in range(2):
                    n = 2 * i + b
                    dve.wait_ge(s["multiplied"], n + 3)
                    dve.wait_ge(s_qv[b], 32 * i)
                    dve.wait_ge(s_k[b], 16 * i)
                    move(dve.tensor_copy, b, 1).then_inc(s["evac_hi"], 1)

        @block.scalar
        def _(act):
            with act.Fori(0, NP // P // 2) as i:
                for b in range(2):
                    n = 2 * i + b
                    act.wait_ge(s["turned"], n + 3)
                    act.wait_ge(s["multiplied"], n + 1)
                    act.copy(placedT[b].rearrange("p h n -> p (h n)"),
                             k.psum[:, 0:2, :].rearrange("p a b -> p (a b)")).then_inc(s["copied"], 1)
                for b in range(2):
                    n = 2 * i + b
                    act.wait_ge(s["multiplied"], n + 3)
                    act.wait_ge(s_k[b], 16 * i)
                    act.wait_ge(s_qv[b], 32 * i)
                    move(act.copy, b, 0)
                    act.copy(k_row[b][:, 2 * D:], k.psum[:, 4 + 3 * b, 0:D]).then_inc(s["evac_lo"], 1)
                    act.wait_ge(s["evac_lo"], n + 3)
                    act.wait_ge(s["evac_hi"], n + 3)
                    act.dma_start(dram.key_rows[ds(n * P * TE, P * TE), :].rearrange("(p e) d -> p (e d)", e=TE),
                                  k_row[b]).then_inc(s_k[b], 16)
            for b in range(2):
                act.wait_ge(s_k[b], 16 * (NP // P // 2))

        @block.tensor
        def _(pe):
            with pe.Fori(0, NP // P // 2) as i:
                for b in range(2):
                    n = 2 * i + b
                    pe.wait_ge(s["placed"], n + 3)
                    pe.wait_ge(s["copied"], n + 1)
                    for h in range(H):
                        t = pe.transpose(k.psum[:, h // 4, (h % 4) * P:(h % 4 + 1) * P], placed[b][:, h, :],
                                         k.ident[:, :])
                    t.then_inc(s["turned"], 1)
                for b in range(2):
                    n = 2 * i + b
                    pe.wait_ge(s["copied"], n + 2)
                    pe.wait_ge(s["evac_lo"], n + 1)
                    pe.wait_ge(s["evac_hi"], n + 1)
                    for h in range(H):
                        out = k.psum[:, 2 + 3 * b + h // 4, :].rearrange("p (g h d) -> p g h d", g=4, h=4)
                        pe.matmul(out[:, :, h % 4, :], placedT[b][:, h, :], weights[:, h, 0:4 * HD],
                                  start=True, stop=True)
                        t = pe.matmul(k.psum[:, 4 + 3 * b, h * HD:(h + 1) * HD], placedT[b][:, h, :],
                                      weights[:, h, 4 * HD:5 * HD], start=True, stop=True)
                    t.then_inc(s["multiplied"], 1)

        @block.gpsimd
        def _(pool):
            pool.wait_ge(s["ones"], 2)
            with pool.Fori(0, NP // P // 2) as i:
                for b in range(2):
                    n = 2 * i + b
                    passed(pool, s, s["evac_lo"], n + 3)
                    passed(pool, s, s["evac_hi"], n + 3)
                    pool.dma_start(dram.q[ds(n * P, P), :], q_row[b]).then_inc(s_qv[b], 16)
                    pool.dma_start(dram.value_rows[ds(n * P, P), :],
                                   v_row[b].rearrange("p h d -> p (h d)")).then_inc(s_qv[b], 16)
            for b in range(2):
                pool.wait_ge(s_qv[b], 32 * (NP // P // 2))


def gather_idx(pool, s, slot, idx, n):
    pool.tensor_copy(slot, idx[:, ds(n * 4, 4)]).then_inc(s["indexed"], 1)
    passed(pool, s, s["indexed"], n + 1)


def build_scores(nc, k, dram):
    a = Arena(k.arena, k.words)
    key_ring = a.take([GV, D])
    query_ring = a.take([GV, D])
    cols = [a.take([4 * P], BF16) for _ in range(2)]
    pick = [a.take([4, P]) for _ in range(2)]
    prod = [a.take([4 * H, HD]) for _ in range(2)]
    index = [a.take([4], I32) for _ in range(GH)]
    names = "picked spread multiplied scored indexed passed cols0 cols1 " + \
        " ".join(f"key{q} query{q}" for q in range(GV))
    with stage(nc, "scores", names, True) as (block, s):
        s_key = [s[f"key{q}"] for q in range(GV)]
        s_query = [s[f"query{q}"] for q in range(GV)]
        s_cols = [s["cols0"], s["cols1"]]

        @block.sync
        def _(sp):
            sp.sem_inc(s["picked"], 2)
            for sem in (s["spread"], s["multiplied"], s["scored"]):
                sp.sem_inc(sem, GH)
            with sp.Fori(0, NG) as i:
                for h in range(GH):
                    n = i * GH + h
                    _, rows = nc.values_load_multi_w_load_instructions(
                        k.block_row[0:1, ds(n * 4, 4)], engines=(mybir.EngineType.SP,),
                        min_val=0, max_val=BLK - 1)
                    sp.wait_ge(s["spread"], n + 1)
                    for q in range(4):
                        sp.dma_start(query_ring[:, 4 * h + q, :],
                                     dram.q[ds(rows[q] * P, P), :]).then_inc(s_query[4 * h + q], 16)

        @block.scalar
        def _(act):
            with act.Fori(0, NG) as i:
                for h in range(GH):
                    n = i * GH + h
                    act.wait_ge(s["picked"], n + 1)
                    act.dma_start(cols[h % 2], dram.keyrow[ds(n * 4, 4), :].rearrange("v s -> (v s)")
                                  .partition_broadcast(P)).then_inc(s_cols[h % 2], 16)

        @block.gpsimd
        def _(pool):
            with pool.Fori(0, NG) as i:
                for h in range(GH):
                    n = i * GH + h
                    passed(pool, s, s["multiplied"], n + 1)
                    gather_idx(pool, s, index[h], k.idx_key, n)
                    for q in range(4):
                        pool.indirect_dma_start(
                            out=key_ring[:, 4 * h + q, :], out_offset=None, in_=dram.key_rows,
                            in_offset=bass.IndirectOffsetOnAxis(ap=index[h][:, q:q + 1], axis=0)
                        ).then_inc(s_key[4 * h + q], 16)

        @block.tensor
        def _(pe):
            with pe.Fori(0, NG) as i:
                for h in range(GH):
                    n = i * GH + h
                    pe.wait_ge(s["picked"], n + 3)
                    pe.wait_ge(s["multiplied"], n + GH - 1)
                    for q in range(4):
                        pe.wait_ge(s_query[4 * h + q], 16 * i + 16)
                        t = pe.matmul(k.psum[:, 2 * (h % 2) + q // 2, (q % 2) * D:(q % 2 + 1) * D],
                                      pick[h % 2][:, q, :], query_ring[:, 4 * h + q, :], start=True, stop=True)
                    t.then_inc(s["spread"], 1)

        @block.vector
        def _(dve):
            def choose(i, h):
                n = i * GH + h
                dve.wait_ge(s_cols[h % 2], (i * GH + h - h % 2) * 8 + 16)
                dve.wait_ge(s["spread"], n + GH - 1)
                dve.tensor_scalar(pick[h % 2].rearrange("p v s -> p (v s)"), cols[h % 2], k.iota_col[:, 0:1], None,
                                  ALU.is_equal).then_inc(s["picked"], 1)

            def multiply(i, h):
                n = i * GH + h
                dve.wait_ge(s["spread"], n + GH + 1)
                dve.wait_ge(s["scored"], n + GH - 1)
                for q in range(4):
                    dve.wait_ge(s_key[4 * h + q], 16 * i + 16)
                b = 2 * (h % 2)
                dve.tensor_tensor(prod[h % 2].rearrange("p a d -> p (a d)"),
                                  k.psum[:, b:b + 2, :].rearrange("p b n -> p (b n)"),
                                  key_ring[:, 4 * h:4 * h + 4, :].rearrange("p q d -> p (q d)"),
                                  ALU.mult).then_inc(s["multiplied"], 1)

            def reduce(i, h):
                n = i * GH + h
                passed(dve, s, s["multiplied"], n + GH + 1)
                dve.tensor_reduce(k.scores[:, ds(n * 4 * H, 4 * H)], prod[h % 2], AX,
                                  ALU.add).then_inc(s["scored"], 1)

            with dve.Fori(0, NG) as i:
                choose(i, 0)
                for h in range(GH):
                    if h + 1 < GH:
                        choose(i, h + 1)
                    multiply(i, h)
                    if h:
                        reduce(i, h - 1)
                reduce(i, GH - 1)


def build_softmax(nc, k, dram):
    a = Arena(k.arena, k.words)
    last, initial = a.take([4]), a.take([4])
    state8, last8 = a.take([4, SC]), a.take([4, SC])
    by_visit = k.scores[:, :].rearrange("p (c k h) -> p k c h", c=SC, k=VK)
    with stage(nc, "toscan", "ordered turned copied") as (block, s):
        @block.vector
        def _(dve):
            for g in range(VK // 4):
                dve.tensor_copy(k.stream[:, g * 512:(g + 1) * 512].rearrange("p (k c h) -> p k c h", k=4, c=SC),
                                by_visit[:, 4 * g:4 * g + 4]).then_inc(s["ordered"], 1)

        @block.tensor
        def _(pe):
            for g in range(VK // 4):
                pe.wait_ge(s["ordered"], g + 1)
                if g >= 2:
                    pe.wait_ge(s["copied"], g - 1)
                for q in range(4):
                    t = pe.transpose(k.psum[:, g % 2, q * P:(q + 1) * P],
                                     k.stream[:, (4 * g + q) * P:(4 * g + q + 1) * P], k.ident[:, :])
                t.then_inc(s["turned"], 1)

        @block.scalar
        def _(act):
            act.wait_ge(s["ordered"], VK // 4)
            for g in range(VK // 4):
                act.wait_ge(s["turned"], g + 1)
                act.copy(k.scores[:, g * 512:(g + 1) * 512], k.psum[:, g % 2, :]).then_inc(s["copied"], 1)

    with stage(nc, "scan", "initial scanned stored back chained sent loaded maximum less") as (block, s):
        passes = [(False, k.breaks[:, 0:CL], k.edge_f8, k.scores, CL - 1),
                  (True, k.breaks[:, 1:CL + 1], k.edge_b8, k.stream, 0)]

        @block.vector
        def _(dve):
            dve.memset(initial, -BIG).then_inc(s["initial"], 1)
            dve.wait_ge(s["initial"], 1)
            for n, (backward, breaks, edges, data, end) in enumerate(passes):
                turn = (lambda ap: ap[:, ::-1]) if backward else (lambda ap: ap)
                out = k.arena[:, 64:64 + CL]
                dve.tensor_tensor_scan(turn(out), turn(breaks), turn(data[:, 0:CL]), initial[:, 3:4],
                                       ALU.add, ALU.max).then_inc(s["scanned"], 1)
                dve.wait_ge(s["back"], 16 * (n + 1))
                dve.tensor_tensor_scan(turn(state8[0:H, n]), turn(edges[0:H, :]), turn(last8[0:H, n]), -BIG,
                                       ALU.add, ALU.max).then_inc(s["chained"], 1)
                dve.wait_ge(s["loaded"], 16 * (n + 1))
                dve.tensor_tensor_scan(turn(k.stream[:, 0:CL]), turn(breaks), turn(data[:, 0:CL]),
                                       initial[:, n:n + 1], ALU.add, ALU.max).then_inc(s["maximum"], 1)
                dve.wait_ge(s["maximum"], n + 1)
            dve.scalar_tensor_tensor(k.stream[:, 0:CL], k.stream[:, 0:CL], -1.0e9, k.scores[:, 0:CL],
                                     ALU.max, ALU.subtract).then_inc(s["less"], 1)

        @block.sync
        def _(sp):
            with nc.allow_non_contiguous_dma(reason="128 words"):
                for n, (backward, _, _, _, end) in enumerate(passes):
                    sp.wait_ge(s["scanned"], n + 1)
                    sp.dma_start(dram.carry[n], k.arena[:, 64 + end]).then_inc(s["stored"], 16)
                    sp.wait_ge(s["stored"], 16 * (n + 1))
                    sp.dma_start(last8[0:H, n], dram.carry[n].rearrange("(c h) -> h c", h=H)).then_inc(s["back"], 16)
                    sp.wait_ge(s["chained"], n + 1)
                    sp.dma_start(dram.carried[n].rearrange("(c h) -> h c", h=H), state8[0:H, n]).then_inc(s["sent"], 16)
                    sp.wait_ge(s["sent"], 16 * (n + 1))
                    to, of = (slice(0, P - H), slice(H, P)) if backward else (slice(H, P), slice(0, P - H))
                    sp.dma_start(initial[to, n:n + 1], dram.carried[n, of].unsqueeze(1)).then_inc(s["loaded"], 16)

        @block.scalar
        def _(act):
            act.wait_ge(s["less"], 1)
            act.activation(k.stream[:, 0:CL], k.stream[:, 0:CL], ACT.Exp, scale=-1.0)

    with stage(nc, "fromscan", "turned copied") as (block, s):
        weights = k.scores[:, :].rearrange("p (c k h) -> p k c h", c=SC, k=VK)

        @block.tensor
        def _(pe):
            for g in range(VK // 4):
                if g >= 2:
                    pe.wait_ge(s["copied"], g - 1)
                for q in range(4):
                    t = pe.transpose(k.psum[:, g % 2, q * P:(q + 1) * P],
                                     k.stream[:, (4 * g + q) * P:(4 * g + q + 1) * P], k.ident[:, :])
                t.then_inc(s["turned"], 1)

        @block.scalar
        def _(act):
            for g in range(VK // 4):
                act.wait_ge(s["turned"], g + 1)
                act.copy(weights[:, 4 * g:4 * g + 4], k.psum[:, g % 2, :].rearrange("p (k c h) -> p k c h", k=4, c=SC)
                         ).then_inc(s["copied"], 1)


def build_sums(nc, k, dram):
    a = Arena(k.arena, k.words)
    values = a.take([GV, RW])
    pick = [a.take([4, P]) for _ in range(2)]
    weighed = [a.take([4, RW]) for _ in range(2)]
    sums = a.take([GV, RW])
    index = [a.take([4], I32) for _ in range(GH)]
    names = "picked weighed multiplied summed indexed passed cleared " + \
        " ".join(f"value{q}" for q in range(GV)) + " " + " ".join(f"stored{h}" for h in range(GH))
    with stage(nc, "sums", names, True) as (block, s):
        s_value = [s[f"value{q}"] for q in range(GV)]
        s_stored = [s[f"stored{h}"] for h in range(GH)]

        @block.sync
        def _(sp):
            for sem in (s["picked"], s["weighed"], s["multiplied"]):
                sp.sem_inc(sem, GH)
            sp.sem_inc(s["summed"], GV)
            with sp.Fori(0, NG) as i:
                for h in range(GH):
                    n = i * GH + h
                    sp.wait_ge(s["summed"], n * 4 + 4 + GV)
                    sp.dma_start(dram.sums[ds(n * 4 * P, 4 * P), :].rearrange("(q p) n -> p q n", p=P),
                                 sums[:, 4 * h:4 * h + 4, :]).then_inc(s_stored[h], 16)
            for h in range(GH):
                sp.wait_ge(s_stored[h], 16 * NG)

        @block.gpsimd
        def _(pool):
            with pool.Fori(0, NG) as i:
                for h in range(GH):
                    n = i * GH + h
                    passed(pool, s, s["weighed"], n + 1)
                    gather_idx(pool, s, index[h], k.idx_value, n)
                    for q in range(4):
                        pool.indirect_dma_start(
                            out=values[:, 4 * h + q, :], out_offset=None, in_=dram.value_rows,
                            in_offset=bass.IndirectOffsetOnAxis(ap=index[h][:, q:q + 1], axis=0)
                        ).then_inc(s_value[4 * h + q], 16)

        @block.tensor
        def _(pe):
            with pe.Fori(0, NG) as i:
                for h in range(GH):
                    n = i * GH + h
                    pe.wait_ge(s["picked"], n + GH + 1)
                    pe.wait_ge(s["weighed"], n + GH + 1)
                    for q in range(4):
                        pe.wait_ge(s["summed"], n * 4 + q + 1 + GV - 8)
                        t = pe.matmul(k.psum[:, 4 * (h % 2) + q, 0:RW], pick[h % 2][:, q, :],
                                      weighed[h % 2][:, q, :], start=True, stop=True)
                    t.then_inc(s["multiplied"], 1)

        @block.vector
        def _(dve):
            dve.memset(sums, 0.0).then_inc(s["cleared"], 1)
            dve.wait_ge(s["cleared"], 1)
            weights = k.scores[:, :].rearrange("p (v h) -> p v h", h=H)

            def choose(i, h):
                n = i * GH + h
                dve.wait_ge(s["multiplied"], n + GH - 1)
                dve.tensor_tensor(pick[h % 2], along(k.iota_row[:, :], 1, 4),
                                  along(k.keycol[:, ds(n * 4, 4)], 2, P), ALU.is_equal).then_inc(s["picked"], 1)

            def weigh(i, h, pair):
                n = i * GH + h
                for q in (pair, pair + 1):
                    dve.wait_ge(s_value[4 * h + q], 16 * i + 16)
                ins = dve.tensor_tensor(
                    weighed[h % 2][:, pair:pair + 2].rearrange("p q (h d) -> p q h d", h=H),
                    values[:, 4 * h + pair:4 * h + pair + 2, :].rearrange("p q (h d) -> p q h d", h=H),
                    along(weights[:, ds(n * 4 + pair, 2), :], 3, HD + 1), ALU.mult)
                if pair:
                    ins.then_inc(s["weighed"], 1)

            def add(i, h, q):
                n = i * GH + h
                m = n * 4 + q
                if q == 0:
                    dve.wait_ge(s["multiplied"], n + GH + 1)
                    dve.wait_ge(s_stored[h], 16 * i)
                dve.wait_ge(s["summed"], m + GV)
                at = 4 * h + q
                dve.scalar_tensor_tensor(sums[:, at, :], sums[:, (at - 1) % GV, :], k.same_block[:, ds(m, 1)],
                                         k.psum[:, 4 * (h % 2) + q, 0:RW], ALU.mult, ALU.add).then_inc(s["summed"], 1)

            def turn(i, first=False, last=False):
                for h in range(GH):
                    ahead = (i, h + 1) if h + 1 < GH else (i + 1, 0)
                    back = (i, h - 1) if h else (i - 1, GH - 1)
                    more, had = not (last and h + 1 == GH), not (first and h == 0)
                    if more:
                        choose(*ahead)
                    if had:
                        add(*back, 0)
                    if more:
                        weigh(*ahead, 0)
                    if had:
                        add(*back, 1)
                    if more:
                        weigh(*ahead, 2)
                    if had:
                        add(*back, 2)
                        add(*back, 3)

            choose(0, 0)
            weigh(0, 0, 0)
            weigh(0, 0, 2)
            turn(0, first=True)
            with dve.Fori(1, NG - 1) as i:
                turn(i)
            turn(NG - 1, last=True)
            for q in range(4):
                add(NG - 1, GH - 1, q)


class Kept:
    pass


class Dram:
    pass


def setup(nc, ctx):
    k, dram = Kept(), Dram()

    def sb(name, shape, dtype=F32):
        return ctx.enter_context(nc.sbuf_tensor(name, shape, dtype))

    k.ident = sb("ident", [P, P])
    k.iota_row = sb("iota_row", [P, P])
    k.iota_col = sb("iota_col", [P, 1])
    k.idx_key = sb("idx_key", [P, V], I32)
    k.idx_value = sb("idx_value", [P, V], I32)
    k.keycol = sb("keycol", [P, V])
    k.same_block = sb("same_block", [P, V])
    k.block_row = sb("block_row", [1, V], I32)
    k.idx_sums = sb("idx_sums", [P, NCH * NB], I32)
    k.onehot = sb("onehot", [P, NCH * NB, TN])
    k.breaks = sb("breaks", [P, CL + 1], BF16)
    k.edge_f8 = sb("edge_f8", [H, SC])
    k.edge_b8 = sb("edge_b8", [H, SC])
    k.scores = sb("scores", [P, V * H])
    k.stream = sb("stream", [P, V * H])
    k.words = 30000
    k.arena = ctx.enter_context(nc.sbuf_tensor("arena", [P, k.words], F32))
    k.psum = ctx.enter_context(nc.psum_tensor("psum", [P, 8, 512], F32))

    def dr(name, shape, dtype=F32):
        return nc.dram_tensor(f"scratch_{name}", shape, dtype, kind="Internal").ap()

    dram.comb = dr("comb", (TILES, 3 * P))
    dram.reach = dr("reach", (TILES,))
    dram.keyrow = dr("keyrow", (V, P), BF16)
    dram.key = dr("key", (V * P,))
    dram.blocks_i = dr("blocks_i", (V,), I32)
    dram.blocks_f = dr("blocks_f", (V,))
    dram.edge_f = dr("edge_f", (P,))
    dram.edge_b = dr("edge_b", (P,))
    dram.counts = dr("counts", (NCH * NB,))
    dram.carry = dr("carry", (4, P))
    dram.carried = dr("carried", (4, P))
    dram.state = dr("state", (NP, D))
    dram.xn = dr("xn", (NP, D))
    dram.q = dr("q", (NP, D))
    dram.key_rows = dr("key_rows", (NP * TE, D))
    dram.value_rows = dr("value_rows", (NP, RW))
    dram.sums = dr("sums", (V * P, RW))
    return k, dram


def transpose_chunk(pe, k, banks, rows):
    for f in range(2):
        for q in range(NB):
            t = pe.transpose(k.psum[:, banks + f, q * P:(q + 1) * P], rows[:, q, f * P:(f + 1) * P], k.ident[:, :])
    return t


def two_banks(k, bank):
    return k.psum[:, bank:bank + 2, :].rearrange("p a (b d) -> p (a b) d", d=D)


def copy_turned(act, k, bank, to):
    return act.copy(to.rearrange("p f n -> p (f n)"), k.psum[:, bank:bank + 2, :].rearrange("p a n -> p (a n)"))


def build_layer_tail(nc, k, w, layer, dram):
    a = Arena(k.arena, k.words)
    names = "bo ln1_g ln1_b b2 ln2_g ln2_b"
    vec = {n: a.take([D]) for n in names.split()}
    wo, w1, w2, b1 = a.take([2, D]), a.take([2, FF]), a.take([FF // P, D]), a.take([FF // P])
    index = a.take([NB], I32)
    got, state = a.take([NB, RW]), a.take([NB, D])
    total, inverse = a.take([NB, H]), a.take([NB, H])
    mean, y, unit = a.take([NB, D]), a.take([NB, D]), a.take([NB, D])
    meanT, unitT = a.take([2, CH]), a.take([2, CH])
    hidden = a.take([FF // P, CH])
    stats, moments, rstd = a.take([NB, 6]), a.take([NB, 2]), a.take([NB])
    eps, minus_half = a.take([NB]), a.take([NB])
    y2, out = a.take([NB, D]), a.take([NB, D])
    stats2, moments2, rstd2 = a.take([NB, 6]), a.take([NB, 2]), a.take([NB])
    with stage(nc, "tail", "weights consts indexed got0 got1 got2 got3 state total inverse mean turned1 copied1 "
               "attended added1 biased1 turned2 copied2 hidden gelu second added2 biased2 stored passed "
               + norm_sems("ln1") + " " + norm_sems("ln2"), True) as (block, s):
        s_got = [s["got0"], s["got1"], s["got2"], s["got3"]]
        n_weights = 16 * (len(vec) + 4)

        @block.sync
        def _(sp):
            lay = ds(layer, 1)
            for n, to in vec.items():
                sp.dma_start(to, w[n][lay, :].rearrange("a d -> (a d)").partition_broadcast(P)).then_inc(s["weights"], 16)
            sp.dma_start(wo, w["Wo"][lay].rearrange("a (f p) n -> (a p) f n", p=P)).then_inc(s["weights"], 16)
            sp.dma_start(w1, w["w1"][lay].rearrange("a (f p) n -> (a p) f n", p=P)).then_inc(s["weights"], 16)
            sp.dma_start(w2, w["w2"][lay].rearrange("a (f p) n -> (a p) f n", p=P)).then_inc(s["weights"], 16)
            with nc.allow_non_contiguous_dma(reason="once a layer"):
                sp.dma_start(b1, w["b1"][lay, :].rearrange("a (f p) -> (a p) f", p=P)).then_inc(s["weights"], 16)
            with sp.Fori(0, NCH) as c:
                sp.wait_ge(s["biased1"], c)
                sp.dma_start(state, chunk_rows(dram.state, c)).then_inc(s["state"], 16)

        @block.gpsimd
        def _(pool):
            pool.memset(eps, 1e-5)
            pool.memset(minus_half, -0.5).then_inc(s["consts"], 1)
            pool.wait_ge(s["consts"], 1)
            with pool.Fori(0, NCH) as c:
                passed(pool, s, s["mean"], c)
                pool.tensor_copy(index, k.idx_sums[:, ds(c * NB, NB)]).then_inc(s["indexed"], 1)
                passed(pool, s, s["indexed"], c + 1)
                for q in range(NB):
                    pool.indirect_dma_start(
                        out=got[:, q, :], out_offset=None, in_=dram.sums,
                        in_offset=bass.IndirectOffsetOnAxis(ap=index[:, q:q + 1], axis=0)).then_inc(s_got[q], 16)
                inverse_root(pool, s, "ln1", c + 1, moments, rstd, eps, minus_half)
                inverse_root(pool, s, "ln2", c + 1, moments2, rstd2, eps, minus_half)

        @block.vector
        def _(dve):
            dve.wait_ge(s["weights"], n_weights)
            with dve.Fori(0, NCH) as c:
                for q in range(NB):
                    dve.wait_ge(s_got[q], 16 * c + 16)
                rows = got.rearrange("p q (h d) -> p q h d", h=H)
                dve.tensor_scalar(total, rows[:, :, :, HD], 1e-10, None, ALU.add).then_inc(s["total"], 1)
                dve.wait_ge(s["total"], c + 1)
                dve.reciprocal(inverse, total).then_inc(s["inverse"], 1)
                dve.wait_ge(s["inverse"], c + 1)
                dve.tensor_tensor(mean.rearrange("p q (h d) -> p q h d", h=H), rows[:, :, :, 0:HD],
                                  along(inverse, 3, HD), ALU.mult).then_inc(s["mean"], 1)
                dve.wait_ge(s["attended"], c + 1)
                dve.wait_ge(s["state"], 16 * c + 16)
                dve.tensor_tensor(y, two_banks(k, 2), state, ALU.add).then_inc(s["added1"], 1)
                dve.wait_ge(s["added1"], c + 1)
                dve.tensor_tensor(y, y, along(vec["bo"], 1, NB), ALU.add).then_inc(s["biased1"], 1)
                dve.wait_ge(s["biased1"], c + 1)
                normalize(dve, s, "ln1", c + 1, y, unit, stats, moments, rstd, vec["ln1_g"], vec["ln1_b"])
                dve.wait_ge(s["second"], c + 1)
                dve.tensor_tensor(y2, two_banks(k, 2), unit, ALU.add).then_inc(s["added2"], 1)
                dve.wait_ge(s["added2"], c + 1)
                dve.tensor_tensor(y2, y2, along(vec["b2"], 1, NB), ALU.add).then_inc(s["biased2"], 1)
                dve.wait_ge(s["biased2"], c + 1)
                dve.wait_ge(s["stored"], 16 * c)
                normalize(dve, s, "ln2", c + 1, y2, out, stats2, moments2, rstd2, vec["ln2_g"], vec["ln2_b"])

        @block.tensor
        def _(pe):
            pe.wait_ge(s["weights"], n_weights)
            with pe.Fori(0, NCH) as c:
                pe.wait_ge(s["mean"], c + 1)
                transpose_chunk(pe, k, 0, mean).then_inc(s["turned1"], 1)
                pe.wait_ge(s["copied1"], c + 1)
                pe.wait_ge(s["added2"], c)
                for q in range(NB):
                    for f in range(2):
                        t = pe.matmul(two_banks(k, 2)[:, q, :], meanT[:, f, q * P:(q + 1) * P], wo[:, f, :],
                                      start=(f == 0), stop=(f == 1))
                t.then_inc(s["attended"], 1)
                pe.wait_ge(s["ln1_shifted"], c + 1)
                transpose_chunk(pe, k, 0, unit).then_inc(s["turned2"], 1)
                pe.wait_ge(s["copied2"], c + 1)
                for j in range(FF // P):
                    if j >= 4:
                        pe.wait_ge(s["gelu"], c * (FF // P) + j - 3)
                    for f in range(2):
                        t = pe.matmul(k.psum[:, 4 + j % 4, :], w1[:, f, j * P:(j + 1) * P], unitT[:, f, :],
                                      start=(f == 0), stop=(f == 1))
                    t.then_inc(s["hidden"], 1)
                pe.wait_ge(s["gelu"], (c + 1) * (FF // P))
                for q in range(NB):
                    for j in range(FF // P):
                        t = pe.matmul(two_banks(k, 2)[:, q, :], hidden[:, j, q * P:(q + 1) * P], w2[:, j, :],
                                      start=(j == 0), stop=(j == FF // P - 1))
                t.then_inc(s["second"], 1)

        @block.scalar
        def _(act):
            act.wait_ge(s["weights"], n_weights)
            with act.Fori(0, NCH) as c:
                act.wait_ge(s["turned1"], c + 1)
                copy_turned(act, k, 0, meanT).then_inc(s["copied1"], 1)
                act.wait_ge(s["turned2"], c + 1)
                copy_turned(act, k, 0, unitT).then_inc(s["copied2"], 1)
                for j in range(FF // P):
                    act.wait_ge(s["hidden"], c * (FF // P) + j + 1)
                    if j == 0:
                        act.wait_ge(s["second"], c)
                    act.activation(hidden[:, j, :], k.psum[:, 4 + j % 4, :], ACT.Gelu,
                                   bias=b1[:, j:j + 1]).then_inc(s["gelu"], 1)
                act.wait_ge(s["ln2_shifted"], c + 1)
                act.dma_start(chunk_rows(dram.state, c), out).then_inc(s["stored"], 16)
            act.wait_ge(s["stored"], 16 * NCH)


def build_linear_attention(nc, k, w, mixed, dram):
    a = Arena(k.arena, k.words)
    assert a.take([2, D]) is not None
    wq, wk, wv, wo = (a.take([2, D]) for _ in range(4))
    wkvT, woT = a.take([2, 2 * D]), a.take([2, D])
    g = [a.take([MD]) for _ in range(4)]
    rows, rowsT = a.take([D]), a.take([2, P])
    kv, square = a.take([2 * MH, MD]), a.take([2 * MH, MD])
    sums, mean, var, rstd = (a.take([2 * MH]) for _ in range(4))
    eps, minus_half, mask = a.take([2 * MH]), a.take([2 * MH]), a.take([BLK])
    total, paired, first = a.take([2, P]), a.take([2, P]), a.take([2, D])
    with stage(nc, "mixkv", "weights turned copied loaded xturned xcopied projected summed mean centred squared "
               "spread var eps rstd unit scaled shifted masked product added consts mask zeroed passed scaledk") as (block, s):
        @block.sync
        def _(sp):
            for to, n in ((wq, "wq"), (wk, "wk"), (wv, "wv"), (wo, "wo")):
                sp.dma_start(to, w[n].rearrange("(f p) n -> p f n", p=P)).then_inc(s["weights"], 16)
            for to, n in zip(g, ("ln_k_g", "ln_k_b", "ln_v_g", "ln_v_b")):
                sp.dma_start(to, w[n].partition_broadcast(P)).then_inc(s["weights"], 16)
            with sp.Fori(0, BLK) as b:
                sp.wait_ge(s["xturned"], b)
                sp.dma_start(rows, dram.xn[ds(b * P, P), :]).then_inc(s["loaded"], 16)

        @block.gpsimd
        def _(pool):
            pool.memset(eps, 1e-5).then_inc(s["consts"], 1)
            pool.memset(minus_half, -0.5).then_inc(s["consts"], 1)
            pool.memset(mask, 1.0).then_inc(s["consts"], 1)
            pool.wait_ge(s["consts"], 3)
            pool.affine_select(out=mask, in_=mask, compare_op=ALU.is_ge, fill=0.0, base=N - 1,
                               pattern=[[-P, BLK]], channel_multiplier=-1).then_inc(s["mask"], 1)
            with pool.Fori(0, BLK) as b:
                pool.wait_ge(s["var"], b + 1)
                pool.tensor_tensor(rstd, var, eps, ALU.add).then_inc(s["eps"], 1)
                pool.wait_ge(s["eps"], b + 1)
                pool.tensor_tensor(rstd, rstd, minus_half, ALU.pow).then_inc(s["rstd"], 1)

        @block.tensor
        def _(pe):
            pe.wait_ge(s["weights"], 16 * 8)
            for n, of in enumerate((wk, wv, wo)):
                for f in range(2):
                    for o in range(2):
                        t = pe.transpose(k.psum[:, n, (f * 2 + o) * P:(f * 2 + o + 1) * P],
                                         of[:, o, f * P:(f + 1) * P], k.ident[:, :])
            t.then_inc(s["turned"], 1)
            pe.wait_ge(s["copied"], 3)
            with pe.Fori(0, BLK) as b:
                pe.wait_ge(s["loaded"], 16 * b + 16)
                for f in range(2):
                    t = pe.transpose(k.psum[:, 3, f * P:(f + 1) * P], rows[:, f * P:(f + 1) * P], k.ident[:, :])
                t.then_inc(s["xturned"], 1)
                pe.wait_ge(s["xcopied"], b + 1)
                for f in range(2):
                    t = pe.matmul(k.psum[:, 4, :], rowsT[:, f, :], wkvT[:, f, :], start=(f == 0), stop=(f == 1))
                t.then_inc(s["projected"], 1)
                pe.wait_ge(s["masked"], b + 1)
                for f in range(2):
                    t = pe.matmul(k.psum[:, 5, f * P:(f + 1) * P],
                                  kv[:, 2 * f:2 * f + 2, :].rearrange("p a b -> p (a b)"),
                                  kv[:, MH + 2 * f:MH + 2 * f + 2, :].rearrange("p a b -> p (a b)"),
                                  start=True, stop=True)
                t.then_inc(s["product"], 1)

        @block.scalar
        def _(act):
            act.wait_ge(s["turned"], 1)
            for n in range(2):
                act.copy(wkvT[:, :, n * D:(n + 1) * D],
                         k.psum[:, n, :].rearrange("p (f n) -> p f n", f=2)).then_inc(s["copied"], 1)
            act.copy(woT, k.psum[:, 2, :].rearrange("p (f n) -> p f n", f=2)).then_inc(s["copied"], 1)
            with act.Fori(0, BLK) as b:
                act.wait_ge(s["xturned"], b + 1)
                act.wait_ge(s["projected"], b)
                act.copy(rowsT.rearrange("p f n -> p (f n)"), k.psum[:, 3, 0:2 * P]).then_inc(s["xcopied"], 1)
                act.wait_ge(s["centred"], b + 1)
                act.wait_ge(s["spread"], b)
                act.activation(square, kv, ACT.Square).then_inc(s["squared"], 1)

        @block.vector
        def _(dve):
            dve.memset(total, 0.0).then_inc(s["zeroed"], 1)
            dve.memset(paired, 0.0).then_inc(s["zeroed"], 1)
            dve.wait_ge(s["zeroed"], 2)
            dve.wait_ge(s["weights"], 16 * 8)
            dve.wait_ge(s["mask"], 1)
            with dve.Fori(0, BLK) as b:
                out = k.psum[:, 4, :].rearrange("p (h d) -> p h d", h=2 * MH)
                dve.wait_ge(s["projected"], b + 1)
                dve.tensor_reduce(sums, out, AX, ALU.add).then_inc(s["summed"], 1)
                dve.wait_ge(s["summed"], b + 1)
                dve.tensor_scalar(mean, sums, 1.0 / MD, None, ALU.mult).then_inc(s["mean"], 1)
                dve.wait_ge(s["mean"], b + 1)
                dve.wait_ge(s["product"], b)
                dve.tensor_tensor(kv, out, along(mean, 2, MD), ALU.subtract).then_inc(s["centred"], 1)
                dve.wait_ge(s["squared"], b + 1)
                dve.tensor_reduce(sums, square, AX, ALU.add).then_inc(s["spread"], 1)
                dve.wait_ge(s["spread"], b + 1)
                dve.tensor_scalar(var, sums, 1.0 / MD, None, ALU.mult).then_inc(s["var"], 1)
                dve.wait_ge(s["rstd"], b + 1)
                dve.tensor_tensor(kv, kv, along(rstd, 2, MD), ALU.mult).then_inc(s["unit"], 1)
                dve.wait_ge(s["unit"], b + 1)
                for n in range(2):
                    ins = dve.tensor_tensor(kv[:, n * MH:(n + 1) * MH], kv[:, n * MH:(n + 1) * MH],
                                            along(g[2 * n], 1, MH), ALU.mult)
                ins.then_inc(s["scaled"], 1)
                dve.wait_ge(s["scaled"], b + 1)
                for n in range(2):
                    ins = dve.tensor_tensor(kv[:, n * MH:(n + 1) * MH], kv[:, n * MH:(n + 1) * MH],
                                            along(g[2 * n + 1], 1, MH), ALU.add)
                ins.then_inc(s["shifted"], 1)
                dve.wait_ge(s["shifted"], b + 1)
                dve.tensor_scalar(kv[:, 0:MH], kv[:, 0:MH], mask[:, ds(b, 1)], None, ALU.mult).then_inc(s["masked"], 1)
                dve.wait_ge(s["product"], b + 1)
                dve.wait_ge(s["added"], b)
                dve.tensor_tensor(total, total, k.psum[:, 5, 0:2 * P].rearrange("p (f n) -> p f n", f=2),
                                  ALU.add).then_inc(s["added"], 1)
            dve.wait_ge(s["added"], BLK)
            for half in range(2):
                part = slice(half * MD, (half + 1) * MD)
                dve.tensor_scalar(paired[part, :, part], total[part, :, part], 1.0 / N, None, ALU.mult)

    with stage(nc, "mixw", "first copied second") as (block, s):
        @block.tensor
        def _(pe):
            for f in range(2):
                t = pe.matmul(k.psum[:, f, 0:D], paired[:, f, :], wq[:, f, :], start=True, stop=True)
            t.then_inc(s["first"], 1)
            pe.wait_ge(s["copied"], 1)
            for o in range(2):
                for f in range(2):
                    t = pe.matmul(k.psum[:, 2 + o, 0:D], first[:, f, o * P:(o + 1) * P], woT[:, f, :],
                                  start=(f == 0), stop=(f == 1))
            t.then_inc(s["second"], 1)

        @block.vector
        def _(dve):
            dve.wait_ge(s["first"], 1)
            dve.tensor_copy(first, k.psum[:, 0:2, 0:D]).then_inc(s["copied"], 1)
            dve.wait_ge(s["second"], 1)
            dve.tensor_copy(mixed, k.psum[:, 2:4, 0:D])


def build_experts(nc, k, w, x, mixed, mix_bo, gnn_g, gnn_b, out_dram, dram):
    a = Arena(k.arena, k.words)
    a.take([2, D])
    EH = NX * 2
    w1, w2, w3 = (a.take([EH, HE]) for _ in range(3))
    wr, br, bo = a.take([2, NX]), a.take([NX]), a.take([HE], parts=NX)
    bnv = [[a.take([EH]) for _ in range(5)] for _ in range(2)]
    scale, shift = [a.take([EH]) for _ in range(2)], [a.take([EH]) for _ in range(2)]
    og, ob, mbo = a.take([D]), a.take([D]), a.take([D])
    xr, x2, st = a.take([NB, D]), a.take([NB, D]), a.take([NB, D])
    xnT, unitT = a.take([2, CH]), a.take([2, CH])
    h1, h2 = a.take([2, CH]), a.take([2, CH])
    stats, moments, rstd = a.take([NB, 6]), a.take([NB, 2]), a.take([NB])
    stats2, moments2, rstd2 = a.take([NB, 6]), a.take([NB, 2]), a.take([NB])
    eps, minus_half, bneps, bnhalf = a.take([NB]), a.take([NB]), a.take([EH]), a.take([EH])
    logits, most, gates, gsum, ginv = a.take([NB, NX]), a.take([NB]), a.take([NB, NX]), a.take([NB]), a.take([NB])
    gatesT = a.take([CH], parts=NX)
    big = k.scores[:, :]
    xn = big[:, 0:NB * D].rearrange("p (q d) -> p q d", q=NB)
    gn = big[:, NB * D:2 * NB * D].rearrange("p (q d) -> p q d", q=NB)
    acc = [big[:, (2 + n) * NB * D:(3 + n) * NB * D].rearrange("p (q d) -> p q d", q=NB) for n in range(2)]
    unit = big[:, 4 * NB * D:5 * NB * D].rearrange("p (q d) -> p q d", q=NB)
    with stage(nc, "bnfold", "loaded consts eps root scale diff prod done") as (block, s):
        @block.sync
        def _(sp):
            with nc.allow_non_contiguous_dma(reason="once"):
                for layer, names in enumerate((("b1", "g1", "be1", "m1", "v1"), ("b2", "g2", "be2", "m2", "v2"))):
                    for to, n in zip(bnv[layer], names):
                        sp.dma_start(to, w[n].rearrange("e (f p) -> p (e f)", p=P)).then_inc(s["loaded"], 16)
            for to, n in ((w1, "W1"), (w2, "W2"), (w3, "Wo")):
                sp.dma_start(to, w[n].rearrange("e (f p) n -> p (e f) n", p=P)).then_inc(s["loaded"], 16)
            sp.dma_start(wr, w["Wr"].rearrange("(f p) e -> p f e", p=P)).then_inc(s["loaded"], 16)
            sp.dma_start(br, w["br"].partition_broadcast(P)).then_inc(s["loaded"], 16)
            sp.dma_start(bo, w["bo"]).then_inc(s["loaded"], 16)
            for to, of in ((og, gnn_g), (ob, gnn_b), (mbo, mix_bo)):
                sp.dma_start(to, of.partition_broadcast(P)).then_inc(s["loaded"], 16)
            sp.wait_ge(s["loaded"], 16 * 19)

        @block.gpsimd
        def _(pool):
            for to, value in ((bneps, 1e-3), (bnhalf, -0.5), (eps, 1e-5), (minus_half, -0.5)):
                pool.memset(to, value).then_inc(s["consts"], 1)
            pool.wait_ge(s["consts"], 4)
            pool.wait_ge(s["loaded"], 16 * 19)
            for n in range(2):
                pool.tensor_tensor(scale[n], bnv[n][4], bneps, ALU.add).then_inc(s["eps"], 1)
                pool.wait_ge(s["eps"], n + 1)
                pool.tensor_tensor(scale[n], scale[n], bnhalf, ALU.pow).then_inc(s["root"], 1)
                pool.wait_ge(s["root"], n + 1)
                pool.tensor_tensor(scale[n], scale[n], bnv[n][1], ALU.mult).then_inc(s["scale"], 1)
                pool.tensor_tensor(shift[n], bnv[n][0], bnv[n][3], ALU.subtract).then_inc(s["diff"], 1)
                pool.wait_ge(s["scale"], n + 1)
                pool.wait_ge(s["diff"], n + 1)
                pool.tensor_tensor(shift[n], shift[n], scale[n], ALU.mult).then_inc(s["prod"], 1)
                pool.wait_ge(s["prod"], n + 1)
                pool.tensor_tensor(shift[n], shift[n], bnv[n][2], ALU.add).then_inc(s["done"], 1)

    with stage(nc, "experts", "x xn state turned copied mixed summed1 summed2 summed3 turned2 copied2 routed lbias most less exp "
               "gsum ginv gates gturned gcopied biased h1 a1 h2 a2 y acc stored passed "
               + norm_sems("ln1") + " " + norm_sems("ln2")) as (block, s):
        @block.sync
        def _(sp):
            with sp.Fori(0, NCH) as c:
                sp.wait_ge(s["turned"], c)
                sp.dma_start(xn, chunk_rows(dram.xn, c)).then_inc(s["xn"], 16)
                sp.wait_ge(s["summed3"], c)
                sp.dma_start(xr, chunk_rows(x, c)).then_inc(s["x"], 16)
                sp.dma_start(st, chunk_rows(dram.state, c)).then_inc(s["state"], 16)

        @block.gpsimd
        def _(pool):
            with pool.Fori(0, NCH) as c:
                inverse_root(pool, s, "ln1", c + 1, moments, rstd, eps, minus_half)
                inverse_root(pool, s, "ln2", c + 1, moments2, rstd2, eps, minus_half)

        @block.tensor
        def _(pe):
            with pe.Fori(0, NCH) as c:
                pe.wait_ge(s["xn"], 16 * c + 16)
                transpose_chunk(pe, k, 0, xn).then_inc(s["turned"], 1)
                pe.wait_ge(s["copied"], c + 1)
                for q in range(NB):
                    for f in range(2):
                        t = pe.matmul(two_banks(k, 2)[:, q, :], xnT[:, f, q * P:(q + 1) * P], mixed[:, f, :],
                                      start=(f == 0), stop=(f == 1))
                t.then_inc(s["mixed"], 1)
                pe.wait_ge(s["ln2_unit"], c + 1)
                transpose_chunk(pe, k, 0, unit).then_inc(s["turned2"], 1)
                pe.wait_ge(s["copied2"], c + 1)
                for q in range(NB):
                    for f in range(2):
                        t = pe.matmul(k.psum[:, 6, q * NX:(q + 1) * NX], unitT[:, f, q * P:(q + 1) * P], wr[:, f, :],
                                      start=(f == 0), stop=(f == 1))
                t.then_inc(s["routed"], 1)
                pe.wait_ge(s["gates"], c + 1)
                for q in range(NB):
                    t = pe.transpose(k.psum[0:NX, 7, q * P:(q + 1) * P], gates[:, q, :], k.ident[:, :])
                t.then_inc(s["gturned"], 1)
                pe.wait_ge(s["gcopied"], c + 1)
                for q in range(NB):
                    t = pe.matmul(two_banks(k, 2)[:, q, :], gatesT[:, q * P:(q + 1) * P], bo[:, :],
                                  start=True, stop=True)
                t.then_inc(s["biased"], 1)
                for e in range(NX):
                    n = c * NX + e
                    for f2 in range(2):
                        for f in range(2):
                            t = pe.matmul(k.psum[:, f2, :], w1[:, 2 * e + f, f2 * P:(f2 + 1) * P], unitT[:, f, :],
                                          start=(f == 0), stop=(f == 1))
                    t.then_inc(s["h1"], 1)
                    pe.wait_ge(s["a1"], n + 1)
                    for f2 in range(2):
                        for f in range(2):
                            t = pe.matmul(k.psum[:, 4 + f2, :], w2[:, 2 * e + f, f2 * P:(f2 + 1) * P], h1[:, f, :],
                                          start=(f == 0), stop=(f == 1))
                    t.then_inc(s["h2"], 1)
                    pe.wait_ge(s["a2"], n + 1)
                    b = 6 if e % 2 else 2
                    pe.wait_ge(s["acc"], c * (NX + 1) + e if e else c * (NX + 1) + 1)
                    for q in range(NB):
                        for f in range(2):
                            t = pe.matmul(two_banks(k, b)[:, q, :], h2[:, f, q * P:(q + 1) * P], w3[:, 2 * e + f, :],
                                          start=(f == 0), stop=(f == 1))
                    t.then_inc(s["y"], 1)

        @block.scalar
        def _(act):
            with act.Fori(0, NCH) as c:
                act.wait_ge(s["turned"], c + 1)
                copy_turned(act, k, 0, xnT).then_inc(s["copied"], 1)
                act.wait_ge(s["turned2"], c + 1)
                copy_turned(act, k, 0, unitT).then_inc(s["copied2"], 1)
                act.wait_ge(s["less"], c + 1)
                act.activation(logits, logits, ACT.Exp).then_inc(s["exp"], 1)
                act.wait_ge(s["gturned"], c + 1)
                act.copy(gatesT, k.psum[0:NX, 7, :]).then_inc(s["gcopied"], 1)
                for e in range(NX):
                    n = c * NX + e
                    for layer, (ready, done, bank, to) in enumerate(((s["h1"], s["a1"], 0, h1), (s["h2"], s["a2"], 4, h2))):
                        act.wait_ge(ready, n + 1)
                        if layer:
                            act.wait_ge(s["y"], n)
                        for f in range(2):
                            ins = act.activation(to[:, f, :], k.psum[:, bank + f, :], ACT.Relu,
                                                 bias=shift[layer][:, 2 * e + f:2 * e + f + 1],
                                                 scale=scale[layer][:, 2 * e + f:2 * e + f + 1])
                        ins.then_inc(done, 1)
                act.wait_ge(s["acc"], (c + 1) * (NX + 1))
                act.dma_start(chunk_rows(out_dram, c), acc[NX % 2]).then_inc(s["stored"], 16)
            act.wait_ge(s["stored"], 16 * NCH)

        @block.vector
        def _(dve):
            with dve.Fori(0, NCH) as c:
                dve.wait_ge(s["state"], 16 * c + 16)
                normalize(dve, s, "ln1", c + 1, st, gn, stats, moments, rstd, og, ob)
                dve.wait_ge(s["ln1_shifted"], c + 1)
                dve.wait_ge(s["mixed"], c + 1)
                dve.wait_ge(s["x"], 16 * c + 16)
                dve.tensor_tensor(x2, two_banks(k, 2), gn, ALU.add).then_inc(s["summed1"], 1)
                dve.wait_ge(s["summed1"], c + 1)
                dve.tensor_tensor(x2, x2, along(mbo, 1, NB), ALU.add).then_inc(s["summed2"], 1)
                dve.wait_ge(s["summed2"], c + 1)
                dve.tensor_tensor(x2, x2, xr, ALU.add).then_inc(s["summed3"], 1)
                dve.wait_ge(s["summed3"], c + 1)
                normalize(dve, s, "ln2", c + 1, x2, unit, stats2, moments2, rstd2)
                dve.wait_ge(s["routed"], c + 1)
                dve.tensor_tensor(logits, k.psum[:, 6, 0:NB * NX].rearrange("p (q e) -> p q e", q=NB),
                                  along(br, 1, NB), ALU.add).then_inc(s["lbias"], 1)
                dve.wait_ge(s["lbias"], c + 1)
                dve.tensor_reduce(most, logits, AX, ALU.max).then_inc(s["most"], 1)
                dve.wait_ge(s["most"], c + 1)
                dve.tensor_tensor(logits, logits, along(most, 2, NX), ALU.subtract).then_inc(s["less"], 1)
                dve.wait_ge(s["exp"], c + 1)
                dve.tensor_reduce(gsum, logits, AX, ALU.add).then_inc(s["gsum"], 1)
                dve.wait_ge(s["gsum"], c + 1)
                dve.reciprocal(ginv, gsum).then_inc(s["ginv"], 1)
                dve.wait_ge(s["ginv"], c + 1)
                dve.tensor_tensor(gates, logits, along(ginv, 2, NX), ALU.mult).then_inc(s["gates"], 1)
                dve.wait_ge(s["gates"], c + 1)
                dve.wait_ge(s["biased"], c + 1)
                dve.wait_ge(s["stored"], 16 * c)
                dve.tensor_tensor(acc[0], two_banks(k, 2), x2, ALU.add).then_inc(s["acc"], 1)
                for e in range(NX):
                    dve.wait_ge(s["y"], c * NX + e + 1)
                    dve.wait_ge(s["acc"], c * (NX + 1) + e + 1)
                    b = 6 if e % 2 else 2
                    for q in range(NB):
                        ins = dve.scalar_tensor_tensor(acc[(e + 1) % 2][:, q, :], two_banks(k, b)[:, q, :],
                                                       gates[:, q, e:e + 1], acc[e % 2][:, q, :], ALU.mult, ALU.add)
                    ins.then_inc(s["acc"], 1)


def build(nc, t):
    with ExitStack() as ctx:
        k, dram = setup(nc, ctx)
        part = lambda prefix: {n[len(prefix):]: ap for n, ap in t.items() if n.startswith(prefix)}
        gnn, mix, ffn = part("L0_gnn_"), part("L0_mix_"), part("L0_ffn_")
        build_constants(nc, k)
        build_visits(nc, k, t["src"], t["dst"], t["edge_type_3"], t["node_type_4"], dram)
        build_input_norm(nc, k, t["x"], dram)
        weights = Arena(k.arena, k.words).take([H, 5 * HD])
        with nc.Fori(0, L) as layer:
            build_type_weights(nc, k, gnn, layer, weights)
            build_rows(nc, k, weights, dram)
            build_scores(nc, k, dram)
            build_softmax(nc, k, dram)
            build_sums(nc, k, dram)
            build_layer_tail(nc, k, gnn, layer, dram)
        mixed = Arena(k.arena, k.words).take([2, D])
        build_linear_attention(nc, k, mix, mixed, dram)
        build_experts(nc, k, ffn, t["x"], mixed, mix["bo"], gnn["out_g"], gnn["out_b"], t["out"], dram)


_NAMES = ["x", "src", "dst", "edge_type_3", "node_type_4"] + \
    [f"L0_gnn_{n}" for n in ("W_Q", "W_K", "W_V", "W_E", "mu", "Wo", "bo", "ln1_g", "ln1_b", "ln2_g", "ln2_b",
                             "w1", "b1", "w2", "b2", "out_g", "out_b")] + \
    [f"L0_mix_{n}" for n in ("wq", "wk", "wv", "wo", "bo", "ln_k_g", "ln_k_b", "ln_v_g", "ln_v_b")] + \
    [f"L0_ffn_{n}" for n in ("Wr", "br", "W1", "b1", "g1", "be1", "m1", "v1", "W2", "b2", "g2", "be2", "m2",
                             "v2", "Wo", "bo")]
_PADDED = {"x": (NP, 0), "node_type_4": (NP, 0), "src": (EP, 0), "edge_type_3": (EP, 0), "dst": (EP, BLK * P - 1)}


def kernel(**inputs):
    import concourse.bacc as bacc
    from concourse.bass_utils import run_bass_kernel_spmd

    nc = bacc.Bacc("TRN2", target_bir_lowering=False, num_devices=1)
    arrays, tensors = {}, {}
    for name in _NAMES:
        a = np.ascontiguousarray(inputs[name])
        if name in _PADDED:
            rows, fill = _PADDED[name]
            a = np.concatenate([a, np.full((rows - a.shape[0],) + a.shape[1:], fill, a.dtype)])
        arrays[f"in_{name}"] = a
        tensors[name] = nc.dram_tensor(f"in_{name}", a.shape, mybir.dt.from_np(a.dtype), kind="ExternalInput").ap()
    tensors["out"] = nc.dram_tensor("out", (NP, D), F32, kind="ExternalOutput").ap()
    build(nc, tensors)
    result = run_bass_kernel_spmd(nc, [arrays], core_ids=[0])
    return result.results[0]["out"][:N]
```

```python
from contextlib import ExitStack, contextmanager

import numpy as np

import concourse.bass as bass
from concourse import mybir

ALU = mybir.AluOpType
ACT = mybir.ActivationFunctionType
F32 = mybir.dt.float32
BF16 = mybir.dt.bfloat16
I32 = mybir.dt.int32
AX = mybir.AxisListType.X

P = 128
N, E, D = 6250, 100000, 256
L, H, HD, TN, TE = 3, 8, 32, 4, 3
FF = 4 * D
NX, HE = 8, 256
MH, MD = 4, 64
CH = 512
NCH = -(-N // CH)
NB = CH // P
NP = NCH * CH
BLK = -(-N // P)
TILES = 784
EP = TILES * P
V = TILES + BLK - 1
VP = 104
VJ = V // VP
SC = 16
VK = V // SC
CL = VK * P
RW = H * (HD + 1)
GV = 16
GH = GV // 4
NG = V // GV
BIG = 1.0e30
assert VJ * VP == V and SC * VK == V and NG * GV == V and TILES % 112 == 0 and EP >= E
TJ = TILES // 112


def ds(start, size):
    return bass.ds(start, size)


@contextmanager
def stage(nc, name, names, pool_dmas=False):
    with ExitStack() as ctx:
        s = {n: ctx.enter_context(nc.semaphore(f"{name}_{n}")) for n in names.split()}
        with nc.Block() as block:
            yield block, s
        with nc.Block() as clear:
            if pool_dmas:
                @clear.gpsimd
                def _(pool):
                    pool.dma_reset()
                    for x in s.values():
                        pool.sem_clear(x)
            else:
                @clear.sync
                def _(sp):
                    for x in s.values():
                        sp.sem_clear(x)


class Arena:

    def __init__(self, tensor, words):
        self.tensor, self.words, self.at = tensor, words, 0

    def take(self, shape, dtype=F32, parts=P):
        size = int(np.prod(shape))
        words = size if dtype != BF16 else -(-size // 2)
        words = -(-words // 8) * 8
        ap = self.tensor[0:parts, self.at:self.at + words]
        self.at += words
        assert self.at <= self.words, (self.at, self.words)
        if dtype != F32:
            ap = ap.bitcast(dtype)
        ap = ap[:, 0:size]
        if len(shape) == 2:
            ap = ap.rearrange("p (a b) -> p a b", a=shape[0])
        elif len(shape) == 3:
            ap = ap.rearrange("p (a b c) -> p a b c", a=shape[0], b=shape[1])
        return ap


def spread(dram, offset, *dims):
    return bass.AP(tensor=dram.tensor, offset=offset, ap=[list(d) for d in dims])


def along(ap, axis, count):
    ap = ap.unsqueeze(axis)
    shape = list(ap.shape)
    shape[axis] = count
    return ap.broadcast_to(shape)


def build_constants(nc, k):
    with stage(nc, "const", "filled made") as (block, s):
        @block.gpsimd
        def _(pool):
            pool.memset(k.ident[:, :], 0.0).then_inc(s["filled"], 1)
            pool.wait_ge(s["filled"], 1)
            pool.affine_select(out=k.ident[:, :], in_=k.ident[:, :], compare_op=ALU.not_equal, fill=1.0, base=0,
                               pattern=[[-1, P]], channel_multiplier=1)
            pool.iota(k.iota_row[:, :], pattern=[[1, P]], base=0, channel_multiplier=0,
                      allow_small_or_imprecise_dtypes=True)
            pool.iota(k.iota_col[:, :], pattern=[[0, 1]], base=0, channel_multiplier=1,
                      allow_small_or_imprecise_dtypes=True).then_inc(s["made"], 1)


def build_visits(nc, k, src, dst, edge_type, node_type, dram):
    a = Arena(k.arena, k.words)
    T = 112
    src_t, dst_t, et_t = (a.take([TJ * P], I32) for _ in range(3))
    comb = a.take([TJ, 3, P])
    last_i, blk_i = a.take([TJ], I32), a.take([TJ], I32)
    blk_f, tile_no, reach = a.take([TJ]), a.take([TJ]), a.take([TJ])
    reach_all, below = a.take([TILES]), a.take([TILES])
    visit_no, tile_of, block_of, block_off = (a.take([VJ]) for _ in range(4))
    tile_idx, block_i = a.take([VJ], I32), a.take([VJ], I32)
    got = a.take([VJ, 3 * P])
    keyrel, key, over = a.take([VJ, P]), a.take([VJ, P]), a.take([VJ, P])
    keyrel_b = a.take([VJ, P], BF16)
    types_i, types = a.take([NCH * NB], I32), a.take([NCH * NB])
    with stage(nc, "tiles", "edges comb_last made comb_made reach stored_comb stored_reach types shifted typed typ1") as (block, s):
        @block.sync
        def _(sp):
            for to, of in ((src_t, src), (dst_t, dst), (et_t, edge_type)):
                sp.dma_start(to[0:T, :], of.rearrange("(p f) -> p f", p=T)).then_inc(s["edges"], 16)
            with nc.allow_non_contiguous_dma(reason="once, a word per node"):
                sp.dma_start(types_i, node_type.rearrange("(b p) -> p b", p=P)).then_inc(s["types"], 16)
            sp.wait_ge(s["comb_made"], 1)
            sp.dma_start(dram.comb.rearrange("(p j) f -> p (j f)", p=T),
                         comb[0:T].rearrange("p a b c -> p (a b c)")).then_inc(s["stored_comb"], 16)
            sp.wait_ge(s["reach"], 1)
            sp.dma_start(dram.reach.rearrange("(p j) -> p j", p=T), reach[0:T]).then_inc(s["stored_reach"], 16)
            sp.wait_ge(s["stored_comb"], 16)
            sp.wait_ge(s["stored_reach"], 16)

        @block.gpsimd
        def _(pool):
            pool.iota(tile_no[0:T], pattern=[[1, TJ]], base=0, channel_multiplier=TJ,
                      allow_small_or_imprecise_dtypes=True).then_inc(s["made"], 1)
            pool.iota(visit_no[0:VP], pattern=[[VP, VJ]], base=0, channel_multiplier=1,
                      allow_small_or_imprecise_dtypes=True).then_inc(s["made"], 1)

        @block.vector
        def _(dve):
            dve.wait_ge(s["edges"], 48)
            three = [x[0:T].rearrange("p (j f) -> p j f", j=TJ) for x in (src_t, dst_t, et_t)]
            dve.scalar_tensor_tensor(comb[0:T, :, 0, :], three[0], float(TE), three[2], ALU.mult, ALU.add)
            dve.tensor_copy(comb[0:T, :, 1, :], three[0])
            dve.tensor_copy(comb[0:T, :, 2, :], three[1]).then_inc(s["comb_made"], 1)
            dve.tensor_copy(last_i[0:T], three[1][:, :, P - 1]).then_inc(s["comb_last"], 1)
            dve.wait_ge(s["comb_last"], 1)
            dve.tensor_scalar(blk_i[0:T], last_i[0:T], 7, None, ALU.arith_shift_right).then_inc(s["shifted"], 1)
            dve.wait_ge(s["shifted"], 1)
            dve.tensor_copy(blk_f[0:T], blk_i[0:T]).then_inc(s["shifted"], 1)
            dve.wait_ge(s["shifted"], 2)
            dve.wait_ge(s["made"], 2)
            dve.tensor_tensor(reach[0:T], blk_f[0:T], tile_no[0:T], ALU.add).then_inc(s["reach"], 1)
            dve.wait_ge(s["types"], 16)
            dve.tensor_copy(types, types_i).then_inc(s["typed"], 1)
            dve.wait_ge(s["typed"], 1)
            for t in range(TN):
                dve.tensor_scalar(k.onehot[:, :, t], types, float(t), None, ALU.is_equal)

    with stage(nc, "visits", "reach below count index got rel m1 m2 stored tile off turned copied keyb blocki last", True) as (block, s):
        @block.sync
        def _(sp):
            sp.dma_start(reach_all[0:VP], dram.reach.partition_broadcast(VP)).then_inc(s["reach"], 16)
            sp.wait_ge(s["last"], 1)
            sp.dma_start(dram.keyrow.rearrange("(j p) s -> p j s", p=VP), keyrel_b[0:VP]).then_inc(s["stored"], 16)
            sp.dma_start(dram.key.rearrange("(j p s) -> p j s", p=VP, j=VJ), key[0:VP]).then_inc(s["stored"], 16)
            with nc.allow_non_contiguous_dma(reason="once, a word per visit"):
                sp.dma_start(dram.blocks_i.rearrange("(j p) -> p j", p=VP), block_i[0:VP]).then_inc(s["stored"], 16)
                sp.dma_start(dram.blocks_f.rearrange("(j p) -> p j", p=VP), block_of[0:VP]).then_inc(s["stored"], 16)
            sp.wait_ge(s["stored"], 64)

        @block.vector
        def _(dve):
            dve.wait_ge(s["reach"], 16)
            for j in range(VJ):
                if j:
                    dve.wait_ge(s["count"], j)
                dve.tensor_scalar(below[0:VP], reach_all[0:VP], visit_no[0:VP, j:j + 1], None,
                                  ALU.is_lt).then_inc(s["below"], 1)
                dve.wait_ge(s["below"], j + 1)
                dve.tensor_reduce(tile_of[0:VP, j:j + 1], below[0:VP], AX, ALU.add).then_inc(s["count"], 1)
            dve.wait_ge(s["count"], VJ)
            dve.tensor_copy(tile_idx[0:VP], tile_of[0:VP]).then_inc(s["index"], 1)
            dve.tensor_tensor(block_of[0:VP], visit_no[0:VP], tile_of[0:VP], ALU.subtract).then_inc(s["tile"], 1)
            dve.wait_ge(s["tile"], 1)
            dve.tensor_copy(block_i[0:VP], block_of[0:VP])
            dve.tensor_scalar(block_off[0:VP], block_of[0:VP], -float(P), None, ALU.mult).then_inc(s["off"], 1)
            dve.wait_ge(s["off"], 1)
            dve.wait_ge(s["got"], 16 * VJ)
            dst_v = got[0:VP, :, 2 * P:3 * P]
            dve.tensor_tensor(keyrel[0:VP], dst_v, along(block_off[0:VP], 2, P), ALU.add).then_inc(s["rel"], 1)
            dve.wait_ge(s["rel"], 1)
            dve.tensor_copy(keyrel_b[0:VP], keyrel[0:VP])
            dve.tensor_scalar(over[0:VP], keyrel[0:VP], 0.0, 8192.0, ALU.is_lt, ALU.mult).then_inc(s["m1"], 1)
            dve.wait_ge(s["m1"], 1)
            dve.tensor_tensor(key[0:VP], dst_v, over[0:VP], ALU.add).then_inc(s["m2"], 1)
            dve.wait_ge(s["m2"], 1)
            dve.tensor_scalar(over[0:VP], keyrel[0:VP], P - 0.5, 8192.0, ALU.is_gt, ALU.mult).then_inc(s["m1"], 1)
            dve.wait_ge(s["m1"], 2)
            dve.tensor_tensor(key[0:VP], key[0:VP], over[0:VP], ALU.add).then_inc(s["last"], 1)
            for n, to in enumerate((k.idx_key, k.idx_value, k.keycol)):
                for half in range(2):
                    dve.wait_ge(s["turned"], 2 * n + half + 1)
                    dve.tensor_copy(to[:, half * 4 * VP:(half + 1) * 4 * VP],
                                    k.psum[:, 2 * n + half, 0:4 * VP]).then_inc(s["copied"], 1)

        @block.gpsimd
        def _(pool):
            pool.wait_ge(s["index"], 1)
            for j in range(VJ):
                pool.indirect_dma_start(out=got[0:VP, j, :], out_offset=None, in_=dram.comb,
                                        in_offset=bass.IndirectOffsetOnAxis(ap=tile_idx[0:VP, j:j + 1], axis=0)
                                        ).then_inc(s["got"], 16)

        @block.tensor
        def _(pe):
            pe.wait_ge(s["got"], 16 * VJ)
            pe.wait_ge(s["rel"], 1)
            for n in range(3):
                for half in range(2):
                    for q in range(4):
                        j = half * 4 + q
                        of = got[0:VP, j, n * P:(n + 1) * P] if n < 2 else keyrel[0:VP, j, :]
                        t = pe.transpose(k.psum[:, 2 * n + half, q * VP:(q + 1) * VP], of, k.ident[0:VP, 0:VP])
                    t.then_inc(s["turned"], 1)

    a = Arena(k.arena, k.words)
    blocks_all = a.take([V])
    key_run = a.take([CL + 2])
    differ = a.take([CL + 1], BF16)
    edge_f, edge_b = a.take([1]), a.take([1])
    upto, count, count_all, slot_no = a.take([V]), a.take([1]), a.take([NCH * NB]), a.take([NCH * NB])
    with stage(nc, "runs", "blocks keys filled differ pen edges stored upto count counts row made loaded") as (block, s):
        @block.sync
        def _(sp):
            sp.dma_start(blocks_all, dram.blocks_f.partition_broadcast(P)).then_inc(s["blocks"], 16)
            sp.dma_start(k.block_row[0:1, :], dram.blocks_i.unsqueeze(0)).then_inc(s["loaded"], 16)
            sp.wait_ge(s["filled"], 1)
            sp.dma_start(key_run[:, 1:CL + 1], spread(dram.key, 0, [CL, SC], [0, H], [1, CL])).then_inc(s["keys"], 16)
            with nc.allow_non_contiguous_dma(reason="once, a word per partition"):
                sp.dma_start(key_run[H:P, 0:1], spread(dram.key, CL - 1, [CL, SC - 1], [0, H], [1, 1])).then_inc(s["keys"], 16)
                sp.dma_start(key_run[0:P - H, CL + 1:CL + 2],
                             spread(dram.key, CL, [CL, SC - 1], [0, H], [1, 1])).then_inc(s["keys"], 16)
                sp.wait_ge(s["edges"], 2)
                sp.dma_start(dram.edge_f, edge_f[:, 0]).then_inc(s["stored"], 16)
                sp.dma_start(dram.edge_b, edge_b[:, 0]).then_inc(s["stored"], 16)
                sp.wait_ge(s["count"], 1)
                sp.dma_start(dram.counts, count[0:NCH * NB, 0]).then_inc(s["stored"], 16)
                sp.wait_ge(s["stored"], 48)
                sp.dma_start(k.edge_f8[0:H, :], dram.edge_f.rearrange("(c h) -> h c", h=H)).then_inc(s["loaded"], 16)
                sp.dma_start(k.edge_b8[0:H, :], dram.edge_b.rearrange("(c h) -> h c", h=H)).then_inc(s["loaded"], 16)
                sp.dma_start(count_all, dram.counts.partition_broadcast(P)).then_inc(s["counts"], 16)
            sp.wait_ge(s["loaded"], 48)

        @block.gpsimd
        def _(pool):
            pool.iota(slot_no, pattern=[[0, NCH * NB]], base=-P, channel_multiplier=1,
                      allow_small_or_imprecise_dtypes=True).then_inc(s["made"], 1)

        @block.vector
        def _(dve):
            dve.memset(key_run[:, 0:CL + 2:CL + 1], -1.0).then_inc(s["filled"], 1)
            dve.wait_ge(s["blocks"], 16)
            dve.memset(k.same_block[:, 0:1], 0.0)
            dve.tensor_tensor(k.same_block[:, 1:V], blocks_all[:, 1:V], blocks_all[:, 0:V - 1], ALU.is_equal)
            dve.wait_ge(s["keys"], 48)
            dve.wait_ge(s["filled"], 1)
            dve.tensor_tensor(differ, key_run[:, 0:CL + 1], key_run[:, 1:CL + 2], ALU.not_equal).then_inc(s["differ"], 1)
            dve.wait_ge(s["differ"], 1)
            dve.tensor_scalar(k.breaks[:, 0:CL + 1], differ, -BIG, None, ALU.mult).then_inc(s["pen"], 1)
            dve.wait_ge(s["pen"], 1)
            dve.tensor_reduce(edge_f, k.breaks[:, 0:CL], AX, ALU.min).then_inc(s["edges"], 1)
            dve.tensor_reduce(edge_b, k.breaks[:, 1:CL + 1], AX, ALU.min).then_inc(s["edges"], 1)
            B52 = NCH * NB
            dve.tensor_scalar(upto[0:B52], blocks_all[0:B52], k.iota_col[0:B52], None, ALU.is_le).then_inc(s["upto"], 1)
            dve.wait_ge(s["upto"], 1)
            dve.tensor_reduce(count[0:B52], upto[0:B52], AX, ALU.add).then_inc(s["count"], 1)
            dve.wait_ge(s["counts"], 16)
            dve.wait_ge(s["made"], 1)
            dve.scalar_tensor_tensor(k.idx_sums[:, :], count_all, float(P), slot_no, ALU.mult, ALU.add).then_inc(s["row"], 1)


def passed(eng, s, sem, value):
    eng.wait_ge(sem, value)
    eng.sem_inc(s["passed"], 1)


def norm_moments(dve, s, tag, n, x, stats, moments):
    for q in range(NB):
        ins = dve.bn_stats(stats[:, q, :], x[:, q, :])
    ins.then_inc(s[f"{tag}_stats"], 1)
    passed(dve, s, s[f"{tag}_stats"], n)
    for q in range(NB):
        ins = dve.bn_aggr(moments[:, q, :], stats[:, q, :])
    ins.then_inc(s[f"{tag}_moments"], 1)


def norm_rows(dve, s, tag, n, x, out, moments, rstd, scale=None, shift=None):
    dve.wait_ge(s[f"{tag}_rstd"], n)
    for q in range(NB):
        ins = dve.tensor_scalar(out[:, q, :], x[:, q, :], moments[:, q, 0:1], rstd[:, q:q + 1],
                                ALU.subtract, ALU.mult)
    ins.then_inc(s[f"{tag}_unit"], 1)
    if scale is not None:
        dve.wait_ge(s[f"{tag}_unit"], n)
        dve.tensor_tensor(out, out, along(scale, 1, NB), ALU.mult).then_inc(s[f"{tag}_scaled"], 1)
        dve.wait_ge(s[f"{tag}_scaled"], n)
        dve.tensor_tensor(out, out, along(shift, 1, NB), ALU.add).then_inc(s[f"{tag}_shifted"], 1)


def normalize(dve, s, tag, n, x, out, stats, moments, rstd, scale=None, shift=None):
    norm_moments(dve, s, tag, n, x, stats, moments)
    norm_rows(dve, s, tag, n, x, out, moments, rstd, scale, shift)


def inverse_root(pool, s, tag, n, moments, rstd, eps, minus_half):
    step = lambda name: s[f"{tag}_{name}"]
    pool.wait_ge(step("moments"), n)
    pool.tensor_tensor(rstd, moments[:, :, 1], eps, ALU.add).then_inc(step("eps"), 1)
    pool.wait_ge(step("eps"), n)
    pool.tensor_tensor(rstd, rstd, minus_half, ALU.pow).then_inc(step("rstd"), 1)


def norm_sems(tag):
    return " ".join(f"{tag}_{n}" for n in ("stats", "moments", "eps", "rstd", "unit", "scaled", "shifted"))


def chunk_rows(dram, c):
    return dram[ds(c * CH, CH), :].rearrange("(q p) d -> p q d", p=P)


def build_input_norm(nc, k, x, dram):
    a = Arena(k.arena, k.words)
    rows, unit = a.take([NB, D]), a.take([NB, D])
    stats, moments, rstd = a.take([NB, 6]), a.take([NB, 2]), a.take([NB])
    eps, minus_half = a.take([NB]), a.take([NB])
    with stage(nc, "innorm", "loaded stored consts passed " + norm_sems("ln")) as (block, s):
        @block.sync
        def _(sp):
            with sp.Fori(0, NCH) as c:
                sp.wait_ge(s["ln_unit"], c)
                sp.dma_start(rows, chunk_rows(x, c)).then_inc(s["loaded"], 16)

        @block.gpsimd
        def _(pool):
            pool.memset(eps, 1e-5)
            pool.memset(minus_half, -0.5).then_inc(s["consts"], 1)
            pool.wait_ge(s["consts"], 1)
            with pool.Fori(0, NCH) as c:
                inverse_root(pool, s, "ln", c + 1, moments, rstd, eps, minus_half)

        @block.vector
        def _(dve):
            with dve.Fori(0, NCH) as c:
                dve.wait_ge(s["loaded"], 16 * (c + 1))
                dve.wait_ge(s["stored"], 32 * c)
                normalize(dve, s, "ln", c + 1, rows, unit, stats, moments, rstd)

        @block.scalar
        def _(act):
            with act.Fori(0, NCH) as c:
                act.wait_ge(s["ln_unit"], c + 1)
                act.dma_start(chunk_rows(dram.xn, c), unit).then_inc(s["stored"], 16)
                act.dma_start(chunk_rows(dram.state, c), unit).then_inc(s["stored"], 16)
            act.wait_ge(s["stored"], 32 * NCH)


def build_type_weights(nc, k, w, layer, weights):
    a = Arena(k.arena, k.words)
    a.take([H, 5 * HD])
    wk = a.take([H, HD])
    we = a.take([H, TE, HD], parts=HD)
    wkT = a.take([H, P], parts=HD)
    mu = a.take([H * TE])
    with stage(nc, "typew", "loaded turned copied merged") as (block, s):
        @block.sync
        def _(sp):
            for t in range(TN):
                part = slice(t * HD, (t + 1) * HD)
                for of, to in ((w["W_Q"], weights[part, :, 0:HD]), (w["W_V"], weights[part, :, HD:2 * HD]),
                               (w["W_K"], wk[part])):
                    sp.dma_start(to, of[ds(layer, 1), t].rearrange("a h d e -> (a d) h e")).then_inc(s["loaded"], 16)

        @block.scalar
        def _(act):
            for e in range(TE):
                act.dma_start(we[:, :, e, :],
                              w["W_E"][ds(layer, 1), e].rearrange("a h d e -> (a d) h e")).then_inc(s["loaded"], 16)
            act.dma_start(mu, w["mu"][ds(layer, 1)].rearrange("a h t -> (a h t)").partition_broadcast(P)
                          ).then_inc(s["loaded"], 16)

        @block.tensor
        def _(pe):
            pe.wait_ge(s["loaded"], 16 * (3 * TN + TE + 1))
            for h in range(H):
                t = pe.transpose(k.psum[0:HD, h // 4, (h % 4) * P:(h % 4 + 1) * P], wk[:, h, :], k.ident[:, :])
            t.then_inc(s["turned"], 1)
            pe.wait_ge(s["copied"], 1)
            for h in range(H):
                t = pe.matmul(k.psum[:, 2 + h // 4, (h % 4) * P:(h % 4) * P + TE * HD], wkT[:, h, :],
                              we[:, h, :, :].rearrange("p a b -> p (a b)"), start=True, stop=True)
            t.then_inc(s["merged"], 1)

        @block.vector
        def _(dve):
            dve.wait_ge(s["turned"], 1)
            dve.tensor_copy(wkT, k.psum[0:HD, 0:2, :].rearrange("p b (h n) -> p (b h) n", n=P)).then_inc(s["copied"], 1)
            dve.wait_ge(s["merged"], 1)
            dve.wait_ge(s["loaded"], 16 * (3 * TN + TE + 1))
            for h in range(H):
                dve.scalar_tensor_tensor(
                    weights[:, h, 2 * HD:5 * HD].rearrange("p (t f) -> p t f", t=TE),
                    k.psum[:, 2 + h // 4, (h % 4) * P:(h % 4) * P + TE * HD].rearrange("p (t f) -> p t f", t=TE),
                    float(HD) ** -0.5, along(mu[:, h * TE:(h + 1) * TE], 2, HD), ALU.mult, ALU.mult)


def build_rows(nc, k, weights, dram):
    a = Arena(k.arena, k.words)
    a.take([H, 5 * HD])
    x = [a.take([D]) for _ in range(2)]
    placed = [a.take([H, TN * HD]) for _ in range(2)]
    placedT = [a.take([H, P]) for _ in range(2)]
    q_row = [a.take([D]) for _ in range(2)]
    v_row = [a.take([H, HD + 1]) for _ in range(2)]
    k_row = [a.take([TE * D]) for _ in range(2)]
    names = "x0 x1 placed turned copied multiplied evac_lo evac_hi stored_qv0 stored_qv1 stored_k0 stored_k1 ones"
    blocks = NP // P
    with stage(nc, "rows", names) as (block, s):
        s_x, s_qv, s_k = [s["x0"], s["x1"]], [s["stored_qv0"], s["stored_qv1"]], [s["stored_k0"], s["stored_k1"]]

        def steps(eng, step):
            with eng.Fori(0, blocks // 2 - 1) as i:
                for b in range(2):
                    step(2 * i + b, b, i, True, True)
            step(blocks - 2, 0, blocks // 2 - 1, True, False)
            step(blocks - 1, 1, blocks // 2 - 1, False, False)

        def move(copy, b, half):
            out = k.psum[:, 2 + 3 * b + half, :].rearrange("p (g h d) -> p g h d", g=4, h=4)
            copy(q_row[b][:, half * P:(half + 1) * P], out[:, 0].rearrange("p h d -> p (h d)"))
            copy(v_row[b][:, half * 4:(half + 1) * 4, 0:HD], out[:, 1])
            return copy(k_row[b].rearrange("p (e c) -> p e c", e=TE)[:, 0:2, half * P:(half + 1) * P],
                        out[:, 2:4].rearrange("p e h d -> p e (h d)"))

        @block.sync
        def _(sp):
            def load(n, b):
                sp.dma_start(x[b], dram.state[ds(n * P, P), :]).then_inc(s_x[b], 16)

            def step(n, b, i, one, two):
                if two:
                    sp.wait_ge(s["placed"], n + 1)
                    load(n + 2, b)
                sp.wait_ge(s["evac_lo"], n + 3)
                sp.wait_ge(s["evac_hi"], n + 3)
                sp.dma_start(dram.q[ds(n * P, P), :], q_row[b]).then_inc(s_qv[b], 16)
                sp.dma_start(dram.value_rows[ds(n * P, P), :],
                             v_row[b].rearrange("p h d -> p (h d)")).then_inc(s_qv[b], 16)

            sp.sem_inc(s["evac_lo"], 2)
            sp.sem_inc(s["evac_hi"], 2)
            load(0, 0)
            load(1, 1)
            sp.wait_ge(s["ones"], 2)
            steps(sp, step)
            for b in range(2):
                sp.wait_ge(s_qv[b], 32 * (blocks // 2))

        @block.vector
        def _(dve):
            def place(n, b, i):
                dve.wait_ge(s_x[b], 16 * i + 16)
                dve.tensor_tensor(
                    placed[b].rearrange("p h (t d) -> p h t d", t=TN),
                    along(x[b].rearrange("p (h d) -> p h d", h=H), 2, TN),
                    along(along(k.onehot[:, ds(n, 1), :].rearrange("p a t -> p (a t)"), 1, H), 3, HD),
                    ALU.mult).then_inc(s["placed"], 1)

            def step(n, b, i, one, two):
                if two:
                    dve.wait_ge(s["turned"], n + 1)
                    place(n + 2, b, i + 1)
                dve.wait_ge(s["multiplied"], n + 1)
                dve.wait_ge(s_qv[b], 32 * i)
                dve.wait_ge(s_k[b], 16 * i)
                move(dve.tensor_copy, b, 1).then_inc(s["evac_hi"], 1)

            for b in range(2):
                dve.memset(v_row[b][:, :, HD:HD + 1], 1.0).then_inc(s["ones"], 1)
            place(0, 0, 0)
            place(1, 1, 0)
            steps(dve, step)

        @block.scalar
        def _(act):
            def copy(n, b):
                act.wait_ge(s["turned"], n + 1)
                act.copy(placedT[b].rearrange("p h n -> p (h n)"),
                         k.psum[:, 0:2, :].rearrange("p a b -> p (a b)")).then_inc(s["copied"], 1)

            def step(n, b, i, one, two):
                if one:
                    act.wait_ge(s["multiplied"], n)
                    copy(n + 1, 1 - b)
                act.wait_ge(s["multiplied"], n + 1)
                act.wait_ge(s_k[b], 16 * i)
                act.wait_ge(s_qv[b], 32 * i)
                move(act.copy, b, 0)
                act.copy(k_row[b][:, 2 * D:], k.psum[:, 4 + 3 * b, 0:D]).then_inc(s["evac_lo"], 1)
                act.wait_ge(s["evac_lo"], n + 3)
                act.wait_ge(s["evac_hi"], n + 3)
                act.dma_start(dram.key_rows[ds(n * P * TE, P * TE), :].rearrange("(p e) d -> p (e d)", e=TE),
                              k_row[b]).then_inc(s_k[b], 16)

            copy(0, 0)
            steps(act, step)
            for b in range(2):
                act.wait_ge(s_k[b], 16 * (blocks // 2))

        @block.tensor
        def _(pe):
            def turn(n, b):
                pe.wait_ge(s["placed"], n + 1)
                for h in range(H):
                    t = pe.transpose(k.psum[:, h // 4, (h % 4) * P:(h % 4 + 1) * P], placed[b][:, h, :],
                                     k.ident[:, :])
                t.then_inc(s["turned"], 1)

            def step(n, b, i, one, two):
                pe.wait_ge(s["copied"], n + 1)
                if one:
                    turn(n + 1, 1 - b)
                pe.wait_ge(s["evac_lo"], n + 1)
                pe.wait_ge(s["evac_hi"], n + 1)
                for h in range(H):
                    out = k.psum[:, 2 + 3 * b + h // 4, :].rearrange("p (g h d) -> p g h d", g=4, h=4)
                    pe.matmul(out[:, :, h % 4, :], placedT[b][:, h, :], weights[:, h, 0:4 * HD],
                              start=True, stop=True)
                    t = pe.matmul(k.psum[:, 4 + 3 * b, h * HD:(h + 1) * HD], placedT[b][:, h, :],
                                  weights[:, h, 4 * HD:5 * HD], start=True, stop=True)
                t.then_inc(s["multiplied"], 1)

            turn(0, 0)
            steps(pe, step)


def gather_idx(pool, s, slot, idx, n):
    pool.tensor_copy(slot, idx[:, ds(n * 4, 4)]).then_inc(s["indexed"], 1)
    passed(pool, s, s["indexed"], n + 1)


def build_scores(nc, k, dram):
    a = Arena(k.arena, k.words)
    key_ring = a.take([GV, D])
    query_ring = a.take([GV, D])
    cols = [a.take([4 * P], BF16) for _ in range(2)]
    pick = [a.take([4, P]) for _ in range(2)]
    prod = [a.take([4 * H, HD]) for _ in range(2)]
    index = [a.take([4], I32) for _ in range(GH)]
    names = "picked spread multiplied scored indexed passed cols0 cols1 " + \
        " ".join(f"key{q} query{q}" for q in range(GV))
    with stage(nc, "scores", names, True) as (block, s):
        s_key = [s[f"key{q}"] for q in range(GV)]
        s_query = [s[f"query{q}"] for q in range(GV)]
        s_cols = [s["cols0"], s["cols1"]]

        @block.sync
        def _(sp):
            sp.sem_inc(s["picked"], 2)
            for sem in (s["spread"], s["multiplied"], s["scored"]):
                sp.sem_inc(sem, GH)
            with sp.Fori(0, NG) as i:
                for h in range(GH):
                    n = i * GH + h
                    _, rows = nc.values_load_multi_w_load_instructions(
                        k.block_row[0:1, ds(n * 4, 4)], engines=(mybir.EngineType.SP,),
                        min_val=0, max_val=BLK - 1)
                    sp.wait_ge(s["spread"], n + 1)
                    for q in range(4):
                        sp.dma_start(query_ring[:, 4 * h + q, :],
                                     dram.q[ds(rows[q] * P, P), :]).then_inc(s_query[4 * h + q], 16)

        @block.scalar
        def _(act):
            with act.Fori(0, NG) as i:
                for h in range(GH):
                    n = i * GH + h
                    act.wait_ge(s["picked"], n + 1)
                    act.dma_start(cols[h % 2], dram.keyrow[ds(n * 4, 4), :].rearrange("v s -> (v s)")
                                  .partition_broadcast(P)).then_inc(s_cols[h % 2], 16)

        @block.gpsimd
        def _(pool):
            with pool.Fori(0, NG) as i:
                for h in range(GH):
                    n = i * GH + h
                    passed(pool, s, s["multiplied"], n + 1)
                    gather_idx(pool, s, index[h], k.idx_key, n)
                    for q in range(4):
                        pool.indirect_dma_start(
                            out=key_ring[:, 4 * h + q, :], out_offset=None, in_=dram.key_rows,
                            in_offset=bass.IndirectOffsetOnAxis(ap=index[h][:, q:q + 1], axis=0)
                        ).then_inc(s_key[4 * h + q], 16)

        @block.tensor
        def _(pe):
            with pe.Fori(0, NG) as i:
                for h in range(GH):
                    n = i * GH + h
                    pe.wait_ge(s["picked"], n + 3)
                    pe.wait_ge(s["multiplied"], n + GH - 1)
                    for q in range(4):
                        pe.wait_ge(s_query[4 * h + q], 16 * i + 16)
                        t = pe.matmul(k.psum[:, 2 * (h % 2) + q // 2, (q % 2) * D:(q % 2 + 1) * D],
                                      pick[h % 2][:, q, :], query_ring[:, 4 * h + q, :], start=True, stop=True)
                    t.then_inc(s["spread"], 1)

        @block.vector
        def _(dve):
            def choose(i, h):
                n = i * GH + h
                dve.wait_ge(s_cols[h % 2], (i * GH + h - h % 2) * 8 + 16)
                dve.wait_ge(s["spread"], n + GH - 1)
                dve.tensor_scalar(pick[h % 2].rearrange("p v s -> p (v s)"), cols[h % 2], k.iota_col[:, 0:1], None,
                                  ALU.is_equal).then_inc(s["picked"], 1)

            def multiply(i, h):
                n = i * GH + h
                dve.wait_ge(s["spread"], n + GH + 1)
                dve.wait_ge(s["scored"], n + GH - 1)
                for q in range(4):
                    dve.wait_ge(s_key[4 * h + q], 16 * i + 16)
                b = 2 * (h % 2)
                dve.tensor_tensor(prod[h % 2].rearrange("p a d -> p (a d)"),
                                  k.psum[:, b:b + 2, :].rearrange("p b n -> p (b n)"),
                                  key_ring[:, 4 * h:4 * h + 4, :].rearrange("p q d -> p (q d)"),
                                  ALU.mult).then_inc(s["multiplied"], 1)

            def reduce(i, h):
                n = i * GH + h
                passed(dve, s, s["multiplied"], n + GH + 1)
                dve.tensor_reduce(k.scores[:, ds(n * 4 * H, 4 * H)], prod[h % 2], AX,
                                  ALU.add).then_inc(s["scored"], 1)

            with dve.Fori(0, NG) as i:
                choose(i, 0)
                for h in range(GH):
                    if h + 1 < GH:
                        choose(i, h + 1)
                    multiply(i, h)
                    if h:
                        reduce(i, h - 1)
                reduce(i, GH - 1)


def build_softmax(nc, k, dram):
    a = Arena(k.arena, k.words)
    last, initial = a.take([4]), a.take([4])
    state8, last8 = a.take([4, SC]), a.take([4, SC])
    by_visit = k.scores[:, :].rearrange("p (c k h) -> p k c h", c=SC, k=VK)
    with stage(nc, "toscan", "ordered turned copied") as (block, s):
        @block.vector
        def _(dve):
            for g in range(VK // 4):
                dve.tensor_copy(k.stream[:, g * 512:(g + 1) * 512].rearrange("p (k c h) -> p k c h", k=4, c=SC),
                                by_visit[:, 4 * g:4 * g + 4]).then_inc(s["ordered"], 1)

        @block.tensor
        def _(pe):
            for g in range(VK // 4):
                pe.wait_ge(s["ordered"], g + 1)
                if g >= 2:
                    pe.wait_ge(s["copied"], g - 1)
                for q in range(4):
                    t = pe.transpose(k.psum[:, g % 2, q * P:(q + 1) * P],
                                     k.stream[:, (4 * g + q) * P:(4 * g + q + 1) * P], k.ident[:, :])
                t.then_inc(s["turned"], 1)

        @block.scalar
        def _(act):
            act.wait_ge(s["ordered"], VK // 4)
            for g in range(VK // 4):
                act.wait_ge(s["turned"], g + 1)
                act.copy(k.scores[:, g * 512:(g + 1) * 512], k.psum[:, g % 2, :]).then_inc(s["copied"], 1)

    with stage(nc, "scan", "initial scanned stored back chained sent loaded maximum less") as (block, s):
        passes = [(False, k.breaks[:, 0:CL], k.edge_f8, k.scores, CL - 1),
                  (True, k.breaks[:, 1:CL + 1], k.edge_b8, k.stream, 0)]

        @block.vector
        def _(dve):
            dve.memset(initial, -BIG).then_inc(s["initial"], 1)
            dve.wait_ge(s["initial"], 1)
            for n, (backward, breaks, edges, data, end) in enumerate(passes):
                turn = (lambda ap: ap[:, ::-1]) if backward else (lambda ap: ap)
                out = k.arena[:, 64:64 + CL]
                dve.tensor_tensor_scan(turn(out), turn(breaks), turn(data[:, 0:CL]), initial[:, 3:4],
                                       ALU.add, ALU.max).then_inc(s["scanned"], 1)
                dve.wait_ge(s["back"], 16 * (n + 1))
                dve.tensor_tensor_scan(turn(state8[0:H, n]), turn(edges[0:H, :]), turn(last8[0:H, n]), -BIG,
                                       ALU.add, ALU.max).then_inc(s["chained"], 1)
                dve.wait_ge(s["loaded"], 16 * (n + 1))
                dve.tensor_tensor_scan(turn(k.stream[:, 0:CL]), turn(breaks), turn(data[:, 0:CL]),
                                       initial[:, n:n + 1], ALU.add, ALU.max).then_inc(s["maximum"], 1)
                dve.wait_ge(s["maximum"], n + 1)
            dve.scalar_tensor_tensor(k.stream[:, 0:CL], k.stream[:, 0:CL], -1.0e9, k.scores[:, 0:CL],
                                     ALU.max, ALU.subtract).then_inc(s["less"], 1)

        @block.sync
        def _(sp):
            with nc.allow_non_contiguous_dma(reason="128 words"):
                for n, (backward, _, _, _, end) in enumerate(passes):
                    sp.wait_ge(s["scanned"], n + 1)
                    sp.dma_start(dram.carry[n], k.arena[:, 64 + end]).then_inc(s["stored"], 16)
                    sp.wait_ge(s["stored"], 16 * (n + 1))
                    sp.dma_start(last8[0:H, n], dram.carry[n].rearrange("(c h) -> h c", h=H)).then_inc(s["back"], 16)
                    sp.wait_ge(s["chained"], n + 1)
                    sp.dma_start(dram.carried[n].rearrange("(c h) -> h c", h=H), state8[0:H, n]).then_inc(s["sent"], 16)
                    sp.wait_ge(s["sent"], 16 * (n + 1))
                    to, of = (slice(0, P - H), slice(H, P)) if backward else (slice(H, P), slice(0, P - H))
                    sp.dma_start(initial[to, n:n + 1], dram.carried[n, of].unsqueeze(1)).then_inc(s["loaded"], 16)

        @block.scalar
        def _(act):
            act.wait_ge(s["less"], 1)
            act.activation(k.stream[:, 0:CL], k.stream[:, 0:CL], ACT.Exp, scale=-1.0)

    with stage(nc, "fromscan", "turned copied") as (block, s):
        weights = k.scores[:, :].rearrange("p (c k h) -> p k c h", c=SC, k=VK)

        @block.tensor
        def _(pe):
            for g in range(VK // 4):
                if g >= 2:
                    pe.wait_ge(s["copied"], g - 1)
                for q in range(4):
                    t = pe.transpose(k.psum[:, g % 2, q * P:(q + 1) * P],
                                     k.stream[:, (4 * g + q) * P:(4 * g + q + 1) * P], k.ident[:, :])
                t.then_inc(s["turned"], 1)

        @block.scalar
        def _(act):
            for g in range(VK // 4):
                act.wait_ge(s["turned"], g + 1)
                act.copy(weights[:, 4 * g:4 * g + 4], k.psum[:, g % 2, :].rearrange("p (k c h) -> p k c h", k=4, c=SC)
                         ).then_inc(s["copied"], 1)


def build_sums(nc, k, dram):
    a = Arena(k.arena, k.words)
    values = a.take([GV, RW])
    pick = [a.take([4, P]) for _ in range(2)]
    weighed = [a.take([4, RW]) for _ in range(2)]
    sums = a.take([GV, RW])
    index = [a.take([4], I32) for _ in range(GH)]
    names = "picked weighed multiplied summed indexed passed cleared " + \
        " ".join(f"value{q}" for q in range(GV)) + " " + " ".join(f"stored{h}" for h in range(GH))
    with stage(nc, "sums", names, True) as (block, s):
        s_value = [s[f"value{q}"] for q in range(GV)]
        s_stored = [s[f"stored{h}"] for h in range(GH)]

        @block.sync
        def _(sp):
            for sem in (s["picked"], s["weighed"], s["multiplied"]):
                sp.sem_inc(sem, GH)
            sp.sem_inc(s["summed"], GV)
            with sp.Fori(0, NG) as i:
                for h in range(GH):
                    n = i * GH + h
                    sp.wait_ge(s["summed"], n * 4 + 4 + GV)
                    sp.dma_start(dram.sums[ds(n * 4 * P, 4 * P), :].rearrange("(q p) n -> p q n", p=P),
                                 sums[:, 4 * h:4 * h + 4, :]).then_inc(s_stored[h], 16)
            for h in range(GH):
                sp.wait_ge(s_stored[h], 16 * NG)

        @block.gpsimd
        def _(pool):
            with pool.Fori(0, NG) as i:
                for h in range(GH):
                    n = i * GH + h
                    passed(pool, s, s["weighed"], n + 1)
                    gather_idx(pool, s, index[h], k.idx_value, n)
                    for q in range(4):
                        pool.indirect_dma_start(
                            out=values[:, 4 * h + q, :], out_offset=None, in_=dram.value_rows,
                            in_offset=bass.IndirectOffsetOnAxis(ap=index[h][:, q:q + 1], axis=0)
                        ).then_inc(s_value[4 * h + q], 16)

        @block.tensor
        def _(pe):
            with pe.Fori(0, NG) as i:
                for h in range(GH):
                    n = i * GH + h
                    pe.wait_ge(s["picked"], n + GH + 1)
                    pe.wait_ge(s["weighed"], n + GH + 1)
                    for q in range(4):
                        pe.wait_ge(s["summed"], n * 4 + q + 1 + GV - 8)
                        t = pe.matmul(k.psum[:, 4 * (h % 2) + q, 0:RW], pick[h % 2][:, q, :],
                                      weighed[h % 2][:, q, :], start=True, stop=True)
                    t.then_inc(s["multiplied"], 1)

        @block.vector
        def _(dve):
            dve.memset(sums, 0.0).then_inc(s["cleared"], 1)
            dve.wait_ge(s["cleared"], 1)
            weights = k.scores[:, :].rearrange("p (v h) -> p v h", h=H)

            def choose(i, h):
                n = i * GH + h
                dve.wait_ge(s["multiplied"], n + GH - 1)
                dve.tensor_tensor(pick[h % 2], along(k.iota_row[:, :], 1, 4),
                                  along(k.keycol[:, ds(n * 4, 4)], 2, P), ALU.is_equal).then_inc(s["picked"], 1)

            def weigh(i, h, pair):
                n = i * GH + h
                for q in (pair, pair + 1):
                    dve.wait_ge(s_value[4 * h + q], 16 * i + 16)
                ins = dve.tensor_tensor(
                    weighed[h % 2][:, pair:pair + 2].rearrange("p q (h d) -> p q h d", h=H),
                    values[:, 4 * h + pair:4 * h + pair + 2, :].rearrange("p q (h d) -> p q h d", h=H),
                    along(weights[:, ds(n * 4 + pair, 2), :], 3, HD + 1), ALU.mult)
                if pair:
                    ins.then_inc(s["weighed"], 1)

            def add(i, h, q):
                n = i * GH + h
                m = n * 4 + q
                if q == 0:
                    dve.wait_ge(s["multiplied"], n + GH + 1)
                    dve.wait_ge(s_stored[h], 16 * i)
                dve.wait_ge(s["summed"], m + GV)
                at = 4 * h + q
                dve.scalar_tensor_tensor(sums[:, at, :], sums[:, (at - 1) % GV, :], k.same_block[:, ds(m, 1)],
                                         k.psum[:, 4 * (h % 2) + q, 0:RW], ALU.mult, ALU.add).then_inc(s["summed"], 1)

            def turn(i, first=False, last=False):
                for h in range(GH):
                    ahead = (i, h + 1) if h + 1 < GH else (i + 1, 0)
                    back = (i, h - 1) if h else (i - 1, GH - 1)
                    more, had = not (last and h + 1 == GH), not (first and h == 0)
                    if more:
                        choose(*ahead)
                    if had:
                        add(*back, 0)
                    if more:
                        weigh(*ahead, 0)
                    if had:
                        add(*back, 1)
                    if more:
                        weigh(*ahead, 2)
                    if had:
                        add(*back, 2)
                        add(*back, 3)

            choose(0, 0)
            weigh(0, 0, 0)
            weigh(0, 0, 2)
            turn(0, first=True)
            with dve.Fori(1, NG - 1) as i:
                turn(i)
            turn(NG - 1, last=True)
            for q in range(4):
                add(NG - 1, GH - 1, q)


class Kept:
    pass


class Dram:
    pass


def setup(nc, ctx):
    k, dram = Kept(), Dram()

    def sb(name, shape, dtype=F32):
        return ctx.enter_context(nc.sbuf_tensor(name, shape, dtype))

    k.ident = sb("ident", [P, P])
    k.iota_row = sb("iota_row", [P, P])
    k.iota_col = sb("iota_col", [P, 1])
    k.idx_key = sb("idx_key", [P, V], I32)
    k.idx_value = sb("idx_value", [P, V], I32)
    k.keycol = sb("keycol", [P, V])
    k.same_block = sb("same_block", [P, V])
    k.block_row = sb("block_row", [1, V], I32)
    k.idx_sums = sb("idx_sums", [P, NCH * NB], I32)
    k.onehot = sb("onehot", [P, NCH * NB, TN])
    k.breaks = sb("breaks", [P, CL + 1], BF16)
    k.edge_f8 = sb("edge_f8", [H, SC])
    k.edge_b8 = sb("edge_b8", [H, SC])
    k.scores = sb("scores", [P, V * H])
    k.stream = sb("stream", [P, V * H])
    k.words = 30000
    k.arena = ctx.enter_context(nc.sbuf_tensor("arena", [P, k.words], F32))
    k.psum = ctx.enter_context(nc.psum_tensor("psum", [P, 8, 512], F32))

    def dr(name, shape, dtype=F32):
        return nc.dram_tensor(f"scratch_{name}", shape, dtype, kind="Internal").ap()

    dram.comb = dr("comb", (TILES, 3 * P))
    dram.reach = dr("reach", (TILES,))
    dram.keyrow = dr("keyrow", (V, P), BF16)
    dram.key = dr("key", (V * P,))
    dram.blocks_i = dr("blocks_i", (V,), I32)
    dram.blocks_f = dr("blocks_f", (V,))
    dram.edge_f = dr("edge_f", (P,))
    dram.edge_b = dr("edge_b", (P,))
    dram.counts = dr("counts", (NCH * NB,))
    dram.carry = dr("carry", (4, P))
    dram.carried = dr("carried", (4, P))
    dram.state = dr("state", (NP, D))
    dram.xn = dr("xn", (NP, D))
    dram.q = dr("q", (NP, D))
    dram.key_rows = dr("key_rows", (NP * TE, D))
    dram.value_rows = dr("value_rows", (NP, RW))
    dram.sums = dr("sums", (V * P, RW))
    return k, dram


def transpose_chunk(pe, k, banks, rows):
    for f in range(2):
        for q in range(NB):
            t = pe.transpose(k.psum[:, banks + f, q * P:(q + 1) * P], rows[:, q, f * P:(f + 1) * P], k.ident[:, :])
    return t


def two_banks(k, bank):
    return k.psum[:, bank:bank + 2, :].rearrange("p a (b d) -> p (a b) d", d=D)


def copy_turned(act, k, bank, to):
    return act.copy(to.rearrange("p f n -> p (f n)"), k.psum[:, bank:bank + 2, :].rearrange("p a n -> p (a n)"))


def build_layer_tail(nc, k, w, layer, dram):
    a = Arena(k.arena, k.words)
    names = "bo ln1_g ln1_b b2 ln2_g ln2_b"
    vec = {n: a.take([D]) for n in names.split()}
    wo, w1, w2, b1 = a.take([2, D]), a.take([2, FF]), a.take([FF // P, D]), a.take([FF // P])
    index = a.take([NB], I32)
    got, state = a.take([NB, RW]), a.take([NB, D])
    total, inverse = a.take([NB, H]), a.take([NB, H])
    mean, y, unit = a.take([NB, D]), a.take([NB, D]), a.take([NB, D])
    meanT, unitT = a.take([2, CH]), a.take([2, CH])
    hidden = a.take([FF // P, CH])
    stats, moments, rstd = a.take([NB, 6]), a.take([NB, 2]), a.take([NB])
    eps, minus_half = a.take([NB]), a.take([NB])
    rest, y2, out = a.take([NB, D]), a.take([NB, D]), a.take([NB, D])
    stats2, moments2, rstd2 = a.take([NB, 6]), a.take([NB, 2]), a.take([NB])
    with stage(nc, "tail", "weights consts indexed got0 got1 got2 got3 state total inverse mean turned1 copied1 "
               "attended added1 biased1 turned2 copied2 hidden gelu second added2 rest stored passed "
               + norm_sems("ln1") + " " + norm_sems("ln2"), True) as (block, s):
        s_got = [s["got0"], s["got1"], s["got2"], s["got3"]]
        n_weights = 16 * (len(vec) + 4)
        J = FF // P

        def chunks(eng, layers):
            with eng.Fori(0, NCH - 2) as c:
                layers(c, True, True)
            layers(NCH - 2, True, False)
            layers(NCH - 1, False, False)

        @block.sync
        def _(sp):
            lay = ds(layer, 1)
            for n, to in vec.items():
                sp.dma_start(to, w[n][lay, :].rearrange("a d -> (a d)").partition_broadcast(P)).then_inc(s["weights"], 16)
            sp.dma_start(wo, w["Wo"][lay].rearrange("a (f p) n -> (a p) f n", p=P)).then_inc(s["weights"], 16)
            sp.dma_start(w1, w["w1"][lay].rearrange("a (f p) n -> (a p) f n", p=P)).then_inc(s["weights"], 16)
            sp.dma_start(w2, w["w2"][lay].rearrange("a (f p) n -> (a p) f n", p=P)).then_inc(s["weights"], 16)
            with nc.allow_non_contiguous_dma(reason="once a layer"):
                sp.dma_start(b1, w["b1"][lay, :].rearrange("a (f p) -> (a p) f", p=P)).then_inc(s["weights"], 16)
            sp.dma_start(state, chunk_rows(dram.state, 0)).then_inc(s["state"], 16)
            sp.wait_ge(s["biased1"], 1)
            sp.dma_start(state, chunk_rows(dram.state, 1)).then_inc(s["state"], 16)

            def layers(c, one, two):
                if two:
                    sp.wait_ge(s["biased1"], c + 2)
                    sp.dma_start(state, chunk_rows(dram.state, c + 2)).then_inc(s["state"], 16)
                sp.wait_ge(s["ln2_shifted"], c + 1)
                sp.dma_start(chunk_rows(dram.state, c), out).then_inc(s["stored"], 16)

            chunks(sp, layers)
            sp.wait_ge(s["stored"], 16 * NCH)

        @block.gpsimd
        def _(pool):
            pool.memset(eps, 1e-5)
            pool.memset(minus_half, -0.5).then_inc(s["consts"], 1)
            pool.wait_ge(s["consts"], 1)

            def gather(c):
                passed(pool, s, s["mean"], c)
                pool.tensor_copy(index, k.idx_sums[:, ds(c * NB, NB)]).then_inc(s["indexed"], 1)
                passed(pool, s, s["indexed"], c + 1)
                for q in range(NB):
                    pool.indirect_dma_start(
                        out=got[:, q, :], out_offset=None, in_=dram.sums,
                        in_offset=bass.IndirectOffsetOnAxis(ap=index[:, q:q + 1], axis=0)).then_inc(s_got[q], 16)

            def layers(c, one, two):
                if two:
                    gather(c + 2)
                if one:
                    inverse_root(pool, s, "ln1", c + 2, moments, rstd, eps, minus_half)
                inverse_root(pool, s, "ln2", c + 1, moments2, rstd2, eps, minus_half)

            gather(0)
            gather(1)
            inverse_root(pool, s, "ln1", 1, moments, rstd, eps, minus_half)
            chunks(pool, layers)

        @block.vector
        def _(dve):
            def average(c):
                for q in range(NB):
                    dve.wait_ge(s_got[q], 16 * c + 16)
                rows = got.rearrange("p q (h d) -> p q h d", h=H)
                dve.tensor_scalar(total, rows[:, :, :, HD], 1e-10, None, ALU.add).then_inc(s["total"], 1)
                dve.wait_ge(s["total"], c + 1)
                dve.reciprocal(inverse, total).then_inc(s["inverse"], 1)
                dve.wait_ge(s["inverse"], c + 1)
                dve.wait_ge(s["turned1"], c)
                dve.tensor_tensor(mean.rearrange("p q (h d) -> p q h d", h=H), rows[:, :, :, 0:HD],
                                  along(inverse, 3, HD), ALU.mult).then_inc(s["mean"], 1)

            def first_norm(c):
                dve.wait_ge(s["attended"], c + 1)
                dve.wait_ge(s["state"], 16 * c + 16)
                dve.tensor_tensor(y, two_banks(k, 2), state, ALU.add).then_inc(s["added1"], 1)
                dve.wait_ge(s["added1"], c + 1)
                dve.tensor_tensor(y, y, along(vec["bo"], 1, NB), ALU.add).then_inc(s["biased1"], 1)
                dve.wait_ge(s["biased1"], c + 1)
                dve.wait_ge(s["turned2"], c)
                normalize(dve, s, "ln1", c + 1, y, unit, stats, moments, rstd, vec["ln1_g"], vec["ln1_b"])

            def residual(c):
                dve.wait_ge(s["ln1_shifted"], c + 1)
                dve.tensor_tensor(rest, unit, along(vec["b2"], 1, NB), ALU.add).then_inc(s["rest"], 1)

            def layers(c, one, two):
                if one:
                    first_norm(c + 1)
                if two:
                    average(c + 2)
                dve.wait_ge(s["second"], c + 1)
                dve.wait_ge(s["rest"], c + 1)
                dve.tensor_tensor(y2, two_banks(k, 4), rest, ALU.add).then_inc(s["added2"], 1)
                dve.wait_ge(s["added2"], c + 1)
                dve.wait_ge(s["stored"], 16 * c)
                normalize(dve, s, "ln2", c + 1, y2, out, stats2, moments2, rstd2, vec["ln2_g"], vec["ln2_b"])
                if one:
                    residual(c + 1)

            dve.wait_ge(s["weights"], n_weights)
            average(0)
            first_norm(0)
            average(1)
            residual(0)
            chunks(dve, layers)

        @block.tensor
        def _(pe):
            def turn_mean(c):
                pe.wait_ge(s["mean"], c + 1)
                transpose_chunk(pe, k, 0, mean).then_inc(s["turned1"], 1)

            def attend(c):
                pe.wait_ge(s["copied1"], c + 1)
                pe.wait_ge(s["added1"], c)
                for q in range(NB):
                    for f in range(2):
                        t = pe.matmul(two_banks(k, 2)[:, q, :], meanT[:, f, q * P:(q + 1) * P], wo[:, f, :],
                                      start=(f == 0), stop=(f == 1))
                t.then_inc(s["attended"], 1)

            def turn_unit(c):
                pe.wait_ge(s["ln1_shifted"], c + 1)
                transpose_chunk(pe, k, 0, unit).then_inc(s["turned2"], 1)

            def first(c, j):
                if j >= 2:
                    pe.wait_ge(s["gelu"], c * J + j - 1)
                for f in range(2):
                    t = pe.matmul(k.psum[:, 6 + j % 2, :], w1[:, f, j * P:(j + 1) * P], unitT[:, f, :],
                                  start=(f == 0), stop=(f == 1))
                t.then_inc(s["hidden"], 1)

            def layers(c, one, two):
                pe.wait_ge(s["copied2"], c + 1)
                for j in range(J):
                    if j == J // 2 and one:
                        turn_mean(c + 1)
                    first(c, j)
                if one:
                    attend(c + 1)
                pe.wait_ge(s["gelu"], (c + 1) * J)
                pe.wait_ge(s["added2"], c)
                for q in range(NB):
                    for j in range(J):
                        t = pe.matmul(two_banks(k, 4)[:, q, :], hidden[:, j, q * P:(q + 1) * P], w2[:, j, :],
                                      start=(j == 0), stop=(j == J - 1))
                t.then_inc(s["second"], 1)
                if one:
                    turn_unit(c + 1)

            pe.wait_ge(s["weights"], n_weights)
            turn_mean(0)
            attend(0)
            turn_unit(0)
            chunks(pe, layers)

        @block.scalar
        def _(act):
            def copy_mean(c):
                act.wait_ge(s["turned1"], c + 1)
                copy_turned(act, k, 0, meanT).then_inc(s["copied1"], 1)

            def copy_unit(c):
                act.wait_ge(s["turned2"], c + 1)
                copy_turned(act, k, 0, unitT).then_inc(s["copied2"], 1)

            def layers(c, one, two):
                for j in range(J):
                    if j == J // 2 and one:
                        copy_mean(c + 1)
                    act.wait_ge(s["hidden"], c * J + j + 1)
                    if j == 0:
                        act.wait_ge(s["second"], c)
                    act.activation(hidden[:, j, :], k.psum[:, 6 + j % 2, :], ACT.Gelu,
                                   bias=b1[:, j:j + 1]).then_inc(s["gelu"], 1)
                if one:
                    copy_unit(c + 1)

            act.wait_ge(s["weights"], n_weights)
            copy_mean(0)
            copy_unit(0)
            chunks(act, layers)


def build_linear_attention(nc, k, w, mixed, dram):
    a = Arena(k.arena, k.words)
    assert a.take([2, D]) is not None
    wq, wk, wv, wo = (a.take([2, D]) for _ in range(4))
    wkvT, woT = a.take([2, 2 * D]), a.take([2, D])
    g = [a.take([MD]) for _ in range(4)]
    rows, rowsT = [a.take([D]) for _ in range(2)], a.take([2, P])
    kvs, square = [a.take([2 * MH, MD]) for _ in range(2)], a.take([2 * MH, MD])
    sums, mean, var, rstd = (a.take([2 * MH]) for _ in range(4))
    eps, minus_half, mask = a.take([2 * MH]), a.take([2 * MH]), a.take([BLK])
    total, paired, first = a.take([2, P]), a.take([2, P]), a.take([2, D])
    with stage(nc, "mixkv", "weights turned copied loaded0 loaded1 xturned xcopied projected summed mean centred squared "
               "spread var eps rstd unit scaled shifted masked product added consts mask zeroed") as (block, s):
        s_loaded = [s["loaded0"], s["loaded1"]]

        def steps(eng, step):
            with eng.Fori(0, (BLK - 2) // 2) as i:
                for b in range(2):
                    step(2 * i + b, b, i, True, True)
            for n in range((BLK - 2) // 2 * 2, BLK):
                step(n, n % 2, n // 2, n + 1 < BLK, n + 2 < BLK)

        @block.sync
        def _(sp):
            for to, n in ((wq, "wq"), (wk, "wk"), (wv, "wv"), (wo, "wo")):
                sp.dma_start(to, w[n].rearrange("(f p) n -> p f n", p=P)).then_inc(s["weights"], 16)
            for to, n in zip(g, ("ln_k_g", "ln_k_b", "ln_v_g", "ln_v_b")):
                sp.dma_start(to, w[n].partition_broadcast(P)).then_inc(s["weights"], 16)

            def load(n, b):
                sp.dma_start(rows[b], dram.xn[ds(n * P, P), :]).then_inc(s_loaded[b], 16)

            def step(n, b, i, one, two):
                if two:
                    sp.wait_ge(s["xturned"], n + 1)
                    load(n + 2, b)

            load(0, 0)
            load(1, 1)
            steps(sp, step)

        @block.gpsimd
        def _(pool):
            pool.memset(eps, 1e-5).then_inc(s["consts"], 1)
            pool.memset(minus_half, -0.5).then_inc(s["consts"], 1)
            pool.memset(mask, 1.0).then_inc(s["consts"], 1)
            pool.wait_ge(s["consts"], 3)
            pool.affine_select(out=mask, in_=mask, compare_op=ALU.is_ge, fill=0.0, base=N - 1,
                               pattern=[[-P, BLK]], channel_multiplier=-1).then_inc(s["mask"], 1)
            with pool.Fori(0, BLK) as b:
                pool.wait_ge(s["var"], b + 1)
                pool.tensor_tensor(rstd, var, eps, ALU.add).then_inc(s["eps"], 1)
                pool.wait_ge(s["eps"], b + 1)
                pool.tensor_tensor(rstd, rstd, minus_half, ALU.pow).then_inc(s["rstd"], 1)

        @block.tensor
        def _(pe):
            pe.wait_ge(s["weights"], 16 * 8)
            for n, of in enumerate((wk, wv, wo)):
                for f in range(2):
                    for o in range(2):
                        t = pe.transpose(k.psum[:, n, (f * 2 + o) * P:(f * 2 + o + 1) * P],
                                         of[:, o, f * P:(f + 1) * P], k.ident[:, :])
            t.then_inc(s["turned"], 1)
            pe.wait_ge(s["copied"], 3)

            def project(n, b, i):
                pe.wait_ge(s_loaded[b], 16 * i + 16)
                for f in range(2):
                    t = pe.transpose(k.psum[:, 3, f * P:(f + 1) * P], rows[b][:, f * P:(f + 1) * P], k.ident[:, :])
                t.then_inc(s["xturned"], 1)
                pe.wait_ge(s["xcopied"], n + 1)
                for f in range(2):
                    t = pe.matmul(k.psum[:, 6 + b, :], rowsT[:, f, :], wkvT[:, f, :], start=(f == 0), stop=(f == 1))
                t.then_inc(s["projected"], 1)

            def step(n, b, i, one, two):
                if two:
                    pe.wait_ge(s["centred"], n + 1)
                    project(n + 2, b, i + 1)
                pe.wait_ge(s["masked"], n + 1)
                for f in range(2):
                    t = pe.matmul(k.psum[:, 5, f * P:(f + 1) * P],
                                  kvs[b][:, 2 * f:2 * f + 2, :].rearrange("p a b -> p (a b)"),
                                  kvs[b][:, MH + 2 * f:MH + 2 * f + 2, :].rearrange("p a b -> p (a b)"),
                                  start=True, stop=True)
                t.then_inc(s["product"], 1)

            project(0, 0, 0)
            project(1, 1, 0)
            steps(pe, step)

        @block.scalar
        def _(act):
            act.wait_ge(s["turned"], 1)
            for n in range(2):
                act.copy(wkvT[:, :, n * D:(n + 1) * D],
                         k.psum[:, n, :].rearrange("p (f n) -> p f n", f=2)).then_inc(s["copied"], 1)
            act.copy(woT, k.psum[:, 2, :].rearrange("p (f n) -> p f n", f=2)).then_inc(s["copied"], 1)

            def copy(n):
                act.wait_ge(s["xturned"], n + 1)
                act.wait_ge(s["projected"], n)
                act.copy(rowsT.rearrange("p f n -> p (f n)"), k.psum[:, 3, 0:2 * P]).then_inc(s["xcopied"], 1)

            def squares(n, b):
                act.wait_ge(s["centred"], n + 1)
                act.wait_ge(s["spread"], n)
                act.activation(square, kvs[b], ACT.Square).then_inc(s["squared"], 1)

            def step(n, b, i, one, two):
                if two:
                    copy(n + 2)
                if one:
                    squares(n + 1, 1 - b)

            copy(0)
            copy(1)
            squares(0, 0)
            steps(act, step)

        @block.vector
        def _(dve):
            dve.memset(total, 0.0).then_inc(s["zeroed"], 1)
            dve.memset(paired, 0.0).then_inc(s["zeroed"], 1)
            dve.wait_ge(s["zeroed"], 2)
            dve.wait_ge(s["weights"], 16 * 8)
            dve.wait_ge(s["mask"], 1)

            def centre(n, b):
                out = k.psum[:, 6 + b, :].rearrange("p (h d) -> p h d", h=2 * MH)
                dve.wait_ge(s["projected"], n + 1)
                dve.wait_ge(s["var"], n)
                dve.tensor_reduce(sums, out, AX, ALU.add).then_inc(s["summed"], 1)
                dve.wait_ge(s["summed"], n + 1)
                dve.tensor_scalar(mean, sums, 1.0 / MD, None, ALU.mult).then_inc(s["mean"], 1)
                dve.wait_ge(s["mean"], n + 1)
                dve.tensor_tensor(kvs[b], out, along(mean, 2, MD), ALU.subtract).then_inc(s["centred"], 1)

            def variance(n):
                dve.wait_ge(s["squared"], n + 1)
                dve.tensor_reduce(sums, square, AX, ALU.add).then_inc(s["spread"], 1)
                dve.wait_ge(s["spread"], n + 1)
                dve.tensor_scalar(var, sums, 1.0 / MD, None, ALU.mult).then_inc(s["var"], 1)

            def norm(n, kv):
                dve.wait_ge(s["rstd"], n + 1)
                dve.tensor_tensor(kv, kv, along(rstd, 2, MD), ALU.mult).then_inc(s["unit"], 1)
                dve.wait_ge(s["unit"], n + 1)
                for half in range(2):
                    ins = dve.tensor_tensor(kv[:, half * MH:(half + 1) * MH], kv[:, half * MH:(half + 1) * MH],
                                            along(g[2 * half], 1, MH), ALU.mult)
                ins.then_inc(s["scaled"], 1)
                dve.wait_ge(s["scaled"], n + 1)
                for half in range(2):
                    ins = dve.tensor_tensor(kv[:, half * MH:(half + 1) * MH], kv[:, half * MH:(half + 1) * MH],
                                            along(g[2 * half + 1], 1, MH), ALU.add)
                ins.then_inc(s["shifted"], 1)
                dve.wait_ge(s["shifted"], n + 1)
                dve.tensor_scalar(kv[:, 0:MH], kv[:, 0:MH], mask[:, ds(n, 1)], None, ALU.mult).then_inc(s["masked"], 1)

            def step(n, b, i, one, two):
                if one:
                    centre(n + 1, 1 - b)
                norm(n, kvs[b])
                if one:
                    variance(n + 1)
                dve.wait_ge(s["product"], n + 1)
                dve.wait_ge(s["added"], n)
                dve.tensor_tensor(total, total, k.psum[:, 5, 0:2 * P].rearrange("p (f n) -> p f n", f=2),
                                  ALU.add).then_inc(s["added"], 1)

            centre(0, 0)
            variance(0)
            steps(dve, step)
            dve.wait_ge(s["added"], BLK)
            for half in range(2):
                part = slice(half * MD, (half + 1) * MD)
                dve.tensor_scalar(paired[part, :, part], total[part, :, part], 1.0 / N, None, ALU.mult)

    with stage(nc, "mixw", "first copied second") as (block, s):
        @block.tensor
        def _(pe):
            for f in range(2):
                t = pe.matmul(k.psum[:, f, 0:D], paired[:, f, :], wq[:, f, :], start=True, stop=True)
            t.then_inc(s["first"], 1)
            pe.wait_ge(s["copied"], 1)
            for o in range(2):
                for f in range(2):
                    t = pe.matmul(k.psum[:, 2 + o, 0:D], first[:, f, o * P:(o + 1) * P], woT[:, f, :],
                                  start=(f == 0), stop=(f == 1))
            t.then_inc(s["second"], 1)

        @block.vector
        def _(dve):
            dve.wait_ge(s["first"], 1)
            dve.tensor_copy(first, k.psum[:, 0:2, 0:D]).then_inc(s["copied"], 1)
            dve.wait_ge(s["second"], 1)
            dve.tensor_copy(mixed, k.psum[:, 2:4, 0:D])


def build_experts(nc, k, w, x, mixed, mix_bo, gnn_g, gnn_b, out_dram, dram):
    a = Arena(k.arena, k.words)
    a.take([2, D])
    EH = NX * 2
    w1, w2, w3 = (a.take([EH, HE]) for _ in range(3))
    wr, br, bo = a.take([2, NX]), a.take([NX]), a.take([HE], parts=NX)
    bnv = [[a.take([EH]) for _ in range(5)] for _ in range(2)]
    scale, shift = [a.take([EH]) for _ in range(2)], [a.take([EH]) for _ in range(2)]
    og, ob, mbo = a.take([D]), a.take([D]), a.take([D])
    xr, x2, st = a.take([NB, D]), a.take([NB, D]), a.take([NB, D])
    xnT, unitT = a.take([2, CH]), a.take([2, CH])
    h1, h2 = a.take([2, CH]), a.take([2, CH])
    stats, moments, rstd = a.take([NB, 6]), a.take([NB, 2]), a.take([NB])
    stats2, moments2, rstd2 = a.take([NB, 6]), a.take([NB, 2]), a.take([NB])
    eps, minus_half, bneps, bnhalf = a.take([NB]), a.take([NB]), a.take([EH]), a.take([EH])
    logits, most, gates, gsum, ginv = a.take([NB, NX]), a.take([NB]), a.take([NB, NX]), a.take([NB]), a.take([NB])
    gatesT = a.take([CH], parts=NX)
    big = k.scores[:, :]
    xn = big[:, 0:NB * D].rearrange("p (q d) -> p q d", q=NB)
    gn = big[:, NB * D:2 * NB * D].rearrange("p (q d) -> p q d", q=NB)
    acc = [big[:, (2 + n) * NB * D:(3 + n) * NB * D].rearrange("p (q d) -> p q d", q=NB) for n in range(2)]
    unit = big[:, 4 * NB * D:5 * NB * D].rearrange("p (q d) -> p q d", q=NB)
    start = big[:, 5 * NB * D:6 * NB * D].rearrange("p (q d) -> p q d", q=NB)
    with stage(nc, "bnfold", "loaded consts eps root scale diff prod done") as (block, s):
        @block.sync
        def _(sp):
            with nc.allow_non_contiguous_dma(reason="once"):
                for layer, names in enumerate((("b1", "g1", "be1", "m1", "v1"), ("b2", "g2", "be2", "m2", "v2"))):
                    for to, n in zip(bnv[layer], names):
                        sp.dma_start(to, w[n].rearrange("e (f p) -> p (e f)", p=P)).then_inc(s["loaded"], 16)
            for to, n in ((w1, "W1"), (w2, "W2"), (w3, "Wo")):
                sp.dma_start(to, w[n].rearrange("e (f p) n -> p (e f) n", p=P)).then_inc(s["loaded"], 16)
            sp.dma_start(wr, w["Wr"].rearrange("(f p) e -> p f e", p=P)).then_inc(s["loaded"], 16)
            sp.dma_start(br, w["br"].partition_broadcast(P)).then_inc(s["loaded"], 16)
            sp.dma_start(bo, w["bo"]).then_inc(s["loaded"], 16)
            for to, of in ((og, gnn_g), (ob, gnn_b), (mbo, mix_bo)):
                sp.dma_start(to, of.partition_broadcast(P)).then_inc(s["loaded"], 16)
            sp.wait_ge(s["loaded"], 16 * 19)

        @block.gpsimd
        def _(pool):
            for to, value in ((bneps, 1e-3), (bnhalf, -0.5), (eps, 1e-5), (minus_half, -0.5)):
                pool.memset(to, value).then_inc(s["consts"], 1)
            pool.wait_ge(s["consts"], 4)
            pool.wait_ge(s["loaded"], 16 * 19)
            for n in range(2):
                pool.tensor_tensor(scale[n], bnv[n][4], bneps, ALU.add).then_inc(s["eps"], 1)
                pool.wait_ge(s["eps"], n + 1)
                pool.tensor_tensor(scale[n], scale[n], bnhalf, ALU.pow).then_inc(s["root"], 1)
                pool.wait_ge(s["root"], n + 1)
                pool.tensor_tensor(scale[n], scale[n], bnv[n][1], ALU.mult).then_inc(s["scale"], 1)
                pool.tensor_tensor(shift[n], bnv[n][0], bnv[n][3], ALU.subtract).then_inc(s["diff"], 1)
                pool.wait_ge(s["scale"], n + 1)
                pool.wait_ge(s["diff"], n + 1)
                pool.tensor_tensor(shift[n], shift[n], scale[n], ALU.mult).then_inc(s["prod"], 1)
                pool.wait_ge(s["prod"], n + 1)
                pool.tensor_tensor(shift[n], shift[n], bnv[n][2], ALU.add).then_inc(s["done"], 1)

    with stage(nc, "experts", "x xn state turned copied mixed summed1 summed2 summed3 turned2 copied2 routed lbias most less exp "
               "gsum ginv gates gturned gcopied biased start h1 a1 h2 a2 y acc stored passed "
               + norm_sems("ln1") + " " + norm_sems("ln2")) as (block, s):
        def chunks(eng, turns):
            with eng.Fori(0, NCH - 1) as c:
                turns(c, True)
            turns(NCH - 1, False)

        @block.sync
        def _(sp):
            def load(c):
                sp.wait_ge(s["ln1_unit"], c)
                sp.dma_start(st, chunk_rows(dram.state, c)).then_inc(s["state"], 16)
                sp.wait_ge(s["turned"], c)
                sp.dma_start(xn, chunk_rows(dram.xn, c)).then_inc(s["xn"], 16)
                sp.wait_ge(s["summed3"], c)
                sp.dma_start(xr, chunk_rows(x, c)).then_inc(s["x"], 16)

            def turns(c, more):
                if more:
                    load(c + 1)
                sp.wait_ge(s["acc"], (c + 1) * NX)
                sp.dma_start(chunk_rows(out_dram, c), acc[(NX - 1) % 2]).then_inc(s["stored"], 16)

            load(0)
            chunks(sp, turns)
            sp.wait_ge(s["stored"], 16 * NCH)

        @block.gpsimd
        def _(pool):
            with pool.Fori(0, NCH) as c:
                inverse_root(pool, s, "ln1", c + 1, moments, rstd, eps, minus_half)
                inverse_root(pool, s, "ln2", c + 1, moments2, rstd2, eps, minus_half)

        @block.tensor
        def _(pe):
            def product(bank, wts, e, of):
                for f2 in range(2):
                    for f in range(2):
                        t = pe.matmul(k.psum[:, bank + f2, :], wts[:, 2 * e + f, f2 * P:(f2 + 1) * P], of[:, f, :],
                                      start=(f == 0), stop=(f == 1))
                return t

            def turn_xn(c):
                pe.wait_ge(s["xn"], 16 * c + 16)
                pe.wait_ge(s["start"], c)
                transpose_chunk(pe, k, 6, xn).then_inc(s["turned"], 1)

            def mix(c):
                pe.wait_ge(s["copied"], c + 1)
                for q in range(NB):
                    for f in range(2):
                        t = pe.matmul(two_banks(k, 6)[:, q, :], xnT[:, f, q * P:(q + 1) * P], mixed[:, f, :],
                                      start=(f == 0), stop=(f == 1))
                t.then_inc(s["mixed"], 1)

            def turn_unit(c):
                pe.wait_ge(s["summed1"], c + 1)
                pe.wait_ge(s["ln2_unit"], c + 1)
                transpose_chunk(pe, k, 6, unit).then_inc(s["turned2"], 1)

            def first(c, e):
                pe.wait_ge(s["a1"], c * NX + e)
                product(0, w1, e, unitT).then_inc(s["h1"], 1)

            def route(c):
                pe.wait_ge(s["copied2"], c + 1)
                first(c, 0)
                for q in range(NB):
                    for f in range(2):
                        t = pe.matmul(k.psum[:, 6, q * NX:(q + 1) * NX], unitT[:, f, q * P:(q + 1) * P], wr[:, f, :],
                                      start=(f == 0), stop=(f == 1))
                t.then_inc(s["routed"], 1)

            def turns(c, more):
                for e in range(NX):
                    n = c * NX + e
                    pe.wait_ge(s["a1"], n + 1)
                    pe.wait_ge(s["a2"], n)
                    product(4, w2, e, h1).then_inc(s["h2"], 1)
                    if e == 0:
                        pe.wait_ge(s["gates"], c + 1)
                        for q in range(NB):
                            t = pe.transpose(k.psum[0:NX, 7, q * P:(q + 1) * P], gates[:, q, :], k.ident[:, :])
                        t.then_inc(s["gturned"], 1)
                    if e < NX - 1:
                        first(c, e + 1)
                    elif more:
                        route(c + 1)
                    if e == 0:
                        pe.wait_ge(s["gcopied"], c + 1)
                        for q in range(NB):
                            t = pe.matmul(two_banks(k, 6)[:, q, :], gatesT[:, q * P:(q + 1) * P], bo[:, :],
                                          start=True, stop=True)
                        t.then_inc(s["biased"], 1)
                    if e == 1 and more:
                        turn_xn(c + 1)
                    if e == 2 and more:
                        mix(c + 1)
                    if e == 6 and more:
                        turn_unit(c + 1)
                    pe.wait_ge(s["a2"], n + 1)
                    pe.wait_ge(s["acc"], n)
                    for q in range(NB):
                        for f in range(2):
                            t = pe.matmul(two_banks(k, 2)[:, q, :], h2[:, f, q * P:(q + 1) * P], w3[:, 2 * e + f, :],
                                          start=(f == 0), stop=(f == 1))
                    t.then_inc(s["y"], 1)

            turn_xn(0)
            mix(0)
            turn_unit(0)
            route(0)
            chunks(pe, turns)

        @block.scalar
        def _(act):
            def rectify(layer, e, bank, to):
                for f in range(2):
                    ins = act.activation(to[:, f, :], k.psum[:, bank + f, :], ACT.Relu,
                                         bias=shift[layer][:, 2 * e + f:2 * e + f + 1],
                                         scale=scale[layer][:, 2 * e + f:2 * e + f + 1])
                return ins

            def copy_xn(c):
                act.wait_ge(s["turned"], c + 1)
                copy_turned(act, k, 6, xnT).then_inc(s["copied"], 1)

            def copy_unit(c):
                act.wait_ge(s["turned2"], c + 1)
                act.wait_ge(s["h1"], c * NX)
                act.wait_ge(s["routed"], c)
                copy_turned(act, k, 6, unitT).then_inc(s["copied2"], 1)

            def first(c, e):
                act.wait_ge(s["h1"], c * NX + e + 1)
                act.wait_ge(s["h2"], c * NX + e)
                rectify(0, e, 0, h1).then_inc(s["a1"], 1)

            def route(c):
                first(c, 0)
                act.wait_ge(s["less"], c + 1)
                act.activation(logits, logits, ACT.Exp).then_inc(s["exp"], 1)

            def turns(c, more):
                for e in range(NX):
                    n = c * NX + e
                    act.wait_ge(s["h2"], n + 1)
                    act.wait_ge(s["y"], n)
                    rectify(1, e, 4, h2).then_inc(s["a2"], 1)
                    if e == 0:
                        act.wait_ge(s["gturned"], c + 1)
                        act.copy(gatesT, k.psum[0:NX, 7, :]).then_inc(s["gcopied"], 1)
                    if e < NX - 1:
                        first(c, e + 1)
                    elif more:
                        route(c + 1)
                    if e == 1 and more:
                        copy_xn(c + 1)
                    if e == 6 and more:
                        copy_unit(c + 1)

            copy_xn(0)
            copy_unit(0)
            route(0)
            chunks(act, turns)

        @block.vector
        def _(dve):
            def state_moments(c):
                dve.wait_ge(s["state"], 16 * c + 16)
                norm_moments(dve, s, "ln1", c + 1, st, stats, moments)

            def state_rows(c):
                norm_rows(dve, s, "ln1", c + 1, st, gn, moments, rstd, og, ob)

            def add_up(c):
                dve.wait_ge(s["ln1_shifted"], c + 1)
                dve.wait_ge(s["mixed"], c + 1)
                dve.tensor_tensor(x2, two_banks(k, 6), gn, ALU.add).then_inc(s["summed1"], 1)
                dve.wait_ge(s["summed1"], c + 1)
                dve.tensor_tensor(x2, x2, along(mbo, 1, NB), ALU.add).then_inc(s["summed2"], 1)
                dve.wait_ge(s["summed2"], c + 1)
                dve.wait_ge(s["x"], 16 * c + 16)
                dve.tensor_tensor(x2, x2, xr, ALU.add).then_inc(s["summed3"], 1)

            def unit_moments(c):
                dve.wait_ge(s["summed3"], c + 1)
                norm_moments(dve, s, "ln2", c + 1, x2, stats2, moments2)

            def unit_rows(c):
                dve.wait_ge(s["turned2"], c)
                norm_rows(dve, s, "ln2", c + 1, x2, unit, moments2, rstd2)

            def weigh(c):
                dve.wait_ge(s["routed"], c + 1)
                dve.tensor_tensor(logits, k.psum[:, 6, 0:NB * NX].rearrange("p (q e) -> p q e", q=NB),
                                  along(br, 1, NB), ALU.add).then_inc(s["lbias"], 1)
                dve.wait_ge(s["lbias"], c + 1)
                dve.tensor_reduce(most, logits, AX, ALU.max).then_inc(s["most"], 1)
                dve.wait_ge(s["most"], c + 1)
                dve.tensor_tensor(logits, logits, along(most, 2, NX), ALU.subtract).then_inc(s["less"], 1)
                dve.wait_ge(s["exp"], c + 1)
                dve.tensor_reduce(gsum, logits, AX, ALU.add).then_inc(s["gsum"], 1)
                dve.wait_ge(s["gsum"], c + 1)
                dve.reciprocal(ginv, gsum).then_inc(s["ginv"], 1)

            def turns(c, more):
                dve.wait_ge(s["ginv"], c + 1)
                dve.wait_ge(s["acc"], c * NX)
                dve.tensor_tensor(gates, logits, along(ginv, 2, NX), ALU.mult).then_inc(s["gates"], 1)
                dve.wait_ge(s["biased"], c + 1)
                dve.tensor_tensor(start, two_banks(k, 6), x2, ALU.add).then_inc(s["start"], 1)
                dve.wait_ge(s["gates"], c + 1)
                dve.wait_ge(s["start"], c + 1)
                within = {2: state_moments, 3: state_rows, 4: add_up, 5: unit_moments, 6: unit_rows, 7: weigh}
                for e in range(NX):
                    n = c * NX + e
                    if e in within and more:
                        within[e](c + 1)
                    if e == 1:
                        dve.wait_ge(s["stored"], 16 * c)
                    dve.wait_ge(s["y"], n + 1)
                    dve.wait_ge(s["acc"], n)
                    for q in range(NB):
                        ins = dve.scalar_tensor_tensor(acc[e % 2][:, q, :], two_banks(k, 2)[:, q, :],
                                                       gates[:, q, e:e + 1],
                                                       acc[(e + 1) % 2][:, q, :] if e else start[:, q, :],
                                                       ALU.mult, ALU.add)
                    ins.then_inc(s["acc"], 1)

            for step in (state_moments, state_rows, add_up, unit_moments, unit_rows, weigh):
                step(0)
            chunks(dve, turns)


def build(nc, t):
    with ExitStack() as ctx:
        k, dram = setup(nc, ctx)
        part = lambda prefix: {n[len(prefix):]: ap for n, ap in t.items() if n.startswith(prefix)}
        gnn, mix, ffn = part("L0_gnn_"), part("L0_mix_"), part("L0_ffn_")
        build_constants(nc, k)
        build_visits(nc, k, t["src"], t["dst"], t["edge_type_3"], t["node_type_4"], dram)
        build_input_norm(nc, k, t["x"], dram)
        weights = Arena(k.arena, k.words).take([H, 5 * HD])
        with nc.Fori(0, L) as layer:
            build_type_weights(nc, k, gnn, layer, weights)
            build_rows(nc, k, weights, dram)
            build_scores(nc, k, dram)
            build_softmax(nc, k, dram)
            build_sums(nc, k, dram)
            build_layer_tail(nc, k, gnn, layer, dram)
        mixed = Arena(k.arena, k.words).take([2, D])
        build_linear_attention(nc, k, mix, mixed, dram)
        build_experts(nc, k, ffn, t["x"], mixed, mix["bo"], gnn["out_g"], gnn["out_b"], t["out"], dram)


_NAMES = ["x", "src", "dst", "edge_type_3", "node_type_4"] + \
    [f"L0_gnn_{n}" for n in ("W_Q", "W_K", "W_V", "W_E", "mu", "Wo", "bo", "ln1_g", "ln1_b", "ln2_g", "ln2_b",
                             "w1", "b1", "w2", "b2", "out_g", "out_b")] + \
    [f"L0_mix_{n}" for n in ("wq", "wk", "wv", "wo", "bo", "ln_k_g", "ln_k_b", "ln_v_g", "ln_v_b")] + \
    [f"L0_ffn_{n}" for n in ("Wr", "br", "W1", "b1", "g1", "be1", "m1", "v1", "W2", "b2", "g2", "be2", "m2",
                             "v2", "Wo", "bo")]
_PADDED = {"x": (NP, 0), "node_type_4": (NP, 0), "src": (EP, 0), "edge_type_3": (EP, 0), "dst": (EP, BLK * P - 1)}


def kernel(**inputs):
    import concourse.bacc as bacc
    from concourse.bass_utils import run_bass_kernel_spmd

    nc = bacc.Bacc("TRN2", target_bir_lowering=False, num_devices=1)
    arrays, tensors = {}, {}
    for name in _NAMES:
        a = np.ascontiguousarray(inputs[name])
        if name in _PADDED:
            rows, fill = _PADDED[name]
            a = np.concatenate([a, np.full((rows - a.shape[0],) + a.shape[1:], fill, a.dtype)])
        arrays[f"in_{name}"] = a
        tensors[name] = nc.dram_tensor(f"in_{name}", a.shape, mybir.dt.from_np(a.dtype), kind="ExternalInput").ap()
    tensors["out"] = nc.dram_tensor("out", (NP, D), F32, kind="ExternalOutput").ap()
    build(nc, tensors)
    result = run_bass_kernel_spmd(nc, [arrays], core_ids=[0])
    return result.results[0]["out"][:N]
```

```python
from contextlib import ExitStack, contextmanager

import numpy as np

import concourse.bass as bass
from concourse import mybir

ALU = mybir.AluOpType
ACT = mybir.ActivationFunctionType
F32 = mybir.dt.float32
BF16 = mybir.dt.bfloat16
I32 = mybir.dt.int32
AX = mybir.AxisListType.X

P = 128
N, E, D = 6250, 100000, 256
L, H, HD, TN, TE = 3, 8, 32, 4, 3
FF = 4 * D
NX, HE = 8, 256
MH, MD = 4, 64
CH = 512
NCH = -(-N // CH)
NB = CH // P
NP = NCH * CH
BLK = -(-N // P)
TILES = 784
EP = TILES * P
V = TILES + BLK - 1
VP = 104
VJ = V // VP
SC = 16
VK = V // SC
CL = VK * P
RW = H * (HD + 1)
GV = 16
GH = GV // 4
NG = V // GV
BIG = 1.0e30
assert VJ * VP == V and SC * VK == V and NG * GV == V and TILES % 112 == 0 and EP >= E
TJ = TILES // 112


def ds(start, size):
    return bass.ds(start, size)


@contextmanager
def stage(nc, name, names, pool_dmas=False):
    with ExitStack() as ctx:
        s = {n: ctx.enter_context(nc.semaphore(f"{name}_{n}")) for n in names.split()}
        with nc.Block() as block:
            yield block, s
        with nc.Block() as clear:
            if pool_dmas:
                @clear.gpsimd
                def _(pool):
                    pool.dma_reset()
                    for x in s.values():
                        pool.sem_clear(x)
            else:
                @clear.sync
                def _(sp):
                    for x in s.values():
                        sp.sem_clear(x)


class Arena:

    def __init__(self, tensor, words):
        self.tensor, self.words, self.at = tensor, words, 0

    def take(self, shape, dtype=F32, parts=P):
        size = int(np.prod(shape))
        words = size if dtype != BF16 else -(-size // 2)
        words = -(-words // 8) * 8
        ap = self.tensor[0:parts, self.at:self.at + words]
        self.at += words
        assert self.at <= self.words, (self.at, self.words)
        if dtype != F32:
            ap = ap.bitcast(dtype)
        ap = ap[:, 0:size]
        if len(shape) == 2:
            ap = ap.rearrange("p (a b) -> p a b", a=shape[0])
        elif len(shape) == 3:
            ap = ap.rearrange("p (a b c) -> p a b c", a=shape[0], b=shape[1])
        return ap


def spread(dram, offset, *dims):
    return bass.AP(tensor=dram.tensor, offset=offset, ap=[list(d) for d in dims])


def all_queries(k):
    size = NP // P * D
    return k.arena[:, k.words - size:k.words].rearrange("p (b d) -> p b d", d=D)


def all_sums(k):
    return k.arena[:, 0:NP // P * RW].rearrange("p (b n) -> p b n", n=RW)


def along(ap, axis, count):
    ap = ap.unsqueeze(axis)
    shape = list(ap.shape)
    shape[axis] = count
    return ap.broadcast_to(shape)


def build_constants(nc, k):
    with stage(nc, "const", "filled made") as (block, s):
        @block.gpsimd
        def _(pool):
            pool.memset(k.idx_key[:, V:], 0)
            pool.memset(k.idx_value[:, V:], 0)
            pool.memset(k.ident[:, :], 0.0).then_inc(s["filled"], 1)
            pool.wait_ge(s["filled"], 1)
            pool.affine_select(out=k.ident[:, :], in_=k.ident[:, :], compare_op=ALU.not_equal, fill=1.0, base=0,
                               pattern=[[-1, P]], channel_multiplier=1)
            pool.iota(k.iota_row[:, :], pattern=[[1, P]], base=0, channel_multiplier=0,
                      allow_small_or_imprecise_dtypes=True)
            pool.iota(k.iota_col[:, :], pattern=[[0, 1]], base=0, channel_multiplier=1,
                      allow_small_or_imprecise_dtypes=True).then_inc(s["made"], 1)


def build_visits(nc, k, src, dst, edge_type, node_type, dram):
    a = Arena(k.arena, k.words)
    T = 112
    src_t, dst_t, et_t = (a.take([TJ * P], I32) for _ in range(3))
    comb = a.take([TJ, 3, P])
    last_i, blk_i = a.take([TJ], I32), a.take([TJ], I32)
    blk_f, tile_no, reach = a.take([TJ]), a.take([TJ]), a.take([TJ])
    reach_all, below = a.take([TILES]), a.take([TILES])
    visit_no, tile_of, block_of, block_off = (a.take([VJ]) for _ in range(4))
    tile_idx, block_i = a.take([VJ], I32), a.take([VJ], I32)
    got = a.take([VJ, 3 * P])
    keyrel, key, over = a.take([VJ, P]), a.take([VJ, P]), a.take([VJ, P])
    keyrel_b = a.take([VJ, P], BF16)
    types_i, types = a.take([NCH * NB], I32), a.take([NCH * NB])
    with stage(nc, "tiles", "edges comb_last made comb_made reach stored_comb stored_reach types shifted typed") as (block, s):
        @block.sync
        def _(sp):
            for to, of in ((src_t, src), (dst_t, dst), (et_t, edge_type)):
                sp.dma_start(to[0:T, :], of.rearrange("(p f) -> p f", p=T)).then_inc(s["edges"], 16)
            with nc.allow_non_contiguous_dma(reason="once, a word per node"):
                sp.dma_start(types_i, node_type.rearrange("(b p) -> p b", p=P)).then_inc(s["types"], 16)
            sp.wait_ge(s["comb_made"], 1)
            sp.dma_start(dram.comb.rearrange("(p j) f -> p (j f)", p=T),
                         comb[0:T].rearrange("p a b c -> p (a b c)")).then_inc(s["stored_comb"], 16)
            sp.wait_ge(s["reach"], 1)
            sp.dma_start(dram.reach.rearrange("(p j) -> p j", p=T), reach[0:T]).then_inc(s["stored_reach"], 16)
            sp.wait_ge(s["stored_comb"], 16)
            sp.wait_ge(s["stored_reach"], 16)

        @block.gpsimd
        def _(pool):
            pool.iota(tile_no[0:T], pattern=[[1, TJ]], base=0, channel_multiplier=TJ,
                      allow_small_or_imprecise_dtypes=True).then_inc(s["made"], 1)
            pool.iota(visit_no[0:VP], pattern=[[VP, VJ]], base=0, channel_multiplier=1,
                      allow_small_or_imprecise_dtypes=True).then_inc(s["made"], 1)

        @block.vector
        def _(dve):
            dve.wait_ge(s["edges"], 48)
            three = [x[0:T].rearrange("p (j f) -> p j f", j=TJ) for x in (src_t, dst_t, et_t)]
            dve.scalar_tensor_tensor(comb[0:T, :, 0, :], three[0], float(TE), three[2], ALU.mult, ALU.add)
            dve.tensor_copy(comb[0:T, :, 1, :], three[0])
            dve.tensor_copy(comb[0:T, :, 2, :], three[1]).then_inc(s["comb_made"], 1)
            dve.tensor_copy(last_i[0:T], three[1][:, :, P - 1]).then_inc(s["comb_last"], 1)
            dve.wait_ge(s["comb_last"], 1)
            dve.tensor_scalar(blk_i[0:T], last_i[0:T], 7, None, ALU.arith_shift_right).then_inc(s["shifted"], 1)
            dve.wait_ge(s["shifted"], 1)
            dve.tensor_copy(blk_f[0:T], blk_i[0:T]).then_inc(s["shifted"], 1)
            dve.wait_ge(s["shifted"], 2)
            dve.wait_ge(s["made"], 2)
            dve.tensor_tensor(reach[0:T], blk_f[0:T], tile_no[0:T], ALU.add).then_inc(s["reach"], 1)
            dve.wait_ge(s["types"], 16)
            dve.tensor_copy(types, types_i).then_inc(s["typed"], 1)
            dve.wait_ge(s["typed"], 1)
            for t in range(TN):
                dve.tensor_scalar(k.onehot[:, :, t], types, float(t), None, ALU.is_equal)

    with stage(nc, "visits", "reach below count index got rel m1 m2 stored tile off turned copied last", True) as (block, s):
        @block.sync
        def _(sp):
            sp.dma_start(reach_all[0:VP], dram.reach.partition_broadcast(VP)).then_inc(s["reach"], 16)
            sp.wait_ge(s["last"], 1)
            sp.dma_start(dram.keyrow.rearrange("(j p) s -> p j s", p=VP), keyrel_b[0:VP]).then_inc(s["stored"], 16)
            sp.dma_start(dram.key.rearrange("(j p s) -> p j s", p=VP, j=VJ), key[0:VP]).then_inc(s["stored"], 16)
            with nc.allow_non_contiguous_dma(reason="once, a word per visit"):
                sp.dma_start(dram.blocks_i.rearrange("(j p) -> p j", p=VP), block_i[0:VP]).then_inc(s["stored"], 16)
                sp.dma_start(dram.blocks_f.rearrange("(j p) -> p j", p=VP), block_of[0:VP]).then_inc(s["stored"], 16)
            sp.wait_ge(s["stored"], 64)

        @block.vector
        def _(dve):
            dve.wait_ge(s["reach"], 16)
            for j in range(VJ):
                if j:
                    dve.wait_ge(s["count"], j)
                dve.tensor_scalar(below[0:VP], reach_all[0:VP], visit_no[0:VP, j:j + 1], None,
                                  ALU.is_lt).then_inc(s["below"], 1)
                dve.wait_ge(s["below"], j + 1)
                dve.tensor_reduce(tile_of[0:VP, j:j + 1], below[0:VP], AX, ALU.add).then_inc(s["count"], 1)
            dve.wait_ge(s["count"], VJ)
            dve.tensor_copy(tile_idx[0:VP], tile_of[0:VP]).then_inc(s["index"], 1)
            dve.tensor_tensor(block_of[0:VP], visit_no[0:VP], tile_of[0:VP], ALU.subtract).then_inc(s["tile"], 1)
            dve.wait_ge(s["tile"], 1)
            dve.tensor_copy(block_i[0:VP], block_of[0:VP])
            dve.tensor_scalar(block_off[0:VP], block_of[0:VP], -float(P), None, ALU.mult).then_inc(s["off"], 1)
            dve.wait_ge(s["off"], 1)
            dve.wait_ge(s["got"], 16 * VJ)
            dst_v = got[0:VP, :, 2 * P:3 * P]
            dve.tensor_tensor(keyrel[0:VP], dst_v, along(block_off[0:VP], 2, P), ALU.add).then_inc(s["rel"], 1)
            dve.wait_ge(s["rel"], 1)
            dve.tensor_copy(keyrel_b[0:VP], keyrel[0:VP])
            dve.tensor_scalar(over[0:VP], keyrel[0:VP], 0.0, 8192.0, ALU.is_lt, ALU.mult).then_inc(s["m1"], 1)
            dve.wait_ge(s["m1"], 1)
            dve.tensor_tensor(key[0:VP], dst_v, over[0:VP], ALU.add).then_inc(s["m2"], 1)
            dve.wait_ge(s["m2"], 1)
            dve.tensor_scalar(over[0:VP], keyrel[0:VP], P - 0.5, 8192.0, ALU.is_gt, ALU.mult).then_inc(s["m1"], 1)
            dve.wait_ge(s["m1"], 2)
            dve.tensor_tensor(key[0:VP], key[0:VP], over[0:VP], ALU.add).then_inc(s["last"], 1)
            for n, to in enumerate((k.idx_key, k.idx_value, k.keycol)):
                for half in range(2):
                    dve.wait_ge(s["turned"], 2 * n + half + 1)
                    dve.tensor_copy(to[:, half * 4 * VP:(half + 1) * 4 * VP],
                                    k.psum[:, 2 * n + half, 0:4 * VP]).then_inc(s["copied"], 1)

        @block.gpsimd
        def _(pool):
            pool.wait_ge(s["index"], 1)
            for j in range(VJ):
                pool.indirect_dma_start(out=got[0:VP, j, :], out_offset=None, in_=dram.comb,
                                        in_offset=bass.IndirectOffsetOnAxis(ap=tile_idx[0:VP, j:j + 1], axis=0)
                                        ).then_inc(s["got"], 16)

        @block.tensor
        def _(pe):
            pe.wait_ge(s["got"], 16 * VJ)
            pe.wait_ge(s["rel"], 1)
            for n in range(3):
                for half in range(2):
                    for q in range(4):
                        j = half * 4 + q
                        of = got[0:VP, j, n * P:(n + 1) * P] if n < 2 else keyrel[0:VP, j, :]
                        t = pe.transpose(k.psum[:, 2 * n + half, q * VP:(q + 1) * VP], of, k.ident[0:VP, 0:VP])
                    t.then_inc(s["turned"], 1)

    a = Arena(k.arena, k.words)
    blocks_all = a.take([V])
    key_run = a.take([CL + 2])
    differ = a.take([CL + 1], BF16)
    edge_f, edge_b = a.take([1]), a.take([1])
    with stage(nc, "runs", "blocks keys filled differ pen edges stored loaded") as (block, s):
        @block.sync
        def _(sp):
            sp.dma_start(blocks_all, dram.blocks_f.partition_broadcast(P)).then_inc(s["blocks"], 16)
            sp.dma_start(k.block_row[0:1, :], dram.blocks_i.unsqueeze(0)).then_inc(s["loaded"], 16)
            sp.wait_ge(s["filled"], 1)
            sp.dma_start(key_run[:, 1:CL + 1], spread(dram.key, 0, [CL, SC], [0, H], [1, CL])).then_inc(s["keys"], 16)
            with nc.allow_non_contiguous_dma(reason="once, a word per partition"):
                sp.dma_start(key_run[H:P, 0:1], spread(dram.key, CL - 1, [CL, SC - 1], [0, H], [1, 1])).then_inc(s["keys"], 16)
                sp.dma_start(key_run[0:P - H, CL + 1:CL + 2],
                             spread(dram.key, CL, [CL, SC - 1], [0, H], [1, 1])).then_inc(s["keys"], 16)
                sp.wait_ge(s["edges"], 2)
                sp.dma_start(dram.edge_f, edge_f[:, 0]).then_inc(s["stored"], 16)
                sp.dma_start(dram.edge_b, edge_b[:, 0]).then_inc(s["stored"], 16)
                sp.wait_ge(s["stored"], 32)
                sp.dma_start(k.edge_f8[0:H, :], dram.edge_f.rearrange("(c h) -> h c", h=H)).then_inc(s["loaded"], 16)
                sp.dma_start(k.edge_b8[0:H, :], dram.edge_b.rearrange("(c h) -> h c", h=H)).then_inc(s["loaded"], 16)
            sp.wait_ge(s["loaded"], 48)

        @block.vector
        def _(dve):
            dve.memset(key_run[:, 0:CL + 2:CL + 1], -1.0).then_inc(s["filled"], 1)
            dve.wait_ge(s["blocks"], 16)
            dve.memset(k.same_block[:, 0:1], 0.0)
            dve.tensor_tensor(k.same_block[:, 1:V], blocks_all[:, 1:V], blocks_all[:, 0:V - 1], ALU.is_equal)
            dve.wait_ge(s["keys"], 48)
            dve.wait_ge(s["filled"], 1)
            dve.tensor_tensor(differ, key_run[:, 0:CL + 1], key_run[:, 1:CL + 2], ALU.not_equal).then_inc(s["differ"], 1)
            dve.wait_ge(s["differ"], 1)
            dve.tensor_scalar(k.breaks[:, 0:CL + 1], differ, -BIG, None, ALU.mult).then_inc(s["pen"], 1)
            dve.wait_ge(s["pen"], 1)
            dve.tensor_reduce(edge_f, k.breaks[:, 0:CL], AX, ALU.min).then_inc(s["edges"], 1)
            dve.tensor_reduce(edge_b, k.breaks[:, 1:CL + 1], AX, ALU.min).then_inc(s["edges"], 1)


def passed(eng, s, sem, value, counter="passed"):
    eng.wait_ge(sem, value)
    eng.sem_inc(s[counter], 1)


def norm_moments(dve, s, tag, n, x, stats, moments):
    for q in range(NB):
        ins = dve.bn_stats(stats[:, q, :], x[:, q, :])
    ins.then_inc(s[f"{tag}_stats"], 1)
    passed(dve, s, s[f"{tag}_stats"], n)
    for q in range(NB):
        ins = dve.bn_aggr(moments[:, q, :], stats[:, q, :])
    ins.then_inc(s[f"{tag}_moments"], 1)


def norm_rows(dve, s, tag, n, x, out, moments, rstd, scale=None, shift=None):
    dve.wait_ge(s[f"{tag}_rstd"], n)
    for q in range(NB):
        ins = dve.tensor_scalar(out[:, q, :], x[:, q, :], moments[:, q, 0:1], rstd[:, q:q + 1],
                                ALU.subtract, ALU.mult)
    ins.then_inc(s[f"{tag}_unit"], 1)
    if scale is not None:
        dve.wait_ge(s[f"{tag}_unit"], n)
        dve.tensor_tensor(out, out, along(scale, 1, NB), ALU.mult).then_inc(s[f"{tag}_scaled"], 1)
        dve.wait_ge(s[f"{tag}_scaled"], n)
        dve.tensor_tensor(out, out, along(shift, 1, NB), ALU.add).then_inc(s[f"{tag}_shifted"], 1)


def normalize(dve, s, tag, n, x, out, stats, moments, rstd, scale=None, shift=None):
    norm_moments(dve, s, tag, n, x, stats, moments)
    norm_rows(dve, s, tag, n, x, out, moments, rstd, scale, shift)


def inverse_root(pool, s, tag, n, moments, rstd, eps, minus_half):
    step = lambda name: s[f"{tag}_{name}"]
    pool.wait_ge(step("moments"), n)
    pool.tensor_tensor(rstd, moments[:, :, 1], eps, ALU.add).then_inc(step("eps"), 1)
    pool.wait_ge(step("eps"), n)
    pool.tensor_tensor(rstd, rstd, minus_half, ALU.pow).then_inc(step("rstd"), 1)


def norm_sems(tag):
    return " ".join(f"{tag}_{n}" for n in ("stats", "moments", "eps", "rstd", "unit", "scaled", "shifted"))


def in_slots(eng, count, step):
    with eng.Fori(0, (count - 2) // 2) as i:
        for b in range(2):
            step(2 * i + b, b, i, True, True)
    for n in range((count - 2) // 2 * 2, count):
        step(n, n % 2, n // 2, n + 1 < count, n + 2 < count)


def blocks_in(c):
    return BLK - (NCH - 1) * NB if isinstance(c, int) and c == NCH - 1 else NB


def chunk_rows(dram, c):
    return dram[ds(c * CH, CH), :].rearrange("(q p) d -> p q d", p=P)


def build_input_norm(nc, k, x, dram):
    a = Arena(k.arena, k.words)
    rows = a.take([NP // P, D])
    unit, stats, moments, rstd = ([a.take(shape) for _ in range(2)] for shape in ([NB, D], [NB, 6], [NB, 2], [NB]))
    eps, minus_half = a.take([NB]), a.take([NB])
    with stage(nc, "innorm", "loaded stored0 stored1 consts passed " + norm_sems("ln")) as (block, s):
        s_stored = [s["stored0"], s["stored1"]]

        @block.sync
        def _(sp):
            sp.dma_start(rows, x.rearrange("(b p) d -> p b d", p=P)).then_inc(s["loaded"], 16)

        @block.gpsimd
        def _(pool):
            pool.memset(eps, 1e-5)
            pool.memset(minus_half, -0.5).then_inc(s["consts"], 1)
            pool.wait_ge(s["consts"], 1)
            in_slots(pool, NCH, lambda c, b, i, one, two:
                     inverse_root(pool, s, "ln", c + 1, moments[b], rstd[b], eps, minus_half))

        @block.vector
        def _(dve):
            def chunk(c):
                return rows[:, ds(c * NB, NB), :]

            def measure(c, b):
                norm_moments(dve, s, "ln", c + 1, chunk(c), stats[b], moments[b])

            def step(c, b, i, one, two):
                if one:
                    measure(c + 1, 1 - b)
                dve.wait_ge(s_stored[b], 32 * i)
                norm_rows(dve, s, "ln", c + 1, chunk(c), unit[b], moments[b], rstd[b])

            dve.wait_ge(s["loaded"], 16)
            measure(0, 0)
            in_slots(dve, NCH, step)

        @block.scalar
        def _(act):
            def step(c, b, i, one, two):
                act.wait_ge(s["ln_unit"], c + 1)
                act.dma_start(chunk_rows(dram.xn, c), unit[b]).then_inc(s_stored[b], 16)
                act.dma_start(chunk_rows(dram.state, c), unit[b]).then_inc(s_stored[b], 16)

            in_slots(act, NCH, step)
            for b in range(2):
                act.wait_ge(s_stored[b], 32 * ((NCH + 1 - b) // 2))


def build_type_weights(nc, k, w, layer, weights):
    a = Arena(k.arena, k.words)
    a.take([H, 5 * HD])
    wk = a.take([H, HD])
    we = a.take([H, TE, HD], parts=HD)
    wkT = a.take([H, P], parts=HD)
    mu = a.take([H * TE])
    with stage(nc, "typew", "loaded turned copied merged") as (block, s):
        @block.sync
        def _(sp):
            for t in range(TN):
                part = slice(t * HD, (t + 1) * HD)
                for of, to in ((w["W_Q"], weights[part, :, 0:HD]), (w["W_V"], weights[part, :, HD:2 * HD]),
                               (w["W_K"], wk[part])):
                    sp.dma_start(to, of[ds(layer, 1), t].rearrange("a h d e -> (a d) h e")).then_inc(s["loaded"], 16)

        @block.scalar
        def _(act):
            for e in range(TE):
                act.dma_start(we[:, :, e, :],
                              w["W_E"][ds(layer, 1), e].rearrange("a h d e -> (a d) h e")).then_inc(s["loaded"], 16)
            act.dma_start(mu, w["mu"][ds(layer, 1)].rearrange("a h t -> (a h t)").partition_broadcast(P)
                          ).then_inc(s["loaded"], 16)

        @block.tensor
        def _(pe):
            pe.wait_ge(s["loaded"], 16 * (3 * TN + TE + 1))
            for h in range(H):
                t = pe.transpose(k.psum[0:HD, h // 4, (h % 4) * P:(h % 4 + 1) * P], wk[:, h, :], k.ident[:, :])
            t.then_inc(s["turned"], 1)
            pe.wait_ge(s["copied"], 1)
            for h in range(H):
                t = pe.matmul(k.psum[:, 2 + h // 4, (h % 4) * P:(h % 4) * P + TE * HD], wkT[:, h, :],
                              we[:, h, :, :].rearrange("p a b -> p (a b)"), start=True, stop=True)
            t.then_inc(s["merged"], 1)

        @block.vector
        def _(dve):
            dve.wait_ge(s["turned"], 1)
            dve.tensor_copy(wkT, k.psum[0:HD, 0:2, :].rearrange("p b (h n) -> p (b h) n", n=P)).then_inc(s["copied"], 1)
            dve.wait_ge(s["merged"], 1)
            dve.wait_ge(s["loaded"], 16 * (3 * TN + TE + 1))
            for h in range(H):
                dve.scalar_tensor_tensor(
                    weights[:, h, 2 * HD:5 * HD].rearrange("p (t f) -> p t f", t=TE),
                    k.psum[:, 2 + h // 4, (h % 4) * P:(h % 4) * P + TE * HD].rearrange("p (t f) -> p t f", t=TE),
                    float(HD) ** -0.5, along(mu[:, h * TE:(h + 1) * TE], 2, HD), ALU.mult, ALU.mult)


def build_rows(nc, k, weights, dram):
    a = Arena(k.arena, k.words)
    a.take([H, 5 * HD])
    x = [a.take([D]) for _ in range(2)]
    placed = [a.take([H, TN * HD]) for _ in range(2)]
    placedT = [a.take([H, P]) for _ in range(2)]
    queries = all_queries(k)
    v_row = [a.take([H, HD + 1]) for _ in range(2)]
    k_row = [a.take([TE * D]) for _ in range(2)]
    names = "x0 x1 placed turned copied multiplied evac_lo evac_hi stored_v0 stored_v1 stored_k0 stored_k1 passed copying ones"
    with stage(nc, "rows", names, True) as (block, s):
        s_x, s_v, s_k = [s["x0"], s["x1"]], [s["stored_v0"], s["stored_v1"]], [s["stored_k0"], s["stored_k1"]]

        def move(copy, n, b, j):
            heads = min(3, H - 3 * j)
            part = slice(3 * j * HD, (3 * j + heads) * HD)
            out = k.psum[:, 2 + 3 * b + j, 0:heads * 5 * HD].rearrange("p (h g d) -> p h g d", h=heads, g=5)
            copy(queries[:, ds(n, 1), part].rearrange("p a (h d) -> p (a h) d", d=HD), out[:, :, 0])
            copy(v_row[b][:, 3 * j:3 * j + heads, 0:HD], out[:, :, 1])
            return copy(k_row[b].rearrange("p (e c) -> p e c", e=TE)[:, :, part].rearrange("p e (h d) -> p e h d", d=HD),
                        out[:, :, 2:5].rearrange("p h e d -> p e h d"))

        @block.sync
        def _(sp):
            def step(n, b, i, one, two):
                sp.wait_ge(s["evac_lo"], n + 3)
                sp.wait_ge(s["evac_hi"], n + 3)
                sp.dma_start(dram.key_rows[ds(n * P * TE, P * TE), :].rearrange("(p e) d -> p (e d)", e=TE),
                             k_row[b]).then_inc(s_k[b], 16)
                sp.dma_start(dram.value_rows[ds(n * P, P), :],
                             v_row[b].rearrange("p h d -> p (h d)")).then_inc(s_v[b], 16)

            sp.sem_inc(s["evac_lo"], 2)
            sp.sem_inc(s["evac_hi"], 2)
            sp.wait_ge(s["ones"], 2)
            in_slots(sp, BLK, step)
            for b in range(2):
                sp.wait_ge(s_k[b], 16 * ((BLK + 1 - b) // 2))
                sp.wait_ge(s_v[b], 16 * ((BLK + 1 - b) // 2))

        @block.gpsimd
        def _(pool):
            def load(n, b):
                pool.dma_start(x[b], dram.state[ds(n * P, P), :]).then_inc(s_x[b], 16)

            def step(n, b, i, one, two):
                if two:
                    passed(pool, s, s["placed"], n + 1)
                    load(n + 2, b)

            load(0, 0)
            load(1, 1)
            in_slots(pool, BLK, step)
            for b in range(2):
                pool.wait_ge(s_x[b], 16 * ((BLK + 1 - b) // 2))

        @block.vector
        def _(dve):
            def place(n, b, i):
                dve.wait_ge(s_x[b], 16 * i + 16)
                dve.tensor_tensor(
                    placed[b].rearrange("p h (t d) -> p h t d", t=TN),
                    along(x[b].rearrange("p (h d) -> p h d", h=H), 2, TN),
                    along(along(k.onehot[:, ds(n, 1), :].rearrange("p a t -> p (a t)"), 1, H), 3, HD),
                    ALU.mult).then_inc(s["placed"], 1)

            def step(n, b, i, one, two):
                if two:
                    dve.wait_ge(s["turned"], n + 1)
                    place(n + 2, b, i + 1)
                dve.wait_ge(s["multiplied"], n + 1)
                dve.wait_ge(s_v[b], 16 * i)
                dve.wait_ge(s_k[b], 16 * i)
                move(dve.tensor_copy, n, b, 1).then_inc(s["evac_hi"], 1)

            for b in range(2):
                dve.memset(v_row[b][:, :, HD:HD + 1], 1.0).then_inc(s["ones"], 1)
            place(0, 0, 0)
            place(1, 1, 0)
            in_slots(dve, BLK, step)

        @block.scalar
        def _(act):
            def copy(n, b):
                act.wait_ge(s["turned"], n + 1)
                act.copy(placedT[b].rearrange("p h n -> p (h n)"),
                         k.psum[:, 0:2, :].rearrange("p a b -> p (a b)")).then_inc(s["copied"], 1)

            def step(n, b, i, one, two):
                if one:
                    act.wait_ge(s["multiplied"], n)
                    copy(n + 1, 1 - b)
                act.wait_ge(s_k[b], 16 * i)
                act.wait_ge(s_v[b], 16 * i)
                passed(act, s, s["multiplied"], n + 1, "copying")
                move(act.copy, n, b, 0)
                move(act.copy, n, b, 2).then_inc(s["evac_lo"], 1)

            copy(0, 0)
            in_slots(act, BLK, step)

        @block.tensor
        def _(pe):
            def turn(n, b):
                pe.wait_ge(s["placed"], n + 1)
                for h in range(H):
                    t = pe.transpose(k.psum[:, h // 4, (h % 4) * P:(h % 4 + 1) * P], placed[b][:, h, :],
                                     k.ident[:, :])
                t.then_inc(s["turned"], 1)

            def step(n, b, i, one, two):
                pe.wait_ge(s["copied"], n + 1)
                if one:
                    turn(n + 1, 1 - b)
                pe.wait_ge(s["evac_lo"], n + 1)
                pe.wait_ge(s["evac_hi"], n + 1)
                for h in range(H):
                    t = pe.matmul(k.psum[:, 2 + 3 * b + h // 3, (h % 3) * 5 * HD:(h % 3 + 1) * 5 * HD],
                                  placedT[b][:, h, :], weights[:, h, :], start=True, stop=True)
                t.then_inc(s["multiplied"], 1)

            turn(0, 0)
            in_slots(pe, BLK, step)


def place_indices(eng, s, slot, idx, n):
    eng.tensor_copy(slot, idx[:, ds(n * 4, 4)]).then_inc(s["indexed"], 1)


def build_scores(nc, k, dram):
    a = Arena(k.arena, k.words)
    key_ring = a.take([GV, D])
    query_ring = a.take([GV, D])
    cols = [a.take([4 * P], BF16) for _ in range(2)]
    pick = [a.take([4, P]) for _ in range(2)]
    prod = [a.take([4 * H, HD]) for _ in range(2)]
    index = [a.take([4], I32) for _ in range(GH)]
    queries = all_queries(k)
    names = "picked spread multiplied scored indexed passed copying queried cols0 cols1 " + \
        " ".join(f"key{q}" for q in range(GV))
    with stage(nc, "scores", names, True) as (block, s):
        s_key = [s[f"key{q}"] for q in range(GV)]
        s_cols = [s["cols0"], s["cols1"]]

        @block.sync
        def _(sp):
            sp.sem_inc(s["picked"], 2)
            for sem in (s["spread"], s["multiplied"], s["scored"]):
                sp.sem_inc(sem, GH)
            with sp.Fori(0, NG) as i:
                for h in range(GH):
                    n = i * GH + h
                    sp.wait_ge(s["picked"], n + 1)
                    sp.dma_start(cols[h % 2], dram.keyrow[ds(n * 4, 4), :].rearrange("v s -> (v s)")
                                 .partition_broadcast(P)).then_inc(s_cols[h % 2], 16)

        @block.scalar
        def _(act):
            with act.Fori(0, NG) as i:
                for h in range(GH):
                    n = i * GH + h
                    _, blocks = nc.values_load_multi_w_load_instructions(
                        k.block_row[0:1, ds(n * 4, 4)], engines=(mybir.EngineType.Activation,),
                        min_val=0, max_val=BLK - 1)
                    passed(act, s, s["spread"], n + 1, "copying")
                    for q in range(4):
                        t = act.copy(query_ring[:, 4 * h + q, :],
                                     queries[:, ds(blocks[q], 1), :].rearrange("p a d -> p (a d)"))
                    t.then_inc(s["queried"], 1)

        @block.gpsimd
        def _(pool):
            with pool.Fori(0, NG) as i:
                for h in range(GH):
                    n = i * GH + h
                    pool.wait_ge(s["indexed"], n + 1)
                    passed(pool, s, s["multiplied"], n + 1)
                    for q in range(4):
                        pool.indirect_dma_start(
                            out=key_ring[:, 4 * h + q, :], out_offset=None, in_=dram.key_rows,
                            in_offset=bass.IndirectOffsetOnAxis(ap=index[h][:, q:q + 1], axis=0)
                        ).then_inc(s_key[4 * h + q], 16)

        @block.tensor
        def _(pe):
            with pe.Fori(0, NG) as i:
                for h in range(GH):
                    n = i * GH + h
                    pe.wait_ge(s["picked"], n + 3)
                    pe.wait_ge(s["multiplied"], n + GH - 1)
                    pe.wait_ge(s["queried"], n + 1)
                    for q in range(4):
                        t = pe.matmul(k.psum[:, 2 * (h % 2) + q // 2, (q % 2) * D:(q % 2 + 1) * D],
                                      pick[h % 2][:, q, :], query_ring[:, 4 * h + q, :], start=True, stop=True)
                    t.then_inc(s["spread"], 1)

        @block.vector
        def _(dve):
            def choose(i, h):
                n = i * GH + h
                dve.wait_ge(s_cols[h % 2], (i * GH + h - h % 2) * 8 + 16)
                dve.wait_ge(s["spread"], n + GH - 1)
                dve.tensor_scalar(pick[h % 2].rearrange("p v s -> p (v s)"), cols[h % 2], k.iota_col[:, 0:1], None,
                                  ALU.is_equal).then_inc(s["picked"], 1)

            def multiply(i, h):
                n = i * GH + h
                dve.wait_ge(s["spread"], n + GH + 1)
                dve.wait_ge(s["scored"], n + GH - 1)
                for q in range(4):
                    dve.wait_ge(s_key[4 * h + q], 16 * i + 16)
                place_indices(dve, s, index[h], k.idx_key, n + GH)
                b = 2 * (h % 2)
                dve.tensor_tensor(prod[h % 2].rearrange("p a d -> p (a d)"),
                                  k.psum[:, b:b + 2, :].rearrange("p b n -> p (b n)"),
                                  key_ring[:, 4 * h:4 * h + 4, :].rearrange("p q d -> p (q d)"),
                                  ALU.mult).then_inc(s["multiplied"], 1)

            def reduce(i, h):
                n = i * GH + h
                passed(dve, s, s["multiplied"], n + GH + 1)
                dve.tensor_reduce(k.scores[:, ds(n * 4 * H, 4 * H)], prod[h % 2], AX,
                                  ALU.add).then_inc(s["scored"], 1)

            for h in range(GH):
                place_indices(dve, s, index[h], k.idx_key, h)
            with dve.Fori(0, NG) as i:
                choose(i, 0)
                for h in range(GH):
                    if h + 1 < GH:
                        choose(i, h + 1)
                    multiply(i, h)
                    if h:
                        reduce(i, h - 1)
                reduce(i, GH - 1)


def build_softmax(nc, k, dram):
    a = Arena(k.arena, k.words)
    initial = a.take([4])
    state8, last8 = a.take([2, SC]), a.take([2, SC])
    forward, backward = a.take([CL]), k.stream[:, 0:CL]
    by_visit = k.scores[:, :].rearrange("p (c k h) -> p k c h", c=SC, k=VK)
    with stage(nc, "toscan", "ordered turned copied") as (block, s):
        @block.vector
        def _(dve):
            for g in range(VK // 4):
                dve.tensor_copy(k.stream[:, g * 512:(g + 1) * 512].rearrange("p (k c h) -> p k c h", k=4, c=SC),
                                by_visit[:, 4 * g:4 * g + 4]).then_inc(s["ordered"], 1)

        @block.tensor
        def _(pe):
            for g in range(VK // 4):
                pe.wait_ge(s["ordered"], g + 1)
                if g >= 2:
                    pe.wait_ge(s["copied"], g - 1)
                for q in range(4):
                    t = pe.transpose(k.psum[:, g % 2, q * P:(q + 1) * P],
                                     k.stream[:, (4 * g + q) * P:(4 * g + q + 1) * P], k.ident[:, :])
                t.then_inc(s["turned"], 1)

        @block.scalar
        def _(act):
            act.wait_ge(s["ordered"], VK // 4)
            for g in range(VK // 4):
                act.wait_ge(s["turned"], g + 1)
                act.copy(k.scores[:, g * 512:(g + 1) * 512], k.psum[:, g % 2, :]).then_inc(s["copied"], 1)

    ways = [(k.breaks[:, 0:CL], k.edge_f8, CL - 1, False, forward),
            (k.breaks[:, 1:CL + 1], k.edge_b8, 0, True, backward)]
    groups = VK // 4
    with stage(nc, "scan", "initial scanned0 scanned1 stored back0 back1 chained sent0 sent1 loaded0 loaded1 forward "
               "backward larger less exp turned copied0 copied1") as (block, s):
        s_scanned, s_back = [s["scanned0"], s["scanned1"]], [s["back0"], s["back1"]]
        s_sent, s_loaded = [s["sent0"], s["sent1"]], [s["loaded0"], s["loaded1"]]
        s_maximum, s_copied = [s["forward"], s["backward"]], [s["copied0"], s["copied1"]]

        def copy_back(eng, copy, odd):
            eng.wait_ge(s["less"], groups)
            for g in range(odd, groups, 2):
                eng.wait_ge(s["turned"], g + 1)
                copy(k.scores[:, :].rearrange("p (c k h) -> p k c h", c=SC, k=VK)[:, 4 * g:4 * g + 4],
                     k.psum[:, g % 8, :].rearrange("p (k c h) -> p k c h", k=4, c=SC)).then_inc(s_copied[odd], 1)

        @block.vector
        def _(dve):
            def scan(n, first, done):
                breaks, _, _, turned, out = ways[n]
                turn = (lambda ap: ap[:, ::-1]) if turned else (lambda ap: ap)
                dve.tensor_tensor_scan(turn(out), turn(breaks), turn(k.scores[:, 0:CL]), initial[:, first:first + 1],
                                       ALU.add, ALU.max).then_inc(done, 1)

            def chain(n):
                _, edges, _, turned, _ = ways[n]
                turn = (lambda ap: ap[:, ::-1]) if turned else (lambda ap: ap)
                dve.wait_ge(s_back[n], 16)
                dve.tensor_tensor_scan(turn(state8[0:H, n]), turn(edges[0:H, :]), turn(last8[0:H, n]), -BIG,
                                       ALU.add, ALU.max).then_inc(s["chained"], 1)

            def subtract(g):
                part = slice(g * 4 * P, (g + 1) * 4 * P)
                dve.wait_ge(s["larger"], g + 1)
                dve.tensor_tensor(k.stream[:, part], k.stream[:, part], k.scores[:, part],
                                  ALU.subtract).then_inc(s["less"], 1)

            dve.memset(initial, -BIG).then_inc(s["initial"], 1)
            dve.wait_ge(s["initial"], 1)
            scan(0, 3, s_scanned[0])
            scan(1, 3, s_scanned[1])
            for n in range(2):
                chain(n)
            for n in range(2):
                dve.wait_ge(s_loaded[n], 16)
                dve.wait_ge(s["stored"], 32)
                scan(n, n, s_maximum[n])
            dve.wait_ge(s["forward"], 1)
            dve.wait_ge(s["backward"], 1)
            for g in range(groups):
                part = slice(g * 4 * P, (g + 1) * 4 * P)
                dve.scalar_tensor_tensor(k.stream[:, part], k.stream[:, part], -1.0e9, forward[:, part],
                                         ALU.max, ALU.max).then_inc(s["larger"], 1)
                if g:
                    subtract(g - 1)
            subtract(groups - 1)
            copy_back(dve, dve.tensor_copy, 1)

        @block.sync
        def _(sp):
            with nc.allow_non_contiguous_dma(reason="128 words"):
                for n in range(2):
                    end = ways[n][2]
                    sp.wait_ge(s_scanned[n], 1)
                    sp.dma_start(dram.carry[n], ways[n][4][:, end]).then_inc(s["stored"], 16)
                    sp.wait_ge(s["stored"], 16 * (n + 1))
                    sp.dma_start(last8[0:H, n], dram.carry[n].rearrange("(c h) -> h c", h=H)).then_inc(s_back[n], 16)
                for n in range(2):
                    sp.wait_ge(s["chained"], n + 1)
                    sp.dma_start(dram.carried[n].rearrange("(c h) -> h c", h=H), state8[0:H, n]).then_inc(s_sent[n], 16)
                for n in range(2):
                    sp.wait_ge(s_sent[n], 16)
                    to, of = (slice(0, P - H), slice(H, P)) if ways[n][3] else (slice(H, P), slice(0, P - H))
                    sp.dma_start(initial[to, n:n + 1], dram.carried[n, of].unsqueeze(1)).then_inc(s_loaded[n], 16)

        @block.scalar
        def _(act):
            for g in range(groups):
                part = slice(g * 4 * P, (g + 1) * 4 * P)
                act.wait_ge(s["less"], g + 1)
                act.activation(k.stream[:, part], k.stream[:, part], ACT.Exp, scale=-1.0).then_inc(s["exp"], 1)
            copy_back(act, act.copy, 0)

        @block.tensor
        def _(pe):
            for g in range(groups):
                pe.wait_ge(s["exp"], g + 1)
                if g >= 8:
                    pe.wait_ge(s_copied[g % 2], (g - 8) // 2 + 1)
                for q in range(4):
                    t = pe.transpose(k.psum[:, g % 8, q * P:(q + 1) * P],
                                     k.stream[:, (4 * g + q) * P:(4 * g + q + 1) * P], k.ident[:, :])
                t.then_inc(s["turned"], 1)


def tail_weights(k):
    a = Arena(k.stream, V * H)
    vec = {n: a.take([D]) for n in "bo ln1_g ln1_b b2 ln2_g ln2_b".split()}
    return vec, a.take([2, D]), a.take([2, FF]), a.take([FF // P, D]), a.take([FF // P])


def build_sums(nc, k, w, layer, dram):
    a = Arena(k.arena, k.words)
    a.take([NP // P, RW])
    kept = all_sums(k)
    values = a.take([GV, RW])
    pick = [a.take([4, P]) for _ in range(2)]
    weighed = [a.take([4, RW]) for _ in range(2)]
    sums = a.take([GV, RW])
    index = [a.take([4], I32) for _ in range(GH)]
    names = "picked weighed multiplied summed indexed passed copying kept cleared weights " + \
        " ".join(f"value{q}" for q in range(GV))
    with stage(nc, "sums", names, True) as (block, s):
        s_value = [s[f"value{q}"] for q in range(GV)]

        @block.sync
        def _(sp):
            for sem in (s["picked"], s["weighed"], s["multiplied"]):
                sp.sem_inc(sem, GH)
            sp.sem_inc(s["summed"], GV)
            sp.sem_inc(s["kept"], GV)
            vec, wo, w1, w2, b1 = tail_weights(k)
            lay = ds(layer, 1)
            for n, to in vec.items():
                sp.dma_start(to, w[n][lay, :].rearrange("a d -> (a d)").partition_broadcast(P)).then_inc(s["weights"], 16)
            sp.dma_start(wo, w["Wo"][lay].rearrange("a (f p) n -> (a p) f n", p=P)).then_inc(s["weights"], 16)
            sp.dma_start(w1, w["w1"][lay].rearrange("a (f p) n -> (a p) f n", p=P)).then_inc(s["weights"], 16)
            sp.dma_start(w2, w["w2"][lay].rearrange("a (f p) n -> (a p) f n", p=P)).then_inc(s["weights"], 16)
            with nc.allow_non_contiguous_dma(reason="once a layer"):
                sp.dma_start(b1, w["b1"][lay, :].rearrange("a (f p) -> (a p) f", p=P)).then_inc(s["weights"], 16)
            sp.wait_ge(s["weights"], 16 * (len(vec) + 4))

        @block.scalar
        def _(act):
            with act.Fori(0, NG) as i:
                for h in range(GH):
                    n = i * GH + h
                    _, blocks = nc.values_load_multi_w_load_instructions(
                        k.block_row[0:1, ds(n * 4, 4)], engines=(mybir.EngineType.Activation,),
                        min_val=0, max_val=BLK - 1)
                    act.wait_ge(s["summed"], n * 4 + 4 + GV)
                    for q in range(4):
                        passed(act, s, s["kept"], n * 4 + q + GV, "copying")
                        act.copy(kept[:, ds(blocks[q], 1), :].rearrange("p a n -> p (a n)"),
                                 sums[:, 4 * h + q, :]).then_inc(s["kept"], 1)

        @block.gpsimd
        def _(pool):
            with pool.Fori(0, NG) as i:
                for h in range(GH):
                    n = i * GH + h
                    pool.wait_ge(s["indexed"], n + 1)
                    passed(pool, s, s["weighed"], n + 1)
                    for q in range(4):
                        pool.indirect_dma_start(
                            out=values[:, 4 * h + q, :], out_offset=None, in_=dram.value_rows,
                            in_offset=bass.IndirectOffsetOnAxis(ap=index[h][:, q:q + 1], axis=0)
                        ).then_inc(s_value[4 * h + q], 16)

        @block.tensor
        def _(pe):
            with pe.Fori(0, NG) as i:
                for h in range(GH):
                    n = i * GH + h
                    pe.wait_ge(s["picked"], n + GH + 1)
                    pe.wait_ge(s["weighed"], n + GH + 1)
                    for q in range(4):
                        pe.wait_ge(s["summed"], n * 4 + q + 1 + GV - 8)
                        t = pe.matmul(k.psum[:, 4 * (h % 2) + q, 0:RW], pick[h % 2][:, q, :],
                                      weighed[h % 2][:, q, :], start=True, stop=True)
                    t.then_inc(s["multiplied"], 1)

        @block.vector
        def _(dve):
            dve.memset(kept[:, BLK:], 0.0)
            dve.memset(sums, 0.0).then_inc(s["cleared"], 1)
            dve.wait_ge(s["cleared"], 1)
            weights = k.scores[:, :].rearrange("p (v h) -> p v h", h=H)

            def choose(i, h):
                n = i * GH + h
                dve.wait_ge(s["multiplied"], n + GH - 1)
                dve.tensor_tensor(pick[h % 2], along(k.iota_row[:, :], 1, 4),
                                  along(k.keycol[:, ds(n * 4, 4)], 2, P), ALU.is_equal).then_inc(s["picked"], 1)

            def weigh(i, h, pair):
                n = i * GH + h
                for q in (pair, pair + 1):
                    dve.wait_ge(s_value[4 * h + q], 16 * i + 16)
                if pair:
                    place_indices(dve, s, index[h], k.idx_value, n + GH)
                ins = dve.tensor_tensor(
                    weighed[h % 2][:, pair:pair + 2].rearrange("p q (h d) -> p q h d", h=H),
                    values[:, 4 * h + pair:4 * h + pair + 2, :].rearrange("p q (h d) -> p q h d", h=H),
                    along(weights[:, ds(n * 4 + pair, 2), :], 3, HD + 1), ALU.mult)
                if pair:
                    ins.then_inc(s["weighed"], 1)

            def add(i, h, q):
                n = i * GH + h
                m = n * 4 + q
                if q == 0:
                    dve.wait_ge(s["multiplied"], n + GH + 1)
                    dve.wait_ge(s["kept"], n * 4 + 4)
                dve.wait_ge(s["summed"], m + GV)
                at = 4 * h + q
                dve.scalar_tensor_tensor(sums[:, at, :], sums[:, (at - 1) % GV, :], k.same_block[:, ds(m, 1)],
                                         k.psum[:, 4 * (h % 2) + q, 0:RW], ALU.mult, ALU.add).then_inc(s["summed"], 1)

            def turn(i, first=False, last=False):
                for h in range(GH):
                    ahead = (i, h + 1) if h + 1 < GH else (i + 1, 0)
                    back = (i, h - 1) if h else (i - 1, GH - 1)
                    more, had = not (last and h + 1 == GH), not (first and h == 0)
                    if more:
                        choose(*ahead)
                    if had:
                        add(*back, 0)
                    if more:
                        weigh(*ahead, 0)
                    if had:
                        add(*back, 1)
                    if more:
                        weigh(*ahead, 2)
                    if had:
                        add(*back, 2)
                        add(*back, 3)

            for h in range(GH):
                place_indices(dve, s, index[h], k.idx_value, h)
            choose(0, 0)
            weigh(0, 0, 0)
            weigh(0, 0, 2)
            turn(0, first=True)
            with dve.Fori(1, NG - 1) as i:
                turn(i)
            turn(NG - 1, last=True)
            for q in range(4):
                add(NG - 1, GH - 1, q)


class Kept:
    pass


class Dram:
    pass


def setup(nc, ctx):
    k, dram = Kept(), Dram()

    def sb(name, shape, dtype=F32):
        return ctx.enter_context(nc.sbuf_tensor(name, shape, dtype))

    k.ident = sb("ident", [P, P])
    k.iota_row = sb("iota_row", [P, P])
    k.iota_col = sb("iota_col", [P, 1])
    k.idx_key = sb("idx_key", [P, V + GV], I32)
    k.idx_value = sb("idx_value", [P, V + GV], I32)
    k.keycol = sb("keycol", [P, V])
    k.same_block = sb("same_block", [P, V])
    k.block_row = sb("block_row", [1, V], I32)
    k.onehot = sb("onehot", [P, NCH * NB, TN])
    k.breaks = sb("breaks", [P, CL + 1], BF16)
    k.edge_f8 = sb("edge_f8", [H, SC])
    k.edge_b8 = sb("edge_b8", [H, SC])
    k.scores = sb("scores", [P, V * H])
    k.stream = sb("stream", [P, V * H])
    k.words = 30000
    k.arena = ctx.enter_context(nc.sbuf_tensor("arena", [P, k.words], F32))
    k.psum = ctx.enter_context(nc.psum_tensor("psum", [P, 8, 512], F32))

    def dr(name, shape, dtype=F32):
        return nc.dram_tensor(f"scratch_{name}", shape, dtype, kind="Internal").ap()

    dram.comb = dr("comb", (TILES, 3 * P))
    dram.reach = dr("reach", (TILES,))
    dram.keyrow = dr("keyrow", (V, P), BF16)
    dram.key = dr("key", (V * P,))
    dram.blocks_i = dr("blocks_i", (V,), I32)
    dram.blocks_f = dr("blocks_f", (V,))
    dram.edge_f = dr("edge_f", (P,))
    dram.edge_b = dr("edge_b", (P,))
    dram.carry = dr("carry", (4, P))
    dram.carried = dr("carried", (4, P))
    dram.state = dr("state", (NP, D))
    dram.xn = dr("xn", (NP, D))
    dram.key_rows = dr("key_rows", (BLK * P * TE, D))
    dram.value_rows = dr("value_rows", (BLK * P, RW))
    return k, dram


def transpose_chunk(pe, k, banks, rows, blocks=NB):
    for f in range(2):
        for q in range(blocks):
            t = pe.transpose(k.psum[:, banks + f, q * P:(q + 1) * P], rows[:, q, f * P:(f + 1) * P], k.ident[:, :])
    return t


def two_banks(k, bank):
    return k.psum[:, bank:bank + 2, :].rearrange("p a (b d) -> p (a b) d", d=D)


def copy_turned(act, k, bank, to):
    return act.copy(to.rearrange("p f n -> p (f n)"), k.psum[:, bank:bank + 2, :].rearrange("p a n -> p (a n)"))


def build_layer_tail(nc, k, dram):
    a = Arena(k.arena, k.words)
    a.take([NP // P, RW])
    sums = all_sums(k)
    b = Arena(k.scores, V * H)
    vec, wo, w1, w2, b1 = tail_weights(k)
    state = a.take([NB, D])
    total, inverse = a.take([NB, H]), a.take([NB, H])
    mean, y, unit = b.take([NB, D]), b.take([NB, D]), b.take([NB, D])
    meanT, unitT = a.take([2, CH]), a.take([2, CH])
    hidden = a.take([FF // P, CH])
    stats, moments, rstd = a.take([NB, 6]), a.take([NB, 2]), a.take([NB])
    eps, minus_half = a.take([NB]), a.take([NB])
    rest, y2, out = b.take([NB, D]), b.take([NB, D]), b.take([NB, D])
    stats2, moments2, rstd2 = a.take([NB, 6]), a.take([NB, 2]), a.take([NB])
    with stage(nc, "tail", "consts state total inverse mean turned1 copied1 "
               "attended added1 biased1 turned2 copied2 hidden gelu second added2 rest stored passed "
               + norm_sems("ln1") + " " + norm_sems("ln2")) as (block, s):
        J = FF // P

        def chunks(eng, layers):
            with eng.Fori(0, NCH - 2) as c:
                layers(c, True, True)
            layers(NCH - 2, True, False)
            layers(NCH - 1, False, False)

        @block.sync
        def _(sp):
            sp.dma_start(state, chunk_rows(dram.state, 0)).then_inc(s["state"], 16)
            sp.wait_ge(s["biased1"], 1)
            sp.dma_start(state, chunk_rows(dram.state, 1)).then_inc(s["state"], 16)

            def layers(c, one, two):
                if two:
                    sp.wait_ge(s["biased1"], c + 2)
                    sp.dma_start(state, chunk_rows(dram.state, c + 2)).then_inc(s["state"], 16)
                sp.wait_ge(s["ln2_shifted"], c + 1)
                sp.dma_start(chunk_rows(dram.state, c), out).then_inc(s["stored"], 16)

            chunks(sp, layers)
            sp.wait_ge(s["stored"], 16 * NCH)

        @block.gpsimd
        def _(pool):
            pool.memset(eps, 1e-5)
            pool.memset(minus_half, -0.5).then_inc(s["consts"], 1)
            pool.wait_ge(s["consts"], 1)

            def layers(c, one, two):
                if one:
                    inverse_root(pool, s, "ln1", c + 2, moments, rstd, eps, minus_half)
                inverse_root(pool, s, "ln2", c + 1, moments2, rstd2, eps, minus_half)

            inverse_root(pool, s, "ln1", 1, moments, rstd, eps, minus_half)
            chunks(pool, layers)

        @block.vector
        def _(dve):
            def average(c):
                rows = sums[:, ds(c * NB, NB), :].rearrange("p q (h d) -> p q h d", h=H)
                dve.wait_ge(s["mean"], c)
                dve.tensor_scalar(total, rows[:, :, :, HD], 1e-10, None, ALU.add).then_inc(s["total"], 1)
                dve.wait_ge(s["total"], c + 1)
                dve.reciprocal(inverse, total).then_inc(s["inverse"], 1)
                dve.wait_ge(s["inverse"], c + 1)
                dve.wait_ge(s["turned1"], c)
                dve.tensor_tensor(mean.rearrange("p q (h d) -> p q h d", h=H), rows[:, :, :, 0:HD],
                                  along(inverse, 3, HD), ALU.mult).then_inc(s["mean"], 1)

            def first_norm(c):
                dve.wait_ge(s["attended"], c + 1)
                dve.wait_ge(s["state"], 16 * c + 16)
                dve.tensor_tensor(y, two_banks(k, 2), state, ALU.add).then_inc(s["added1"], 1)
                dve.wait_ge(s["added1"], c + 1)
                dve.tensor_tensor(y, y, along(vec["bo"], 1, NB), ALU.add).then_inc(s["biased1"], 1)
                dve.wait_ge(s["biased1"], c + 1)
                dve.wait_ge(s["turned2"], c)
                normalize(dve, s, "ln1", c + 1, y, unit, stats, moments, rstd, vec["ln1_g"], vec["ln1_b"])

            def residual(c):
                dve.wait_ge(s["ln1_shifted"], c + 1)
                dve.tensor_tensor(rest, unit, along(vec["b2"], 1, NB), ALU.add).then_inc(s["rest"], 1)

            def layers(c, one, two):
                if one:
                    first_norm(c + 1)
                if two:
                    average(c + 2)
                dve.wait_ge(s["second"], c + 1)
                dve.wait_ge(s["rest"], c + 1)
                dve.tensor_tensor(y2, two_banks(k, 4), rest, ALU.add).then_inc(s["added2"], 1)
                dve.wait_ge(s["added2"], c + 1)
                dve.wait_ge(s["stored"], 16 * c)
                normalize(dve, s, "ln2", c + 1, y2, out, stats2, moments2, rstd2, vec["ln2_g"], vec["ln2_b"])
                if one:
                    residual(c + 1)

            average(0)
            first_norm(0)
            average(1)
            residual(0)
            chunks(dve, layers)

        @block.tensor
        def _(pe):
            def turn_mean(c):
                pe.wait_ge(s["mean"], c + 1)
                transpose_chunk(pe, k, 0, mean, blocks_in(c)).then_inc(s["turned1"], 1)

            def attend(c):
                pe.wait_ge(s["copied1"], c + 1)
                pe.wait_ge(s["added1"], c)
                for q in range(blocks_in(c)):
                    for f in range(2):
                        t = pe.matmul(two_banks(k, 2)[:, q, :], meanT[:, f, q * P:(q + 1) * P], wo[:, f, :],
                                      start=(f == 0), stop=(f == 1))
                t.then_inc(s["attended"], 1)

            def turn_unit(c):
                pe.wait_ge(s["ln1_shifted"], c + 1)
                transpose_chunk(pe, k, 0, unit, blocks_in(c)).then_inc(s["turned2"], 1)

            def first(c, j):
                if j >= 2:
                    pe.wait_ge(s["gelu"], c * J + j - 1)
                nodes = blocks_in(c) * P
                for f in range(2):
                    t = pe.matmul(k.psum[:, 6 + j % 2, 0:nodes], w1[:, f, j * P:(j + 1) * P], unitT[:, f, 0:nodes],
                                  start=(f == 0), stop=(f == 1))
                t.then_inc(s["hidden"], 1)

            def layers(c, one, two):
                pe.wait_ge(s["copied2"], c + 1)
                for j in range(J):
                    if j == J // 2 and one:
                        turn_mean(c + 1)
                    first(c, j)
                if one:
                    attend(c + 1)
                pe.wait_ge(s["gelu"], (c + 1) * J)
                pe.wait_ge(s["added2"], c)
                for q in range(blocks_in(c)):
                    for j in range(J):
                        t = pe.matmul(two_banks(k, 4)[:, q, :], hidden[:, j, q * P:(q + 1) * P], w2[:, j, :],
                                      start=(j == 0), stop=(j == J - 1))
                t.then_inc(s["second"], 1)
                if one:
                    turn_unit(c + 1)

            turn_mean(0)
            attend(0)
            turn_unit(0)
            chunks(pe, layers)

        @block.scalar
        def _(act):
            def copy_mean(c):
                act.wait_ge(s["turned1"], c + 1)
                copy_turned(act, k, 0, meanT).then_inc(s["copied1"], 1)

            def copy_unit(c):
                act.wait_ge(s["turned2"], c + 1)
                copy_turned(act, k, 0, unitT).then_inc(s["copied2"], 1)

            def layers(c, one, two):
                for j in range(J):
                    if j == J // 2 and one:
                        copy_mean(c + 1)
                    act.wait_ge(s["hidden"], c * J + j + 1)
                    if j == 0:
                        act.wait_ge(s["second"], c)
                    nodes = blocks_in(c) * P
                    act.activation(hidden[:, j, 0:nodes], k.psum[:, 6 + j % 2, 0:nodes], ACT.Gelu,
                                   bias=b1[:, j:j + 1]).then_inc(s["gelu"], 1)
                if one:
                    copy_unit(c + 1)

            copy_mean(0)
            copy_unit(0)
            chunks(act, layers)


def expert_weights(a):
    return [a.take([NX * 2, HE]) for _ in range(3)]


def build_linear_attention(nc, k, w, mixed, experts, dram):
    a = Arena(k.arena, k.words)
    assert a.take([2, D]) is not None
    experts_at = expert_weights(a)
    wq, wk, wv, wo = (a.take([2, D]) for _ in range(4))
    wkvT, woT = a.take([2, 2 * D]), a.take([2, D])
    g = [a.take([MD]) for _ in range(4)]
    rows, rowsT = [a.take([D]) for _ in range(2)], a.take([2, P])
    kvs, square = [a.take([2 * MH, MD]) for _ in range(2)], a.take([2 * MH, MD])
    sums, mean, var, rstd = (a.take([2 * MH]) for _ in range(4))
    eps, minus_half, mask = a.take([2 * MH]), a.take([2 * MH]), a.take([BLK])
    zeros, paired, first = a.take([P]), a.take([2, P]), a.take([2, D])
    with stage(nc, "mixkv", "weights experts turned copied loaded0 loaded1 xturned xcopied projected summed mean centred squared "
               "spread var eps rstd unit scaled shifted masked product consts mask zeroed") as (block, s):
        s_loaded = [s["loaded0"], s["loaded1"]]

        @block.sync
        def _(sp):
            for to, n in ((wq, "wq"), (wk, "wk"), (wv, "wv"), (wo, "wo")):
                sp.dma_start(to, w[n].rearrange("(f p) n -> p f n", p=P)).then_inc(s["weights"], 16)
            for to, n in zip(g, ("ln_k_g", "ln_k_b", "ln_v_g", "ln_v_b")):
                sp.dma_start(to, w[n].partition_broadcast(P)).then_inc(s["weights"], 16)

            def load(n, b):
                sp.dma_start(rows[b], dram.xn[ds(n * P, P), :]).then_inc(s_loaded[b], 16)

            def step(n, b, i, one, two):
                if two:
                    sp.wait_ge(s["xturned"], n + 1)
                    load(n + 2, b)

            load(0, 0)
            load(1, 1)
            for to, n in zip(experts_at, ("W1", "W2", "Wo")):
                sp.dma_start(to, experts[n].rearrange("e (f p) n -> p (e f) n", p=P)).then_inc(s["experts"], 16)
            in_slots(sp, BLK, step)
            sp.wait_ge(s["experts"], 48)

        @block.gpsimd
        def _(pool):
            pool.memset(eps, 1e-5).then_inc(s["consts"], 1)
            pool.memset(minus_half, -0.5).then_inc(s["consts"], 1)
            pool.memset(mask, 1.0).then_inc(s["consts"], 1)
            pool.wait_ge(s["consts"], 3)
            pool.affine_select(out=mask, in_=mask, compare_op=ALU.is_ge, fill=0.0, base=N - 1,
                               pattern=[[-P, BLK]], channel_multiplier=-1).then_inc(s["mask"], 1)
            with pool.Fori(0, BLK) as b:
                pool.wait_ge(s["var"], b + 1)
                pool.tensor_tensor(rstd, var, eps, ALU.add).then_inc(s["eps"], 1)
                pool.wait_ge(s["eps"], b + 1)
                pool.tensor_tensor(rstd, rstd, minus_half, ALU.pow).then_inc(s["rstd"], 1)

        @block.tensor
        def _(pe):
            pe.wait_ge(s["weights"], 16 * 8)
            for n, of in enumerate((wk, wv, wo)):
                for f in range(2):
                    for o in range(2):
                        t = pe.transpose(k.psum[:, n, (f * 2 + o) * P:(f * 2 + o + 1) * P],
                                         of[:, o, f * P:(f + 1) * P], k.ident[:, :])
            t.then_inc(s["turned"], 1)
            pe.wait_ge(s["copied"], 3)

            def project(n, b, i):
                pe.wait_ge(s_loaded[b], 16 * i + 16)
                for f in range(2):
                    t = pe.transpose(k.psum[:, 3, f * P:(f + 1) * P], rows[b][:, f * P:(f + 1) * P], k.ident[:, :])
                t.then_inc(s["xturned"], 1)
                pe.wait_ge(s["xcopied"], n + 1)
                for f in range(2):
                    t = pe.matmul(k.psum[:, 6 + b, :], rowsT[:, f, :], wkvT[:, f, :], start=(f == 0), stop=(f == 1))
                t.then_inc(s["projected"], 1)

            def step(n, b, i, one, two):
                if two:
                    pe.wait_ge(s["centred"], n + 1)
                    project(n + 2, b, i + 1)
                pe.wait_ge(s["masked"], n + 1)
                for f in range(2):
                    t = pe.matmul(k.psum[:, 4 + f, 0:P],
                                  kvs[b][:, 2 * f:2 * f + 2, :].rearrange("p a b -> p (a b)"),
                                  kvs[b][:, MH + 2 * f:MH + 2 * f + 2, :].rearrange("p a b -> p (a b)"),
                                  start=False, stop=not one)
                t.then_inc(s["product"], 1)

            project(0, 0, 0)
            project(1, 1, 0)
            pe.wait_ge(s["zeroed"], 2)
            for f in range(2):
                pe.matmul(k.psum[:, 4 + f, 0:P], zeros, zeros, start=True, stop=False)
            in_slots(pe, BLK, step)

        @block.scalar
        def _(act):
            act.wait_ge(s["turned"], 1)
            for n in range(2):
                act.copy(wkvT[:, :, n * D:(n + 1) * D],
                         k.psum[:, n, :].rearrange("p (f n) -> p f n", f=2)).then_inc(s["copied"], 1)
            act.copy(woT, k.psum[:, 2, :].rearrange("p (f n) -> p f n", f=2)).then_inc(s["copied"], 1)

            def copy(n):
                act.wait_ge(s["xturned"], n + 1)
                act.wait_ge(s["projected"], n)
                act.copy(rowsT.rearrange("p f n -> p (f n)"), k.psum[:, 3, 0:2 * P]).then_inc(s["xcopied"], 1)

            def squares(n, b):
                act.wait_ge(s["centred"], n + 1)
                act.wait_ge(s["spread"], n)
                act.activation(square, kvs[b], ACT.Square).then_inc(s["squared"], 1)

            def step(n, b, i, one, two):
                if two:
                    copy(n + 2)
                if one:
                    squares(n + 1, 1 - b)

            copy(0)
            copy(1)
            squares(0, 0)
            in_slots(act, BLK, step)

        @block.vector
        def _(dve):
            dve.memset(zeros, 0.0).then_inc(s["zeroed"], 1)
            dve.memset(paired, 0.0).then_inc(s["zeroed"], 1)
            dve.wait_ge(s["zeroed"], 2)
            dve.wait_ge(s["weights"], 16 * 8)
            dve.wait_ge(s["mask"], 1)

            def centre(n, b):
                out = k.psum[:, 6 + b, :].rearrange("p (h d) -> p h d", h=2 * MH)
                dve.wait_ge(s["projected"], n + 1)
                dve.wait_ge(s["var"], n)
                dve.tensor_reduce(sums, out, AX, ALU.add).then_inc(s["summed"], 1)
                dve.wait_ge(s["summed"], n + 1)
                dve.tensor_scalar(mean, sums, 1.0 / MD, None, ALU.mult).then_inc(s["mean"], 1)
                dve.wait_ge(s["mean"], n + 1)
                if not (isinstance(n, int) and n == 0):
                    dve.wait_ge(s["product"], n - 1)
                dve.tensor_tensor(kvs[b], out, along(mean, 2, MD), ALU.subtract).then_inc(s["centred"], 1)

            def variance(n):
                dve.wait_ge(s["squared"], n + 1)
                dve.tensor_reduce(sums, square, AX, ALU.add).then_inc(s["spread"], 1)
                dve.wait_ge(s["spread"], n + 1)
                dve.tensor_scalar(var, sums, 1.0 / MD, None, ALU.mult).then_inc(s["var"], 1)

            def norm(n, kv):
                dve.wait_ge(s["rstd"], n + 1)
                dve.tensor_tensor(kv, kv, along(rstd, 2, MD), ALU.mult).then_inc(s["unit"], 1)
                dve.wait_ge(s["unit"], n + 1)
                for half in range(2):
                    ins = dve.tensor_tensor(kv[:, half * MH:(half + 1) * MH], kv[:, half * MH:(half + 1) * MH],
                                            along(g[2 * half], 1, MH), ALU.mult)
                ins.then_inc(s["scaled"], 1)
                dve.wait_ge(s["scaled"], n + 1)
                for half in range(2):
                    ins = dve.tensor_tensor(kv[:, half * MH:(half + 1) * MH], kv[:, half * MH:(half + 1) * MH],
                                            along(g[2 * half + 1], 1, MH), ALU.add)
                if not (isinstance(n, int) and n == BLK - 1):
                    ins.then_inc(s["masked"], 1)
                else:
                    ins.then_inc(s["shifted"], 1)
                    dve.wait_ge(s["shifted"], 1)
                    dve.tensor_scalar(kv[:, 0:MH], kv[:, 0:MH], mask[:, n:n + 1], None, ALU.mult).then_inc(s["masked"], 1)

            def step(n, b, i, one, two):
                if one:
                    centre(n + 1, 1 - b)
                norm(n, kvs[b])
                if one:
                    variance(n + 1)

            centre(0, 0)
            variance(0)
            in_slots(dve, BLK, step)
            dve.wait_ge(s["product"], BLK)
            total = k.psum[:, 4:6, 0:P]
            for half in range(2):
                part = slice(half * MD, (half + 1) * MD)
                dve.tensor_scalar(paired[part, :, part], total[part, :, part], 1.0 / N, None, ALU.mult)

    with stage(nc, "mixw", "first copied second") as (block, s):
        @block.tensor
        def _(pe):
            for f in range(2):
                t = pe.matmul(k.psum[:, f, 0:D], paired[:, f, :], wq[:, f, :], start=True, stop=True)
            t.then_inc(s["first"], 1)
            pe.wait_ge(s["copied"], 1)
            for o in range(2):
                for f in range(2):
                    t = pe.matmul(k.psum[:, 2 + o, 0:D], first[:, f, o * P:(o + 1) * P], woT[:, f, :],
                                  start=(f == 0), stop=(f == 1))
            t.then_inc(s["second"], 1)

        @block.vector
        def _(dve):
            dve.wait_ge(s["first"], 1)
            dve.tensor_copy(first, k.psum[:, 0:2, 0:D]).then_inc(s["copied"], 1)
            dve.wait_ge(s["second"], 1)
            dve.tensor_copy(mixed, k.psum[:, 2:4, 0:D])


def build_experts(nc, k, w, x, mixed, mix_bo, gnn_g, gnn_b, out_dram, dram):
    a = Arena(k.arena, k.words)
    a.take([2, D])
    EH = NX * 2
    w1, w2, w3 = expert_weights(a)
    wr, br, bo = a.take([2, NX]), a.take([NX]), a.take([HE], parts=NX)
    bnv = [[a.take([EH]) for _ in range(5)] for _ in range(2)]
    scale, shift = [a.take([EH]) for _ in range(2)], [a.take([EH]) for _ in range(2)]
    og, ob, mbo = a.take([D]), a.take([D]), a.take([D])
    xr, x2, st = a.take([NB, D]), a.take([NB, D]), a.take([NB, D])
    xnT, unitT = a.take([2, CH]), a.take([2, CH])
    h1, h2 = a.take([2, CH]), a.take([2, CH])
    stats, moments, rstd = a.take([NB, 6]), a.take([NB, 2]), a.take([NB])
    stats2, moments2, rstd2 = a.take([NB, 6]), a.take([NB, 2]), a.take([NB])
    eps, minus_half, bneps, bnhalf = a.take([NB]), a.take([NB]), a.take([EH]), a.take([EH])
    logits, most, gates, gsum, ginv = a.take([NB, NX]), a.take([NB]), a.take([NB, NX]), a.take([NB]), a.take([NB])
    gatesT = a.take([CH], parts=NX)
    big = k.scores[:, :]
    xn = big[:, 0:NB * D].rearrange("p (q d) -> p q d", q=NB)
    gn = big[:, NB * D:2 * NB * D].rearrange("p (q d) -> p q d", q=NB)
    acc = [big[:, (2 + n) * NB * D:(3 + n) * NB * D].rearrange("p (q d) -> p q d", q=NB) for n in range(2)]
    unit = big[:, 4 * NB * D:5 * NB * D].rearrange("p (q d) -> p q d", q=NB)
    start = big[:, 5 * NB * D:6 * NB * D].rearrange("p (q d) -> p q d", q=NB)
    with stage(nc, "bnfold", "loaded consts eps root scale diff prod done") as (block, s):
        @block.sync
        def _(sp):
            with nc.allow_non_contiguous_dma(reason="once"):
                for layer, names in enumerate((("b1", "g1", "be1", "m1", "v1"), ("b2", "g2", "be2", "m2", "v2"))):
                    for to, n in zip(bnv[layer], names):
                        sp.dma_start(to, w[n].rearrange("e (f p) -> p (e f)", p=P)).then_inc(s["loaded"], 16)
            sp.dma_start(wr, w["Wr"].rearrange("(f p) e -> p f e", p=P)).then_inc(s["loaded"], 16)
            sp.dma_start(br, w["br"].partition_broadcast(P)).then_inc(s["loaded"], 16)
            sp.dma_start(bo, w["bo"]).then_inc(s["loaded"], 16)
            for to, of in ((og, gnn_g), (ob, gnn_b), (mbo, mix_bo)):
                sp.dma_start(to, of.partition_broadcast(P)).then_inc(s["loaded"], 16)
            sp.wait_ge(s["loaded"], 16 * 16)

        @block.gpsimd
        def _(pool):
            for to, value in ((bneps, 1e-3), (bnhalf, -0.5), (eps, 1e-5), (minus_half, -0.5)):
                pool.memset(to, value).then_inc(s["consts"], 1)
            pool.wait_ge(s["consts"], 4)
            pool.wait_ge(s["loaded"], 16 * 16)
            for n in range(2):
                pool.tensor_tensor(scale[n], bnv[n][4], bneps, ALU.add).then_inc(s["eps"], 1)
                pool.wait_ge(s["eps"], n + 1)
                pool.tensor_tensor(scale[n], scale[n], bnhalf, ALU.pow).then_inc(s["root"], 1)
                pool.wait_ge(s["root"], n + 1)
                pool.tensor_tensor(scale[n], scale[n], bnv[n][1], ALU.mult).then_inc(s["scale"], 1)
                pool.tensor_tensor(shift[n], bnv[n][0], bnv[n][3], ALU.subtract).then_inc(s["diff"], 1)
                pool.wait_ge(s["scale"], n + 1)
                pool.wait_ge(s["diff"], n + 1)
                pool.tensor_tensor(shift[n], shift[n], scale[n], ALU.mult).then_inc(s["prod"], 1)
                pool.wait_ge(s["prod"], n + 1)
                pool.tensor_tensor(shift[n], shift[n], bnv[n][2], ALU.add).then_inc(s["done"], 1)

    with stage(nc, "experts", "x xn state turned copied mixed summed1 summed2 summed3 turned2 copied2 routed lbias most less exp "
               "gsum ginv gates gturned gcopied biased start h1 a1 h2 a2 y acc stored passed "
               + norm_sems("ln1") + " " + norm_sems("ln2")) as (block, s):
        def chunks(eng, turns):
            with eng.Fori(0, NCH - 1) as c:
                turns(c, True)
            turns(NCH - 1, False)

        @block.sync
        def _(sp):
            def load(c):
                sp.wait_ge(s["ln1_unit"], c)
                sp.dma_start(st, chunk_rows(dram.state, c)).then_inc(s["state"], 16)
                sp.wait_ge(s["turned"], c)
                sp.dma_start(xn, chunk_rows(dram.xn, c)).then_inc(s["xn"], 16)
                sp.wait_ge(s["summed3"], c)
                sp.dma_start(xr, chunk_rows(x, c)).then_inc(s["x"], 16)

            def turns(c, more):
                if more:
                    load(c + 1)
                sp.wait_ge(s["acc"], (c + 1) * NX)
                sp.dma_start(chunk_rows(out_dram, c), acc[(NX - 1) % 2]).then_inc(s["stored"], 16)

            load(0)
            chunks(sp, turns)
            sp.wait_ge(s["stored"], 16 * NCH)

        @block.gpsimd
        def _(pool):
            with pool.Fori(0, NCH) as c:
                inverse_root(pool, s, "ln1", c + 1, moments, rstd, eps, minus_half)
                inverse_root(pool, s, "ln2", c + 1, moments2, rstd2, eps, minus_half)

        @block.tensor
        def _(pe):
            def product(bank, wts, e, of, nodes):
                for f2 in range(2):
                    for f in range(2):
                        t = pe.matmul(k.psum[:, bank + f2, 0:nodes], wts[:, 2 * e + f, f2 * P:(f2 + 1) * P],
                                      of[:, f, 0:nodes],
                                      start=(f == 0), stop=(f == 1))
                return t

            def turn_xn(c):
                pe.wait_ge(s["xn"], 16 * c + 16)
                pe.wait_ge(s["start"], c)
                transpose_chunk(pe, k, 6, xn, blocks_in(c)).then_inc(s["turned"], 1)

            def mix(c):
                pe.wait_ge(s["copied"], c + 1)
                for q in range(blocks_in(c)):
                    for f in range(2):
                        t = pe.matmul(two_banks(k, 6)[:, q, :], xnT[:, f, q * P:(q + 1) * P], mixed[:, f, :],
                                      start=(f == 0), stop=(f == 1))
                t.then_inc(s["mixed"], 1)

            def turn_unit(c):
                pe.wait_ge(s["summed1"], c + 1)
                pe.wait_ge(s["ln2_unit"], c + 1)
                transpose_chunk(pe, k, 6, unit, blocks_in(c)).then_inc(s["turned2"], 1)

            def first(c, e):
                pe.wait_ge(s["a1"], c * NX + e)
                product(0, w1, e, unitT, blocks_in(c) * P).then_inc(s["h1"], 1)

            def route(c):
                pe.wait_ge(s["copied2"], c + 1)
                first(c, 0)
                for q in range(NB):
                    for f in range(2):
                        t = pe.matmul(k.psum[:, 6, q * NX:(q + 1) * NX], unitT[:, f, q * P:(q + 1) * P], wr[:, f, :],
                                      start=(f == 0), stop=(f == 1))
                t.then_inc(s["routed"], 1)

            def turns(c, more):
                for e in range(NX):
                    n = c * NX + e
                    pe.wait_ge(s["a1"], n + 1)
                    pe.wait_ge(s["a2"], n)
                    product(4, w2, e, h1, blocks_in(c) * P).then_inc(s["h2"], 1)
                    if e == 0:
                        pe.wait_ge(s["gates"], c + 1)
                        for q in range(NB):
                            t = pe.transpose(k.psum[0:NX, 7, q * P:(q + 1) * P], gates[:, q, :], k.ident[:, :])
                        t.then_inc(s["gturned"], 1)
                    if e < NX - 1:
                        first(c, e + 1)
                    elif more:
                        route(c + 1)
                    if e == 0:
                        pe.wait_ge(s["gcopied"], c + 1)
                        for q in range(NB):
                            t = pe.matmul(two_banks(k, 6)[:, q, :], gatesT[:, q * P:(q + 1) * P], bo[:, :],
                                          start=True, stop=True)
                        t.then_inc(s["biased"], 1)
                    if e == 1 and more:
                        turn_xn(c + 1)
                    if e == 2 and more:
                        mix(c + 1)
                    if e == 6 and more:
                        turn_unit(c + 1)
                    pe.wait_ge(s["a2"], n + 1)
                    pe.wait_ge(s["acc"], n)
                    for q in range(blocks_in(c)):
                        for f in range(2):
                            t = pe.matmul(two_banks(k, 2)[:, q, :], h2[:, f, q * P:(q + 1) * P], w3[:, 2 * e + f, :],
                                          start=(f == 0), stop=(f == 1))
                    t.then_inc(s["y"], 1)

            turn_xn(0)
            mix(0)
            turn_unit(0)
            route(0)
            chunks(pe, turns)

        @block.scalar
        def _(act):
            def rectify(layer, c, e, bank, to):
                nodes = blocks_in(c) * P
                for f in range(2):
                    ins = act.activation(to[:, f, 0:nodes], k.psum[:, bank + f, 0:nodes], ACT.Relu,
                                         bias=shift[layer][:, 2 * e + f:2 * e + f + 1],
                                         scale=scale[layer][:, 2 * e + f:2 * e + f + 1])
                return ins

            def copy_xn(c):
                act.wait_ge(s["turned"], c + 1)
                copy_turned(act, k, 6, xnT).then_inc(s["copied"], 1)

            def copy_unit(c):
                act.wait_ge(s["turned2"], c + 1)
                act.wait_ge(s["h1"], c * NX)
                act.wait_ge(s["routed"], c)
                copy_turned(act, k, 6, unitT).then_inc(s["copied2"], 1)

            def first(c, e):
                act.wait_ge(s["h1"], c * NX + e + 1)
                act.wait_ge(s["h2"], c * NX + e)
                rectify(0, c, e, 0, h1).then_inc(s["a1"], 1)

            def route(c):
                first(c, 0)
                act.wait_ge(s["less"], c + 1)
                act.activation(logits, logits, ACT.Exp).then_inc(s["exp"], 1)

            def turns(c, more):
                for e in range(NX):
                    n = c * NX + e
                    act.wait_ge(s["h2"], n + 1)
                    act.wait_ge(s["y"], n)
                    rectify(1, c, e, 4, h2).then_inc(s["a2"], 1)
                    if e == 0:
                        act.wait_ge(s["gturned"], c + 1)
                        act.copy(gatesT, k.psum[0:NX, 7, :]).then_inc(s["gcopied"], 1)
                    if e < NX - 1:
                        first(c, e + 1)
                    elif more:
                        route(c + 1)
                    if e == 1 and more:
                        copy_xn(c + 1)
                    if e == 6 and more:
                        copy_unit(c + 1)

            copy_xn(0)
            copy_unit(0)
            route(0)
            chunks(act, turns)

        @block.vector
        def _(dve):
            def state_moments(c):
                dve.wait_ge(s["state"], 16 * c + 16)
                norm_moments(dve, s, "ln1", c + 1, st, stats, moments)

            def state_rows(c):
                norm_rows(dve, s, "ln1", c + 1, st, gn, moments, rstd, og, ob)

            def add_up(c):
                dve.wait_ge(s["ln1_shifted"], c + 1)
                dve.wait_ge(s["mixed"], c + 1)
                dve.tensor_tensor(x2, two_banks(k, 6), gn, ALU.add).then_inc(s["summed1"], 1)
                dve.wait_ge(s["summed1"], c + 1)
                dve.tensor_tensor(x2, x2, along(mbo, 1, NB), ALU.add).then_inc(s["summed2"], 1)
                dve.wait_ge(s["summed2"], c + 1)
                dve.wait_ge(s["x"], 16 * c + 16)
                dve.tensor_tensor(x2, x2, xr, ALU.add).then_inc(s["summed3"], 1)

            def unit_moments(c):
                dve.wait_ge(s["summed3"], c + 1)
                norm_moments(dve, s, "ln2", c + 1, x2, stats2, moments2)

            def unit_rows(c):
                dve.wait_ge(s["turned2"], c)
                norm_rows(dve, s, "ln2", c + 1, x2, unit, moments2, rstd2)

            def weigh(c):
                dve.wait_ge(s["routed"], c + 1)
                dve.tensor_tensor(logits, k.psum[:, 6, 0:NB * NX].rearrange("p (q e) -> p q e", q=NB),
                                  along(br, 1, NB), ALU.add).then_inc(s["lbias"], 1)
                dve.wait_ge(s["lbias"], c + 1)
                dve.tensor_reduce(most, logits, AX, ALU.max).then_inc(s["most"], 1)
                dve.wait_ge(s["most"], c + 1)
                dve.tensor_tensor(logits, logits, along(most, 2, NX), ALU.subtract).then_inc(s["less"], 1)
                dve.wait_ge(s["exp"], c + 1)
                dve.tensor_reduce(gsum, logits, AX, ALU.add).then_inc(s["gsum"], 1)
                dve.wait_ge(s["gsum"], c + 1)
                dve.reciprocal(ginv, gsum).then_inc(s["ginv"], 1)

            def turns(c, more):
                dve.wait_ge(s["ginv"], c + 1)
                dve.wait_ge(s["acc"], c * NX)
                dve.tensor_tensor(gates, logits, along(ginv, 2, NX), ALU.mult).then_inc(s["gates"], 1)
                dve.wait_ge(s["biased"], c + 1)
                dve.tensor_tensor(start, two_banks(k, 6), x2, ALU.add).then_inc(s["start"], 1)
                dve.wait_ge(s["gates"], c + 1)
                dve.wait_ge(s["start"], c + 1)
                within = {2: state_moments, 3: state_rows, 4: add_up, 5: unit_moments, 6: unit_rows, 7: weigh}
                for e in range(NX):
                    n = c * NX + e
                    if e in within and more:
                        within[e](c + 1)
                    if e == 1:
                        dve.wait_ge(s["stored"], 16 * c)
                    dve.wait_ge(s["y"], n + 1)
                    dve.wait_ge(s["acc"], n)
                    for q in range(NB):
                        ins = dve.scalar_tensor_tensor(acc[e % 2][:, q, :], two_banks(k, 2)[:, q, :],
                                                       gates[:, q, e:e + 1],
                                                       acc[(e + 1) % 2][:, q, :] if e else start[:, q, :],
                                                       ALU.mult, ALU.add)
                    ins.then_inc(s["acc"], 1)

            for step in (state_moments, state_rows, add_up, unit_moments, unit_rows, weigh):
                step(0)
            chunks(dve, turns)


def build(nc, t):
    with ExitStack() as ctx:
        k, dram = setup(nc, ctx)
        part = lambda prefix: {n[len(prefix):]: ap for n, ap in t.items() if n.startswith(prefix)}
        gnn, mix, ffn = part("L0_gnn_"), part("L0_mix_"), part("L0_ffn_")
        build_constants(nc, k)
        build_visits(nc, k, t["src"], t["dst"], t["edge_type_3"], t["node_type_4"], dram)
        build_input_norm(nc, k, t["x"], dram)
        weights = Arena(k.arena, k.words).take([H, 5 * HD])
        with nc.Fori(0, L) as layer:
            build_type_weights(nc, k, gnn, layer, weights)
            build_rows(nc, k, weights, dram)
            build_scores(nc, k, dram)
            build_softmax(nc, k, dram)
            build_sums(nc, k, gnn, layer, dram)
            build_layer_tail(nc, k, dram)
        mixed = Arena(k.arena, k.words).take([2, D])
        build_linear_attention(nc, k, mix, mixed, ffn, dram)
        build_experts(nc, k, ffn, t["x"], mixed, mix["bo"], gnn["out_g"], gnn["out_b"], t["out"], dram)


_NAMES = ["x", "src", "dst", "edge_type_3", "node_type_4"] + \
    [f"L0_gnn_{n}" for n in ("W_Q", "W_K", "W_V", "W_E", "mu", "Wo", "bo", "ln1_g", "ln1_b", "ln2_g", "ln2_b",
                             "w1", "b1", "w2", "b2", "out_g", "out_b")] + \
    [f"L0_mix_{n}" for n in ("wq", "wk", "wv", "wo", "bo", "ln_k_g", "ln_k_b", "ln_v_g", "ln_v_b")] + \
    [f"L0_ffn_{n}" for n in ("Wr", "br", "W1", "b1", "g1", "be1", "m1", "v1", "W2", "b2", "g2", "be2", "m2",
                             "v2", "Wo", "bo")]
_PADDED = {"x": (NP, 0), "node_type_4": (NP, 0), "src": (EP, 0), "edge_type_3": (EP, 0), "dst": (EP, BLK * P - 1)}


def kernel(**inputs):
    import concourse.bacc as bacc
    from concourse.bass_utils import run_bass_kernel_spmd

    nc = bacc.Bacc("TRN2", target_bir_lowering=False, num_devices=1)
    arrays, tensors = {}, {}
    for name in _NAMES:
        a = np.ascontiguousarray(inputs[name])
        if name in _PADDED:
            rows, fill = _PADDED[name]
            a = np.concatenate([a, np.full((rows - a.shape[0],) + a.shape[1:], fill, a.dtype)])
        arrays[f"in_{name}"] = a
        tensors[name] = nc.dram_tensor(f"in_{name}", a.shape, mybir.dt.from_np(a.dtype), kind="ExternalInput").ap()
    tensors["out"] = nc.dram_tensor("out", (NP, D), F32, kind="ExternalOutput").ap()
    build(nc, tensors)
    result = run_bass_kernel_spmd(nc, [arrays], core_ids=[0])
    return result.results[0]["out"][:N]
```
